# Optimizing a Trainium2 kernel written in Bass

```python
import numpy as np
import jax
import jax.numpy as jnp

def _softmax(x, axis=-1):
    return jax.nn.softmax(x, axis=axis)

def _gelu(x):
    return jax.nn.gelu(x, approximate=True)

def _silu(x):
    return jax.nn.silu(x)

def _sigmoid(x):
    return jax.nn.sigmoid(x)

def _layernorm(x, axis=-1, eps=1e-05):
    m = jnp.mean(x, axis=axis, keepdims=True)
    v = jnp.var(x, axis=axis, keepdims=True)
    return (x - m) / jnp.sqrt(v + eps)

def _scatter_add(tgt, idx, src, axis=0):
    return tgt.at[idx].add(src)

def _segment_sum(src, seg, n):
    return jax.ops.segment_sum(src, seg, n)
kernel_name = 'mk_decoder_preln_d1_seqx_r8_cafabf'

def setup_inputs(seed: int=0):
    np.random.seed(seed)
    _w = jnp.asarray

    def _rec_inputs():
        import jax
        import jax.numpy as jnp
        _rk = jax.random.key(seed)
        x = -0.0002928 + 1 * jax.random.normal(jax.random.fold_in(_rk, 1), (16, 256, 128), jnp.float32)
        _lenS = 256 - jax.random.randint(jax.random.fold_in(_rk, 7), (16,), 0, max(1, 256 // 4) + 1, jnp.int32)
        _lenS2 = 1601 - jax.random.randint(jax.random.fold_in(_rk, 8), (16,), 0, max(1, 1601 // 4) + 1, jnp.int32)
        _ctx_1024P = jax.random.normal(jax.random.fold_in(_rk, 11), (16, 16, 128), jnp.float32)
        _ctx_1024c = jax.random.dirichlet(jax.random.fold_in(_rk, 511), 0.3 * jnp.ones((16,), jnp.float32), (16, 1601))
        _ctx_1024t = jnp.einsum('bsk,bkd->bsd', _ctx_1024c, _ctx_1024P)
        _ctx_1024t = _ctx_1024t * jax.lax.rsqrt(jnp.mean(jnp.square(_ctx_1024t)) + 1e-12) * 0.953939
        ctx_1024 = -1.39393e-06 + 0.999914 * (_ctx_1024t + 0.3 * jax.random.normal(jax.random.fold_in(_rk, 611), (16, 1601, 128), jnp.float32))
        return (x, ctx_1024)
    x, ctx_1024 = _rec_inputs()

    def _L0_attn_setup():
        import jax, jax.numpy as jnp
        import numpy as np
        D_MODEL = 128
        D_QK = 128
        NUM_HEADS = 16
        HEAD_DIM = D_QK // NUM_HEADS
        V_DIM = D_MODEL // NUM_HEADS
        B, S = (2, 256)
        key = jax.random.key(seed)
        ks = jax.random.split(key, 9)
        sc = 0.02
        return {'x': jax.random.normal(ks[0], (B, S, D_MODEL), dtype=jnp.float32), 'Wqk': jax.random.normal(ks[1], (D_MODEL, 2 * D_QK), dtype=jnp.float32) * sc, 'bqk': jax.random.normal(ks[2], (2 * D_QK,), dtype=jnp.float32) * sc, 'Wv': jax.random.normal(ks[3], (D_MODEL, D_MODEL), dtype=jnp.float32) * sc, 'bv': jax.random.normal(ks[4], (D_MODEL,), dtype=jnp.float32) * sc, 'Wn': jax.random.normal(ks[5], (D_MODEL, NUM_HEADS), dtype=jnp.float32) * sc, 'bn': jax.random.normal(ks[6], (NUM_HEADS,), dtype=jnp.float32) * sc, 'Wo': jax.random.normal(ks[7], (D_MODEL, D_MODEL), dtype=jnp.float32) * sc, 'bo': jax.random.normal(ks[8], (D_MODEL,), dtype=jnp.float32) * sc}
    _L0_attn_all = _L0_attn_setup()
    _L0_attn_in = {k: v for k, v in _L0_attn_all.items() if k in ('Wqk', 'bqk', 'Wv', 'bv', 'Wn', 'bn', 'Wo', 'bo')}
    del _L0_attn_all

    def _L0_xattn_setup():
        import jax, jax.numpy as jnp
        import numpy as np
        EMBED_DIM = 128
        NUM_HEADS = 16
        HEAD_DIM = EMBED_DIM // NUM_HEADS
        key = jax.random.key(seed)
        ks = jax.random.split(key, 7)
        B, S, E = (2, 256, EMBED_DIM)
        bound = float(np.sqrt(6.0 / (E + E)))
        mkw = lambda k: jax.random.uniform(k, (E, E), jnp.float32, -bound, bound)
        return {'query': jax.random.normal(ks[0], (B, S, E), jnp.float32), 'key': jax.random.normal(ks[1], (B, S, E), jnp.float32), 'value': jax.random.normal(ks[2], (B, S, E), jnp.float32), 'Wq': mkw(ks[3]), 'Wk': mkw(ks[4]), 'Wv': mkw(ks[5]), 'Wo': mkw(ks[6])}
    _L0_xattn_all = _L0_xattn_setup()
    _L0_xattn_in = {k: v for k, v in _L0_xattn_all.items() if k in ('Wq', 'Wk', 'Wv', 'Wo')}
    del _L0_xattn_all

    def _L0_ffn_setup():
        import jax, jax.numpy as jnp
        import numpy as np
        DIM = 128
        DEPTH = 2
        HEADS = 8
        DIM_HEAD = 64
        WINDOW = 64
        INNER = HEADS * DIM_HEAD
        HID = int(DIM * 4 * 2 / 3)
        B, N = (2, 1024)
        QK_SCALE = 8.0

        def shift_token(t):
            t1, t2 = jnp.split(t, 2, axis=-1)
            t2 = jnp.pad(t2, ((0, 0), (1, 0), (0, 0)))[:, :-1]
            return jnp.concatenate([t1, t2], axis=-1)

        def l2norm(t):
            return t / jnp.clip(jnp.linalg.norm(t, axis=-1, keepdims=True), 1e-12)

        def rotate_half(x):
            x1, x2 = jnp.split(x, 2, axis=-1)
            return jnp.concatenate([-x2, x1], axis=-1)

        def rotary_xpos(q, k):
            n = q.shape[-2]
            half_idx = jnp.arange(0, DIM_HEAD, 2, dtype=jnp.float32)
            inv_freq = 1.0 / 10000.0 ** (half_idx / DIM_HEAD)
            t = jnp.arange(n, dtype=jnp.float32)
            freqs = t[:, None] * inv_freq[None, :]
            freqs = jnp.concatenate([freqs, freqs], axis=-1)
            base = (half_idx + 0.4 * DIM_HEAD) / (1.4 * DIM_HEAD)
            power = (t - n // 2) / float(WINDOW // 2)
            scale = base[None, :] ** power[:, None]
            scale = jnp.concatenate([scale, scale], axis=-1)
            cos, sin = (jnp.cos(freqs), jnp.sin(freqs))
            q = q * cos * scale + rotate_half(q) * sin * scale
            k = k * cos / scale + rotate_half(k) * sin / scale
            return (q, k)

        def local_attention(q, k, v):
            b, h, n, d = q.shape
            w = n // WINDOW
            bq = q.reshape(b, h, w, WINDOW, d) * QK_SCALE
            bk = k.reshape(b, h, w, WINDOW, d)
            bv = v.reshape(b, h, w, WINDOW, d)

            def look_around(t):
                p = jnp.pad(t, ((0, 0), (0, 0), (1, 0), (0, 0), (0, 0)))
                return jnp.concatenate([p[:, :, :w], p[:, :, 1:]], axis=3)
            bk, bv = (look_around(bk), look_around(bv))
            bt = jnp.arange(n).reshape(w, WINDOW)
            btp = jnp.pad(bt, ((1, 0), (0, 0)), constant_values=-1)
            btk = jnp.concatenate([btp[:w], btp[1:]], axis=1)
            sim = jnp.einsum('bhwid,bhwjd->bhwij', bq, bk)
            i = bt[:, :, None]
            j = btk[:, None, :]
            mask = (i < j) | (i > j + WINDOW) | (j == -1)
            sim = jnp.where(mask, -jnp.finfo(sim.dtype).max, sim)
            attn = jax.nn.softmax(sim, axis=-1)
            out = jnp.einsum('bhwij,bhwjd->bhwid', attn, bv)
            return out.reshape(b, h, n, d)

        def _layer(x, wqkv, qs, ksc, wo, lg, lb, w1, b1, w2, b2):
            b, n, _ = x.shape
            h = shift_token(x)
            qkv = h @ wqkv
            q, k, v = jnp.split(qkv, 3, axis=-1)
            to_heads = lambda t: t.reshape(b, n, HEADS, DIM_HEAD).transpose(0, 2, 1, 3)
            q, k, v = (to_heads(q), to_heads(k), to_heads(v))
            q = l2norm(q) * qs
            k = l2norm(k) * ksc
            q, k = rotary_xpos(q, k)
            o = local_attention(q, k, v)
            o = o.transpose(0, 2, 1, 3).reshape(b, n, INNER)
            x = x + o @ wo
            h = shift_token(x)
            mu = h.mean(-1, keepdims=True)
            var = h.var(-1, keepdims=True)
            h = (h - mu) / jnp.sqrt(var + 1e-05) * lg + lb
            h = h @ w1 + b1
            a, g = jnp.split(h, 2, axis=-1)
            h = a * jax.nn.gelu(g, approximate=False)
            x = x + h @ w2 + b2
            return x
        key = jax.random.key(seed)
        ks = jax.random.split(key, 6)
        return {'x': jax.random.normal(ks[0], (B, N, DIM), jnp.float32), 'wqkv': jax.random.normal(ks[1], (DEPTH, DIM, 3 * INNER), jnp.float32) * 0.02, 'q_scale': jnp.ones((DEPTH, DIM_HEAD), jnp.float32), 'k_scale': jnp.ones((DEPTH, DIM_HEAD), jnp.float32), 'wo': jax.random.normal(ks[2], (DEPTH, INNER, DIM), jnp.float32) * 0.02, 'ln_g': jnp.ones((DEPTH, DIM), jnp.float32), 'ln_b': jnp.zeros((DEPTH, DIM), jnp.float32), 'w1': jax.random.normal(ks[3], (DEPTH, DIM, 2 * HID), jnp.float32) * 0.02, 'b1': jnp.zeros((DEPTH, 2 * HID), jnp.float32), 'w2': jax.random.normal(ks[4], (DEPTH, HID, DIM), jnp.float32) * 0.02, 'b2': jnp.zeros((DEPTH, DIM), jnp.float32)}
    _L0_ffn_all = _L0_ffn_setup()
    _L0_ffn_in = {k: v for k, v in _L0_ffn_all.items() if k in ('wqkv', 'q_scale', 'k_scale', 'wo', 'ln_g', 'ln_b', 'w1', 'b1', 'w2', 'b2')}
    del _L0_ffn_all
    return {'x': x, 'ctx_1024': ctx_1024, 'L0_attn_Wqk': _L0_attn_in['Wqk'], 'L0_attn_bqk': _L0_attn_in['bqk'], 'L0_attn_Wv': _L0_attn_in['Wv'], 'L0_attn_bv': _L0_attn_in['bv'], 'L0_attn_Wn': _L0_attn_in['Wn'], 'L0_attn_bn': _L0_attn_in['bn'], 'L0_attn_Wo': _L0_attn_in['Wo'], 'L0_attn_bo': _L0_attn_in['bo'], 'L0_xattn_Wq': _L0_xattn_in['Wq'], 'L0_xattn_Wk': _L0_xattn_in['Wk'], 'L0_xattn_Wv': _L0_xattn_in['Wv'], 'L0_xattn_Wo': _L0_xattn_in['Wo'], 'L0_ffn_wqkv': _L0_ffn_in['wqkv'], 'L0_ffn_q_scale': _L0_ffn_in['q_scale'], 'L0_ffn_k_scale': _L0_ffn_in['k_scale'], 'L0_ffn_wo': _L0_ffn_in['wo'], 'L0_ffn_ln_g': _L0_ffn_in['ln_g'], 'L0_ffn_ln_b': _L0_ffn_in['ln_b'], 'L0_ffn_w1': _L0_ffn_in['w1'], 'L0_ffn_b1': _L0_ffn_in['b1'], 'L0_ffn_w2': _L0_ffn_in['w2'], 'L0_ffn_b2': _L0_ffn_in['b2']}

def reference(x, ctx_1024, L0_attn_Wqk, L0_attn_bqk, L0_attn_Wv, L0_attn_bv, L0_attn_Wn, L0_attn_bn, L0_attn_Wo, L0_attn_bo, L0_xattn_Wq, L0_xattn_Wk, L0_xattn_Wv, L0_xattn_Wo, L0_ffn_wqkv, L0_ffn_q_scale, L0_ffn_k_scale, L0_ffn_wo, L0_ffn_ln_g, L0_ffn_ln_b, L0_ffn_w1, L0_ffn_b1, L0_ffn_w2, L0_ffn_b2):
    import jax
    import jax.numpy as jnp

    def _L0_attn_ref(x, Wqk, bqk, Wv, bv, Wn, bn, Wo, bo):
        import jax, jax.numpy as jnp
        import numpy as np
        D_MODEL = 128
        D_QK = 128
        NUM_HEADS = 16
        HEAD_DIM = D_QK // NUM_HEADS
        V_DIM = D_MODEL // NUM_HEADS
        B, S = (2, 256)
        b, s, _ = x.shape
        qk = x @ Wqk + bqk
        v = x @ Wv + bv
        n = x @ Wn + bn
        qk = qk.reshape(b, s, 2, NUM_HEADS, HEAD_DIM)
        q, k = (qk[:, :, 0], qk[:, :, 1])
        v = v.reshape(b, s, NUM_HEADS, V_DIM)
        scores = jnp.einsum('bthd,bshd->bhts', q, k)
        mask = jnp.tril(jnp.ones((s, s), dtype=scores.dtype))
        n_exp = jnp.exp(jnp.transpose(n, (0, 2, 1)))
        attn = scores * mask / n_exp[:, :, :, None]
        ctx = jnp.einsum('bhts,bshd->bthd', attn, v)
        ctx = ctx.reshape(b, s, D_MODEL)
        return ctx @ Wo + bo

    def _L0_xattn_ref(query, key, value, Wq, Wk, Wv, Wo):
        import jax, jax.numpy as jnp
        import numpy as np
        EMBED_DIM = 128
        NUM_HEADS = 16
        HEAD_DIM = EMBED_DIM // NUM_HEADS
        B, L, E = query.shape
        H, D = (NUM_HEADS, HEAD_DIM)
        scale = D ** (-0.5)
        q = (query @ Wq.T).reshape(B, L, H, D) * scale
        k = (key @ Wk.T).reshape(B, -1, H, D)
        v = (value @ Wv.T).reshape(B, -1, H, D)
        scores = jax.nn.sigmoid(jnp.einsum('blhd,bshd->bhls', q, k))
        o = jnp.einsum('bhls,bshd->blhd', scores, v).reshape(B, L, E)
        return o @ Wo.T

    def _L0_ffn_ref(x, wqkv, q_scale, k_scale, wo, ln_g, ln_b, w1, b1, w2, b2):
        import jax, jax.numpy as jnp
        import numpy as np
        DIM = 128
        DEPTH = 2
        HEADS = 8
        DIM_HEAD = 64
        WINDOW = 64
        INNER = HEADS * DIM_HEAD
        HID = int(DIM * 4 * 2 / 3)
        B, N = (2, 1024)
        QK_SCALE = 8.0

        def shift_token(t):
            t1, t2 = jnp.split(t, 2, axis=-1)
            t2 = jnp.pad(t2, ((0, 0), (1, 0), (0, 0)))[:, :-1]
            return jnp.concatenate([t1, t2], axis=-1)

        def l2norm(t):
            return t / jnp.clip(jnp.linalg.norm(t, axis=-1, keepdims=True), 1e-12)

        def rotate_half(x):
            x1, x2 = jnp.split(x, 2, axis=-1)
            return jnp.concatenate([-x2, x1], axis=-1)

        def rotary_xpos(q, k):
            n = q.shape[-2]
            half_idx = jnp.arange(0, DIM_HEAD, 2, dtype=jnp.float32)
            inv_freq = 1.0 / 10000.0 ** (half_idx / DIM_HEAD)
            t = jnp.arange(n, dtype=jnp.float32)
            freqs = t[:, None] * inv_freq[None, :]
            freqs = jnp.concatenate([freqs, freqs], axis=-1)
            base = (half_idx + 0.4 * DIM_HEAD) / (1.4 * DIM_HEAD)
            power = (t - n // 2) / float(WINDOW // 2)
            scale = base[None, :] ** power[:, None]
            scale = jnp.concatenate([scale, scale], axis=-1)
            cos, sin = (jnp.cos(freqs), jnp.sin(freqs))
            q = q * cos * scale + rotate_half(q) * sin * scale
            k = k * cos / scale + rotate_half(k) * sin / scale
            return (q, k)

        def local_attention(q, k, v):
            b, h, n, d = q.shape
            w = n // WINDOW
            bq = q.reshape(b, h, w, WINDOW, d) * QK_SCALE
            bk = k.reshape(b, h, w, WINDOW, d)
            bv = v.reshape(b, h, w, WINDOW, d)

            def look_around(t):
                p = jnp.pad(t, ((0, 0), (0, 0), (1, 0), (0, 0), (0, 0)))
                return jnp.concatenate([p[:, :, :w], p[:, :, 1:]], axis=3)
            bk, bv = (look_around(bk), look_around(bv))
            bt = jnp.arange(n).reshape(w, WINDOW)
            btp = jnp.pad(bt, ((1, 0), (0, 0)), constant_values=-1)
            btk = jnp.concatenate([btp[:w], btp[1:]], axis=1)
            sim = jnp.einsum('bhwid,bhwjd->bhwij', bq, bk)
            i = bt[:, :, None]
            j = btk[:, None, :]
            mask = (i < j) | (i > j + WINDOW) | (j == -1)
            sim = jnp.where(mask, -jnp.finfo(sim.dtype).max, sim)
            attn = jax.nn.softmax(sim, axis=-1)
            out = jnp.einsum('bhwij,bhwjd->bhwid', attn, bv)
            return out.reshape(b, h, n, d)

        def _layer(x, wqkv, qs, ksc, wo, lg, lb, w1, b1, w2, b2):
            b, n, _ = x.shape
            h = shift_token(x)
            qkv = h @ wqkv
            q, k, v = jnp.split(qkv, 3, axis=-1)
            to_heads = lambda t: t.reshape(b, n, HEADS, DIM_HEAD).transpose(0, 2, 1, 3)
            q, k, v = (to_heads(q), to_heads(k), to_heads(v))
            q = l2norm(q) * qs
            k = l2norm(k) * ksc
            q, k = rotary_xpos(q, k)
            o = local_attention(q, k, v)
            o = o.transpose(0, 2, 1, 3).reshape(b, n, INNER)
            x = x + o @ wo
            h = shift_token(x)
            mu = h.mean(-1, keepdims=True)
            var = h.var(-1, keepdims=True)
            h = (h - mu) / jnp.sqrt(var + 1e-05) * lg + lb
            h = h @ w1 + b1
            a, g = jnp.split(h, 2, axis=-1)
            h = a * jax.nn.gelu(g, approximate=False)
            x = x + h @ w2 + b2
            return x
        for l in range(DEPTH):
            x = _layer(x, wqkv[l], q_scale[l], k_scale[l], wo[l], ln_g[l], ln_b[l], w1[l], b1[l], w2[l], b2[l])
        return x
    x = x + _L0_attn_ref(_layernorm(x, axis=-1), L0_attn_Wqk, L0_attn_bqk, L0_attn_Wv, L0_attn_bv, L0_attn_Wn, L0_attn_bn, L0_attn_Wo, L0_attn_bo)
    x = x + _L0_xattn_ref(_layernorm(x, axis=-1), ctx_1024, ctx_1024, L0_xattn_Wq, L0_xattn_Wk, L0_xattn_Wv, L0_xattn_Wo)
    x = x + _L0_ffn_ref(_layernorm(x, axis=-1), L0_ffn_wqkv, L0_ffn_q_scale, L0_ffn_k_scale, L0_ffn_wo, L0_ffn_ln_g, L0_ffn_ln_b, L0_ffn_w1, L0_ffn_b1, L0_ffn_w2, L0_ffn_b2)
    return x

_drawn_inputs = setup_inputs


def setup_inputs(seed=0):
    import zlib

    import numpy as np

    out = dict(_drawn_inputs(seed))
    spreads = {'L0_ffn_q_scale': (1.0, 0.6),
     'L0_ffn_k_scale': (1.0, 0.6),
     'L0_ffn_ln_g': (1.0, 0.6),
     'L0_ffn_ln_b': (0.0, 0.8),
     'L0_ffn_b1': (0.0, 0.8),
     'L0_ffn_b2': (0.0, 2.0)}
    factors = {'L0_attn_bqk': 8.0,
     'L0_attn_bv': 8.0,
     'L0_attn_Wn': 7.456,
     'L0_attn_bn': 8.0,
     'L0_attn_bo': 21.8,
     'L0_ffn_wqkv': 8.0,
     'L0_ffn_wo': 8.0,
     'L0_ffn_w1': 8.0,
     'L0_ffn_w2': 8.0}
    for name, (base, spread) in spreads.items():
        noise = np.random.default_rng([zlib.crc32(name.encode()), seed]).standard_normal(out[name].shape)
        drawn = base * np.exp(spread * noise) if base else spread * noise
        out[name] = jnp.asarray(drawn.astype(out[name].dtype))
    for name, factor in factors.items():
        out[name] = (out[name] * factor).astype(out[name].dtype)
    return out
```

```python
from contextlib import ExitStack

import concourse.bass as bass
from concourse import mybir
from concourse.bass import ds

F32 = mybir.dt.float32
BF16 = mybir.dt.bfloat16
I32 = mybir.dt.int32
ALU = mybir.AluOpType
ACT = mybir.ActivationFunctionType
AX = mybir.AxisListType

P = 128
B, S, D = 16, 256, 128
T = B * S
H, HD = 16, 8
HG, HL = 4, 4
PARTS = 3
COMBOS = PARTS * PARTS
ROWS = COMBOS * HD
CTX = 1601
ST = (CTX + P - 1) // P
CTXP = ST * P
KCH = CTXP // HG
CH = 512
NCH = T // CH
FH, FD = 8, 64
INNER = FH * FD
WINDOW = 64
DEPTH = 2
HID = 341
HC = (HID + P - 1) // P
NEG = -3.0e38
PHASES = (1, 2, 3)


class Own:

    def __init__(self, eng, sem, per):
        self.eng, self.sem, self.per, self.base, self.n = eng, sem, per, 0, 0

    def turn(self, i):
        assert self.n in (0, self.per), (self.n, self.per)
        self.base, self.n = i * self.per, 0

    def step(self, ins):
        ins.then_inc(self.sem, 1)
        self.n += 1
        return self.n

    def wait(self, n=None):
        self.eng.wait_ge(self.sem, self.base + (self.n if n is None else n))


def layer_norm(nc, tag, src, dst, ones_mean, eps):
    with ExitStack() as ctx:
        sb = lambda name, shape, dt: ctx.enter_context(nc.sbuf_tensor(f"{tag}_{name}", shape, dt))
        ps = lambda name, shape: ctx.enter_context(nc.psum_tensor(f"{tag}_{name}", shape, F32))
        sem = lambda name: ctx.enter_context(nc.semaphore(f"{tag}_{name}"))
        square = [sb(f"square{u}", [P, CH], F32) for u in range(2)]
        std = [sb(f"std{u}", [P, CH], F32) for u in range(2)]
        mean = [ps(f"mean{u}", [P, CH]) for u in range(2)]
        var = [ps(f"var{u}", [P, CH]) for u in range(2)]
        mean_ready, centered, square_ready = sem("mean_ready"), sem("centered"), sem("square_ready")
        var_ready, std_ready, inverted, normed = sem("var_ready"), sem("std_ready"), sem("inverted"), sem("normed")
        block = ctx.enter_context(nc.Block())

        @block.tensor
        def _(pe):
            with pe.Fori(0, NCH // 2) as i:
                for u in range(2):
                    pe.matmul(mean[u][:, :], ones_mean[:, :], src[:, ds((2 * i + u) * CH, CH)],
                              start=True, stop=True).then_inc(mean_ready, 1)
                for u in range(2):
                    pe.wait_ge(square_ready, 2 * i + u + 1)
                    pe.matmul(var[u][:, :], ones_mean[:, :], square[u][:, :],
                              start=True, stop=True).then_inc(var_ready, 1)

        @block.vector
        def _(dve):
            with dve.Fori(0, NCH // 2) as i:
                for u in range(2):
                    at = ds((2 * i + u) * CH, CH)
                    dve.wait_ge(mean_ready, 2 * i + u + 1)
                    dve.tensor_tensor(dst[:, at], src[:, at], mean[u][:, :], ALU.subtract).then_inc(centered, 1)
                for u in range(2):
                    at = ds((2 * i + u) * CH, CH)
                    dve.wait_ge(std_ready, 2 * i + u + 1)
                    dve.reciprocal(std[u][:, :], std[u][:, :]).then_inc(inverted, 1)
                    dve.wait_ge(inverted, 2 * i + u + 1)
                    dve.tensor_tensor(dst[:, at], dst[:, at], std[u][:, :], ALU.mult).then_inc(normed, 1)

        @block.scalar
        def _(act):
            with act.Fori(0, NCH // 2) as i:
                for u in range(2):
                    act.wait_ge(centered, 2 * i + u + 1)
                    act.activation(square[u][:, :], dst[:, ds((2 * i + u) * CH, CH)],
                                   ACT.Square).then_inc(square_ready, 1)
                for u in range(2):
                    act.wait_ge(var_ready, 2 * i + u + 1)
                    act.activation(std[u][:, :], var[u][:, :], ACT.Sqrt, bias=eps[:, 0:1]).then_inc(std_ready, 1)


def retention_project(nc, zT, w, qp, kp, vtok):
    with ExitStack() as ctx:
        sb = lambda name, shape, dt=F32: ctx.enter_context(nc.sbuf_tensor(f"r_{name}", shape, dt))
        ps = lambda name, shape: ctx.enter_context(nc.psum_tensor(f"r_{name}", shape, F32))
        sem = lambda name: ctx.enter_context(nc.semaphore(f"r_{name}"))
        hc = [sb(f"hc{u}", [P, CH]) for u in range(2)]
        inv_n = [sb(f"inv_n{u}", [P, CH]) for u in range(2)]
        q32 = [sb(f"q32{u}", [P, CH]) for u in range(2)]
        k32 = [sb(f"k32{u}", [P, CH]) for u in range(2)]
        psq = [ps(f"psq{u}", [P, CH]) for u in range(2)]
        psk = [ps(f"psk{u}", [P, CH]) for u in range(2)]
        psn = [ps(f"psn{u}", [P, CH]) for u in range(2)]
        psv = [ps(f"psv{u}", [P, CH]) for u in range(2)]
        h_ready, projected, neg_bn = sem("h_ready"), sem("projected"), sem("neg_bn")
        n_exp, k_ready, hi_ready, mid_ready = sem("n_exp"), sem("k_ready"), sem("hi_ready"), sem("mid_ready")
        q_ready, v_ready, rest, last = sem("q_ready"), sem("v_ready"), sem("rest"), sem("last")
        nbn = sb("nbn", [P, 1])
        block = ctx.enter_context(nc.Block())

        @block.tensor
        def _(pe):
            with pe.Fori(0, NCH // 2) as i:
                for u in range(2):
                    n = 2 * i + u
                    pe.wait_ge(h_ready, n + 1)
                    pe.matmul(psn[u][:, :], w["wn"][:, :], hc[u][:, :], start=True, stop=True)
                    pe.matmul(psq[u][:, :], w["wq"][:, :], hc[u][:, :], start=True, stop=True)
                    pe.matmul(psk[u][:, :], w["wk"][:, :], hc[u][:, :], start=True, stop=True)
                    for t in range(CH // P):
                        ins = pe.matmul(psv[u][:, t * P:(t + 1) * P], hc[u][:, t * P:(t + 1) * P],
                                        w["wv"][:, :], start=True, stop=True)
                    ins.then_inc(projected, 1)

        @block.gpsimd
        def _(pool):
            for u in range(2):
                pool.tensor_copy(hc[u][:, :], zT[:, u * CH:(u + 1) * CH]).then_inc(h_ready, 1)
            with pool.Fori(0, NCH // 2 - 1) as i:
                for u in range(2):
                    n = 2 * i + u
                    pool.wait_ge(last, 2 * n + 2)
                    pool.tensor_copy(hc[u][:, :], zT[:, ds((n + 2) * CH, CH)]).then_inc(h_ready, 1)

        @block.scalar
        def _(act):
            act.mul(nbn[:, :], w["bn"][:, :], -1.0).then_inc(neg_bn, 1)
            act.wait_ge(neg_bn, 1)
            with act.Fori(0, NCH // 2) as i:
                for u in range(2):
                    n = 2 * i + u
                    at = ds(n * CH, CH)
                    act.wait_ge(projected, n + 1)
                    act.activation(inv_n[u][:, :], psn[u][:, :], ACT.Exp, bias=nbn[:, 0:1], scale=-1.0).then_inc(n_exp, 1)
                    act.activation(k32[u][:, :], psk[u][:, :], ACT.Identity, bias=w["bk"][:, 0:1]).then_inc(k_ready, 1)
                    act.wait_ge(k_ready, n + 1)
                    act.activation(kp[:, 0, at], k32[u][:, :], ACT.Copy).then_inc(hi_ready, 1)
                    act.wait_ge(q_ready, n + 1)
                    act.activation(qp[:, 0, at], q32[u][:, :], ACT.Copy).then_inc(hi_ready, 1)
                    act.wait_ge(rest, 2 * n + 1)
                    act.activation(kp[:, 1, at], k32[u][:, :], ACT.Copy).then_inc(mid_ready, 1)
                    act.wait_ge(rest, 2 * n + 2)
                    act.activation(qp[:, 1, at], q32[u][:, :], ACT.Copy).then_inc(mid_ready, 1)

        @block.vector
        def _(dve):
            with dve.Fori(0, NCH // 2) as i:
                for u in range(2):
                    n = 2 * i + u
                    at = ds(n * CH, CH)
                    dve.wait_ge(n_exp, n + 1)
                    dve.scalar_tensor_tensor(q32[u][:, :], psq[u][:, :], w["bq"][:, 0:1], inv_n[u][:, :],
                                             ALU.add, ALU.mult).then_inc(q_ready, 1)
                    dve.tensor_tensor(vtok[:, ds(n * (CH // P), CH // P), :],
                                      psv[u][:, :].rearrange("p (t n) -> p t n", n=P),
                                      w["bv"][:, :].unsqueeze(1).broadcast_to([P, CH // P, P]),
                                      ALU.add).then_inc(v_ready, 1)
                    for m, (x, parts) in enumerate(((k32[u], kp), (q32[u], qp))):
                        dve.wait_ge(hi_ready, 2 * n + m + 1)
                        dve.tensor_tensor(x[:, :], x[:, :], parts[:, 0, at], ALU.subtract).then_inc(rest, 1)
                    for m, (x, parts) in enumerate(((k32[u], kp), (q32[u], qp))):
                        dve.wait_ge(mid_ready, 2 * n + m + 1)
                        dve.tensor_tensor(parts[:, 2, at], x[:, :], parts[:, 1, at], ALU.subtract).then_inc(last, 1)


def retention(nc, xT, w, qp, kp, vtok, causal):
    with ExitStack() as ctx:
        sb = lambda name, shape, dt=F32: ctx.enter_context(nc.sbuf_tensor(f"a_{name}", shape, dt))
        ps = lambda name, shape: ctx.enter_context(nc.psum_tensor(f"a_{name}", shape, F32))
        sem = lambda name: ctx.enter_context(nc.semaphore(f"a_{name}"))
        q9 = [sb(f"q9{u}", [P, H, S], BF16) for u in range(2)]
        k9 = [sb(f"k9{u}", [P, H, S], BF16) for u in range(2)]
        vb = [sb(f"vb{u}", [P, 2, D]) for u in range(2)]
        m0 = [sb(f"m0{r}", [P, HL, S]) for r in range(2)]
        m1 = [sb(f"m1{r}", [P, HL, P]) for r in range(2)]
        oT = sb("oT", [P, HG, S])
        ps0 = [ps(f"ps0{r}", [P, HL, S]) for r in range(2)]
        ps1 = ps("ps1", [P, HL, P])
        pso = [ps(f"pso{r}", [P, 2, S]) for r in range(2)]
        psy = ps("psy", [P, CH])
        zeroed, packs = sem("zeroed"), [sem(f"packs{u}") for u in range(2)]
        v_ready = sem("v_ready")
        score0, score1, masked0, masked1 = sem("score0"), sem("score1"), sem("masked0"), sem("masked1")
        mixed, o_ready, out_ready, added = sem("mixed"), sem("o_ready"), sem("out_ready"), sem("added")
        block = ctx.enter_context(nc.Block())
        NDMA = 2 * COMBOS

        @block.sync
        def _(sp):
            def stack(n, u):
                for a in range(PARTS):
                    for b in range(PARTS):
                        r = (a * PARTS + b) * HD
                        sp.dma_start(q9[u][r:r + HD, :, :], qp[:, a, ds(n * S, S)]).then_inc(packs[u], 16)
                        sp.dma_start(k9[u][r:r + HD, :, :], kp[:, b, ds(n * S, S)]).then_inc(packs[u], 16)

            sp.wait_ge(zeroed, 5)
            stack(0, 0)
            stack(1, 1)
            with sp.Fori(0, B // 2 - 1) as i:
                for u in range(2):
                    n = 2 * i + u
                    sp.wait_ge(score1, (n + 1) * HG)
                    stack(n + 2, u)

        @block.gpsimd
        def _(pool):
            for u in range(2):
                pool.memset(q9[u][64:P, :, :], 0.0).then_inc(zeroed, 1)
                pool.memset(k9[u][64:P, :, :], 0.0).then_inc(zeroed, 1)
            pool.wait_ge(zeroed, 5)
            for u in range(2):
                pool.tensor_copy(vb[u][:, :, :], vtok[:, 2 * u:2 * u + 2, :]).then_inc(v_ready, 1)
            with pool.Fori(0, B // 2 - 1) as i:
                for u in range(2):
                    n = 2 * i + u
                    pool.wait_ge(mixed, (n + 1) * HG)
                    pool.tensor_copy(vb[u][:, :, :], vtok[:, ds(2 * (n + 2), 2), :]).then_inc(v_ready, 1)

        @block.tensor
        def _(pe):
            pe.wait_ge(zeroed, 5)
            with pe.Fori(0, B // 2) as i:
                for u in range(2):
                    n = 2 * i + u

                    def scores(g):
                        c = n * HG + g
                        pe.wait_ge(masked0, c + 1)
                        for h in range(HL):
                            ins = pe.matmul(ps0[g % 2][:, h, :], k9[u][:, HL * g + h, 0:P], q9[u][:, HL * g + h, :],
                                            start=True, stop=True)
                        ins.then_inc(score0, 1)
                        pe.wait_ge(masked1, c + 1)
                        for h in range(HL):
                            ins = pe.matmul(ps1[:, h, :], k9[u][:, HL * g + h, P:S], q9[u][:, HL * g + h, P:S],
                                            start=True, stop=True)
                        ins.then_inc(score1, 1)

                    def mix(g):
                        c = n * HG + g
                        if g == 0:
                            pe.wait_ge(v_ready, n + 1)
                        pe.wait_ge(masked0, c + 3)
                        for h in range(HL):
                            lo = (HL * g + h) * HD
                            pe.matmul(pso[g // 2][32 * h:32 * h + HD, g % 2, :], vb[u][:, 0, lo:lo + HD],
                                      m0[g % 2][:, h, :], start=True, stop=False)
                        pe.wait_ge(masked1, c + 2)
                        for h in range(HL):
                            lo = (HL * g + h) * HD
                            ins = pe.matmul(pso[g // 2][32 * h:32 * h + HD, g % 2, P:S], vb[u][:, 1, lo:lo + HD],
                                            m1[g % 2][:, h, :], start=False, stop=True)
                        ins.then_inc(mixed, 1)

                    pe.wait_ge(packs[u], (i + 1) * NDMA * 16)
                    scores(0)
                    for g in range(1, HG):
                        scores(g)
                        mix(g - 1)
                    mix(HG - 1)
                    for g in range(HG):
                        pe.wait_ge(o_ready, 2 * n + g // 2 + 1)
                        ins = pe.matmul(psy[:, 0:S], w["wo"][:, g, :], oT[:, g, :], start=(g == 0), stop=(g == HG - 1))
                    ins.then_inc(out_ready, 1)

        @block.vector
        def _(dve):
            for r in range(2):
                dve.memset(pso[r][:, :, :], 0.0)
            dve.memset(psy[:, :], 0.0).then_inc(zeroed, 1)
            dve.memset(m0[0][:, 0, 0:1], 0.0).then_inc(masked0, 2)
            dve.memset(m1[0][:, 0, 0:1], 0.0).then_inc(masked1, 1)
            with dve.Fori(0, B // 2) as i:
                for u in range(2):
                    n = 2 * i + u
                    for g in range(HG):
                        c = n * HG + g
                        dve.wait_ge(score0, c + 1)
                        dve.tensor_tensor(m0[g % 2][:, :, :], ps0[g % 2][:, :, :],
                                          causal[:, :].unsqueeze(1).broadcast_to([P, HL, S]),
                                          ALU.mult).then_inc(masked0, 1)
                        dve.wait_ge(score1, c + 1)
                        dve.tensor_tensor(m1[g % 2][:, :, :], ps1[:, :, :],
                                          causal[:, 0:P].unsqueeze(1).broadcast_to([P, HL, P]),
                                          ALU.mult).then_inc(masked1, 1)
                    dve.wait_ge(out_ready, n + 1)
                    at = ds(n * S, S)
                    dve.scalar_tensor_tensor(xT[:, at], psy[:, 0:S], w["bo"][:, 0:1], xT[:, at],
                                             ALU.add, ALU.add).then_inc(added, 1)

        @block.scalar
        def _(act):
            act.wait_ge(zeroed, 5)
            with act.Fori(0, B // 2) as i:
                for u in range(2):
                    n = 2 * i + u
                    for r in range(2):
                        act.wait_ge(mixed, n * HG + 2 * r + 2)
                        act.activation(oT[:, 2 * r:2 * r + 2, :], pso[r][:, :, :], ACT.Copy).then_inc(o_ready, 1)


def cross_queries(nc, zT, wq, qp):
    with ExitStack() as ctx:
        sb = lambda name, shape, dt=F32: ctx.enter_context(nc.sbuf_tensor(f"xq_{name}", shape, dt))
        ps = lambda name, shape: ctx.enter_context(nc.psum_tensor(f"xq_{name}", shape, F32))
        sem = lambda name: ctx.enter_context(nc.semaphore(f"xq_{name}"))
        rest = [sb(f"rest{u}", [P, CH]) for u in range(2)]
        psq = [ps(f"psq{u}", [P, CH]) for u in range(2)]
        projected, hi_ready, rest_ready = sem("projected"), sem("hi_ready"), sem("rest_ready")
        mid_ready, lo_ready = sem("mid_ready"), sem("lo_ready")
        block = ctx.enter_context(nc.Block())

        @block.tensor
        def _(pe):
            for n in range(2):
                pe.matmul(psq[n][:, :], wq[:, :], zT[:, n * CH:(n + 1) * CH], start=True, stop=True).then_inc(projected, 1)
            with pe.Fori(0, NCH // 2 - 1) as i:
                for u in range(2):
                    n = 2 * i + u
                    pe.wait_ge(rest_ready, n + 1)
                    pe.matmul(psq[u][:, :], wq[:, :], zT[:, ds((n + 2) * CH, CH)],
                              start=True, stop=True).then_inc(projected, 1)

        @block.scalar
        def _(act):
            with act.Fori(0, NCH // 2) as i:
                for u in range(2):
                    n = 2 * i + u
                    act.wait_ge(projected, n + 1)
                    act.activation(qp[:, 0, ds(n * CH, CH)], psq[u][:, :], ACT.Copy).then_inc(hi_ready, 1)
                    act.wait_ge(rest_ready, n + 1)
                    act.activation(qp[:, 1, ds(n * CH, CH)], rest[u][:, :], ACT.Copy).then_inc(mid_ready, 1)

        @block.vector
        def _(dve):
            with dve.Fori(0, NCH // 2) as i:
                for u in range(2):
                    n = 2 * i + u
                    at = ds(n * CH, CH)
                    dve.wait_ge(hi_ready, n + 1)
                    dve.tensor_tensor(rest[u][:, :], psq[u][:, :], qp[:, 0, at], ALU.subtract).then_inc(rest_ready, 1)
                    dve.wait_ge(mid_ready, n + 1)
                    dve.tensor_tensor(qp[:, 2, at], rest[u][:, :], qp[:, 1, at], ALU.subtract).then_inc(lo_ready, 1)


def cross_attention(nc, xT, w, qp, context):
    UNITS = HG * ST
    HALF = H // 2
    NSTACK = 2 * COMBOS * 16
    VCH = [(0, 4), (4, 7), (7, 10), (10, 13)]
    K_AT = {9: 0, 16: 1, 22: 2, 29: 3}
    V_AT = {32: 0, 35: 1, 42: 2, 45: 3}
    WO_AT = 3
    NP = 4
    with ExitStack() as ctx:
        sb = lambda name, shape, dt=F32: ctx.enter_context(nc.sbuf_tensor(f"x_{name}", shape, dt))
        ps = lambda name, shape: ctx.enter_context(nc.psum_tensor(f"x_{name}", shape, F32))
        sem = lambda name: ctx.enter_context(nc.semaphore(f"x_{name}"))
        cT = sb("cT", [P, CTXP])
        kx = [sb(f"kx{e}", [P, HALF, CTXP], BF16) for e in range(2)]
        qx = [sb(f"qx{e}", [P, HALF, S], BF16) for e in range(2)]
        kp = sb("kp", [P, PARTS, CTXP], BF16)
        krest = sb("krest", [P, KCH])
        vnext = sb("vnext", [P, ST, D])
        v = sb("v", [P, ST, D])
        probs = [sb(f"probs{r}", [P, HL, S]) for r in range(NP)]
        oT = sb("oT", [P, HG, S])
        pss = [ps(f"pss{r}", [P, HL, S]) for r in range(2)]
        acc = [ps(f"acc{r}", [P, CH]) for r in range(2)]
        psk = ps("psk", [P, CH])
        psv = ps("psv", [P, CH])
        zeroed, c_landed, stacked = sem("zeroed"), sem("c_landed"), [sem(f"stacked{e}") for e in range(2)]
        k_projected, k_cut, v_projected, v_copied, v_set = (
            sem("k_projected"), sem("k_cut"), sem("v_projected"), sem("v_copied"), sem("v_set"))
        scored, weighed, mixed, o_ready = sem("scored"), sem("weighed"), sem("mixed"), sem("o_ready")
        out_ready, added = sem("out_ready"), sem("added")
        block = ctx.enter_context(nc.Block())

        def turns(eng, body):
            body(0)
            with eng.Fori(1, B - 1) as i:
                body(i)
            body(B - 1, last=True)

        @block.sync
        def _(sp):
            def load(n):
                sp.dma_start(cT[:, :], context[ds(n, 1), :, :].rearrange("a p s -> (a p) s")).then_inc(c_landed, 16)

            def stack(n, e):
                for a in range(PARTS):
                    for b in range(PARTS):
                        r = (a * PARTS + b) * HD
                        sp.dma_start(qx[e][r:r + HD, :, :],
                                     qp[64 * e:64 * e + 64, a, ds(n * S, S)]).then_inc(stacked[e], 16)
                        sp.dma_start(kx[e][r:r + HD, :, :], kp[64 * e:64 * e + 64, b, :]).then_inc(stacked[e], 16)

            def turn(n, last=False):
                if not (isinstance(n, int) and n == 0):
                    sp.wait_ge(scored, n * UNITS)
                stack(n, 1)
                if not last:
                    sp.wait_ge(k_cut, (n + 2) * 4 * HG)
                    stack(n + 1, 0)
                    if not (isinstance(n, int) and n == B - 2):
                        sp.wait_ge(v_projected, (n + 2) * HG)
                        load(n + 2)

            load(0)
            sp.wait_ge(zeroed, 5)
            sp.wait_ge(k_cut, 4 * HG)
            stack(0, 0)
            sp.wait_ge(v_projected, HG)
            load(1)
            turn(0)
            with sp.Fori(1, B - 2) as i:
                turn(i)
            turn(B - 2)
            turn(B - 1, last=True)

        @block.gpsimd
        def _(pool):
            for e in range(2):
                pool.memset(qx[e][64:P, :, :], 0.0).then_inc(zeroed, 1)
                pool.memset(kx[e][64:P, :, :], 0.0).then_inc(zeroed, 1)

        @block.tensor
        def _(pe):
            def project_keys(m, c):
                pe.wait_ge(c_landed, (m + 1) * 16)
                if not (isinstance(m, int) and m == 0 and c == 0):
                    pe.wait_ge(k_cut, (m * HG + c) * 4 - 2)
                pe.matmul(psk[:, 0:KCH], w["wk"][:, :], cT[:, c * KCH:(c + 1) * KCH],
                          start=True, stop=True).then_inc(k_projected, 1)

            def project_values(m, c):
                if not (isinstance(m, int) and m == 0 and c == 0):
                    pe.wait_ge(v_copied, m * HG + c)
                if c == 0 and not (isinstance(m, int) and m < 2):
                    pe.wait_ge(added, m - 1)
                for j in range(*VCH[c]):
                    ins = pe.matmul(psv[:, (j - VCH[c][0]) * P:(j - VCH[c][0] + 1) * P], cT[:, j * P:(j + 1) * P],
                                    w["wv"][:, :], start=True, stop=True)
                ins.then_inc(v_projected, 1)

            def score(n, u):
                g, j = u // ST, u % ST
                if u % (UNITS // 2) == 0:
                    pe.wait_ge(stacked[g // 2], (n + 1) * NSTACK)
                if not (isinstance(n, int) and n == 0 and u < 2):
                    pe.wait_ge(weighed, n * UNITS + u - 1)
                for h in range(HL):
                    hh = (g % 2) * HL + h
                    ins = pe.matmul(pss[u % 2][:, h, :], kx[g // 2][:, hh, j * P:(j + 1) * P], qx[g // 2][:, hh, :],
                                    start=True, stop=True)
                ins.then_inc(scored, 1)

            def mix(n, u):
                g, j = u // ST, u % ST
                if j == 0:
                    pe.wait_ge(v_set, n * HG + g + 1)
                    if not (isinstance(n, int) and n == 0 and g < 2):
                        pe.wait_ge(o_ready, n * HG + g - 1)
                pe.wait_ge(weighed, n * UNITS + u + 1)
                for h in range(HL):
                    lo = (HL * g + h) * HD
                    ins = pe.matmul(acc[g % 2][32 * h:32 * h + HD, 0:S], v[:, j, lo:lo + HD],
                                    probs[u % NP][:, h, :], start=(j == 0), stop=(j == ST - 1))
                ins.then_inc(mixed, 1)

            def project_out(n):
                pe.wait_ge(o_ready, (n + 1) * HG)
                for g in range(HG):
                    ins = pe.matmul(psv[:, 0:S], w["wo"][:, g, :], oT[:, g, :], start=(g == 0), stop=(g == HG - 1))
                ins.then_inc(out_ready, 1)

            def turn(n, last=False):
                first = isinstance(n, int) and n == 0
                for u in range(UNITS):
                    if u + 2 < UNITS:
                        score(n, u + 2)
                    elif not last:
                        score(n + 1, u + 2 - UNITS)
                    mix(n, u)
                    if u == WO_AT and not first:
                        project_out(n - 1)
                    if u in K_AT and not last:
                        project_keys(n + 1, K_AT[u])
                    if u in V_AT and not last:
                        project_values(n + 1, V_AT[u])

            pe.wait_ge(zeroed, 5)
            for c in range(HG):
                project_keys(0, c)
            for c in range(HG):
                project_values(0, c)
            score(0, 0)
            score(0, 1)
            turns(pe, turn)
            project_out(B - 1)

        @block.scalar
        def _(act):
            def turn(n, last=False):
                for u in range(UNITS):
                    act.wait_ge(scored, n * UNITS + u + 1)
                    if not (isinstance(n, int) and n == 0 and u < NP):
                        act.wait_ge(mixed, n * UNITS + u - NP + 1)
                    act.activation(probs[u % NP][:, :, :], pss[u % 2][:, :, :], ACT.Sigmoid,
                                   scale=HD ** -0.5).then_inc(weighed, 1)

            turns(act, turn)

        @block.vector
        def _(dve):
            def cut_keys(m, c):
                at = slice(c * KCH, (c + 1) * KCH)
                done = (m * HG + c) * 4
                dve.wait_ge(k_projected, m * HG + c + 1)
                dve.tensor_copy(kp[:, 0, at], psk[:, 0:KCH]).then_inc(k_cut, 1)
                dve.wait_ge(k_cut, done + 1)
                dve.tensor_tensor(krest[:, :], psk[:, 0:KCH], kp[:, 0, at], ALU.subtract).then_inc(k_cut, 1)
                dve.wait_ge(k_cut, done + 2)
                dve.tensor_copy(kp[:, 1, at], krest[:, :]).then_inc(k_cut, 1)
                dve.wait_ge(k_cut, done + 3)
                dve.tensor_tensor(kp[:, 2, at], krest[:, :], kp[:, 1, at], ALU.subtract).then_inc(k_cut, 1)

            def copy_values(m, c):
                a, b = VCH[c]
                dve.wait_ge(v_projected, m * HG + c + 1)
                dve.tensor_copy(vnext[:, a:b, :],
                                psv[:, 0:(b - a) * P].rearrange("p (t n) -> p t n", n=P)).then_inc(v_copied, 1)

            def set_values(n, g):
                dve.wait_ge(v_copied, (n + 1) * HG)
                if not (isinstance(n, int) and n == 0):
                    dve.wait_ge(mixed, (n - 1) * UNITS + (g + 1) * ST)
                lo = g * HL * HD
                dve.tensor_copy(v[:, :, lo:lo + HL * HD], vnext[:, :, lo:lo + HL * HD]).then_inc(v_set, 1)

            def take_out(n, g):
                dve.wait_ge(mixed, n * UNITS + (g + 1) * ST)
                dve.tensor_copy(oT[:, g, :], acc[g % 2][:, 0:S]).then_inc(o_ready, 1)

            def add(n):
                dve.wait_ge(out_ready, n + 1)
                at = ds(n * S, S)
                dve.tensor_tensor(xT[:, at], psv[:, 0:S], xT[:, at], ALU.add).then_inc(added, 1)

            def turn(n, last=False):
                first = isinstance(n, int) and n == 0
                if not first:
                    take_out(n - 1, 3)
                for g in range(1, HG):
                    set_values(n, g)
                if not first:
                    add(n - 1)
                if not last:
                    dve.wait_ge(stacked[1], (n + 1) * NSTACK)
                    cut_keys(n + 1, 0)
                take_out(n, 0)
                if not last:
                    cut_keys(n + 1, 1)
                    cut_keys(n + 1, 2)
                take_out(n, 1)
                if not last:
                    cut_keys(n + 1, 3)
                    copy_values(n + 1, 0)
                    copy_values(n + 1, 1)
                take_out(n, 2)
                if not last:
                    copy_values(n + 1, 2)
                    copy_values(n + 1, 3)
                    set_values(n + 1, 0)

            for r in range(2):
                dve.memset(acc[r][:, :], 0.0)
            dve.memset(oT[:, :, :], 0.0).then_inc(zeroed, 1)
            for c in range(HG):
                cut_keys(0, c)
            for c in range(HG):
                copy_values(0, c)
            set_values(0, 0)
            turns(dve, turn)
            take_out(B - 1, 3)
            add(B - 1)


def local_attention(nc, tag, zT, w):
    NSU = 6
    UNIT = [(0, (0, 1, 2, 3)), (0, (4, 5, 6, 7)), (1, (0, 1)), (1, (2, 3)), (1, (4, 5)), (1, (6, 7))]
    NEWTON = 12
    QK = 2 * FH
    with ExitStack() as ctx:
        sb = lambda name, shape, dt=F32: ctx.enter_context(nc.sbuf_tensor(f"{tag}_{name}", shape, dt))
        ps = lambda name, shape: ctx.enter_context(nc.psum_tensor(f"{tag}_{name}", shape, F32))
        sem = lambda name: ctx.enter_context(nc.semaphore(f"{tag}_{name}"))
        hs = sb("hs", [P, S])
        tabA, tabB = sb("tabA", [P, 2, 2, FD]), sb("tabB", [P, 2, 2, FD])
        square = sb("square", [P, QK, FD])
        direct = [sb(f"direct{t}", [P, QK, FD]) for t in range(2)]
        turned_half = [sb(f"turned_half{t}", [P, QK, FD]) for t in range(2)]
        sumsq, inv_norm = sb("sumsq", [P, 2, QK]), sb("inv_norm", [P, 2, QK])
        tmp_a, tmp_b = sb("tmp_a", [P, 2, QK]), sb("tmp_b", [P, 2, QK])
        qz = [sb(f"qz{u}", [P, FH, S]) for u in range(2)]
        kT = [sb(f"kT{u}", [P, FH // 2, S]) for u in range(2)]
        vt = [sb(f"vt{u}", [P, 2, INNER]) for u in range(2)]
        sim = [sb(f"sim{r}", [P, CH]) for r in range(2)]
        prob = [sb(f"prob{r}", [P, CH]) for r in range(2)]
        probT = [sb(f"probT{r}", [P, CH]) for r in range(2)]
        top, neg_top = [sb(f"top{r}", [P, 4]) for r in range(2)], [sb(f"neg_top{r}", [P, 4]) for r in range(2)]
        total, inv_total = [sb(f"total{r}", [P, 4]) for r in range(2)], [sb(f"inv_total{r}", [P, 4]) for r in range(2)]
        oT = sb("oT", [P, FH // 2, S])
        psqk = ps("psqk", [P, QK, FD])
        psvy = ps("psvy", [P, CH])
        pst = ps("pst", [P, CH])
        pss = [ps(f"pss{r}", [P, CH]) for r in range(2)]
        pso = ps("pso", [P, FH // 2, S])
        names = ("ready", "shifted", "projected", "squared", "v_ready", "summed", "rotated", "joined", "newton", "scaled",
                 "flipped", "placed", "scored", "masked", "topped", "negated", "exped", "inverted", "normed", "turned",
                 "copied", "valued", "o_ready", "out_ready", "added")
        (ready, shifted, projected, squared, v_ready, summed, rotated, joined, newton, scaled, flipped, placed, scored,
         masked, topped, negated, exped, inverted, normed, turned, copied, valued, o_ready, out_ready, added) = (
            sem(x) for x in names)
        block = ctx.enter_context(nc.Block())

        def turns(eng, body):
            with eng.Fori(0, B // 2 - 1) as i:
                for u in range(2):
                    body(2 * i + u, u)
            body(B - 2, 0)
            body(B - 1, 1, last=True)

        def unit(tile, s):
            return tile[:, :].rearrange("p (h k) -> p h k", h=len(UNIT[s][1]))

        @block.gpsimd
        def _(pool):
            def shift(n, joins):
                if joins is not None:
                    pool.wait_ge(joined, joins)
                pool.tensor_copy(hs[0:64, :], zT[0:64, ds(n * S, S)]).then_inc(shifted, 1)
                pool.tensor_copy(hs[64:P, 1:S], zT[64:P, ds(n * S, S - 1)]).then_inc(shifted, 1)

            def join(n, t, shifts):
                pool.wait_ge(shifted, shifts)
                pool.wait_ge(rotated, (2 * n + t) * 3 + 3)
                pool.tensor_tensor(direct[t][:, :, :], direct[t][:, :, :], turned_half[t][:, :, :],
                                   ALU.add).then_inc(joined, 1)

            def turn(n, u, last=False):
                if not last:
                    join(n + 1, 0, 2 * n + 4)
                    join(n + 1, 1, 2 * n + 4)
                    if not isinstance(n, int):
                        pool.wait_ge(projected, 2 * n + 4)
                        shift(n + 2, 2 * n + 4)

            pool.wait_ge(ready, 2)
            shift(0, None)
            join(0, 0, 2)
            join(0, 1, 2)
            pool.wait_ge(projected, 2)
            shift(1, 2)
            turns(pool, turn)

        @block.tensor
        def _(pe):
            def project(n, t):
                for m in range(2):
                    pe.matmul(psqk[:, m * FH:(m + 1) * FH, :], hs[:, t * P:(t + 1) * P],
                              w["wqkv"][:, m * INNER:(m + 1) * INNER], start=True, stop=True)
                pe.matmul(psvy[:, :], hs[:, t * P:(t + 1) * P], w["wqkv"][:, 2 * INNER:3 * INNER],
                          start=True, stop=True).then_inc(projected, 1)

            def flip(n, t):
                pe.wait_ge(scaled, 2 * n + t + 1)
                for p in range(FH):
                    ins = pe.transpose(psqk[:, 2 * p:2 * p + 2, :].rearrange("p h d -> p (h d)"),
                                       direct[t][:, 2 * p:2 * p + 2, :].rearrange("p h d -> p (h d)"), w["identity"][:, :])
                ins.then_inc(flipped, 1)

            def score(n, u, s):
                blk, heads = UNIT[s]
                k = CH // len(heads)
                out = unit(pss[s % 2], s)
                for m, h in enumerate(heads):
                    ins = pe.matmul(out[:, m, :], qz[u][:, h, blk * P:(blk + 1) * P], kT[u][:, h // 2, 0:k],
                                    start=True, stop=True)
                ins.then_inc(scored, 1)

            def turn_over(n, s):
                pe.wait_ge(normed, n * NSU + s + 1)
                for m in range(CH // P):
                    ins = pe.transpose(pst[:, m * P:(m + 1) * P], prob[s % 2][:, m * P:(m + 1) * P], w["identity"][:, :])
                ins.then_inc(turned, 1)

            def value(n, u, s):
                blk, heads = UNIT[s]
                pe.wait_ge(copied, n * NSU + s + 1)
                for m, h in enumerate(heads):
                    for j in range(blk + 1):
                        at = (m * (blk + 1) + j) * P
                        ins = pe.matmul(pso[64 * (h % 2):64 * (h % 2) + 64, h // 2, blk * P:(blk + 1) * P],
                                        vt[u][:, j, h * FD:(h + 1) * FD], probT[s % 2][:, at:at + P],
                                        start=(j == 0), stop=(j == blk))
                ins.then_inc(valued, 1)

            def project_out(n, last):
                pe.wait_ge(o_ready, 2 * n + 2)
                if not last:
                    pe.wait_ge(v_ready, 2 * n + 4)
                for p in range(FH // 2):
                    ins = pe.matmul(psvy[:, 0:S], w["wo"][:, p, :], oT[:, p, :], start=(p == 0), stop=(p == FH // 2 - 1))
                ins.then_inc(out_ready, 1)

            def front_start(n, t):
                if t == 0:
                    pe.wait_ge(shifted, 2 * n + 2)
                else:
                    pe.wait_ge(rotated, (2 * n + t) * 3)
                    pe.wait_ge(v_ready, 2 * n + t)
                project(n, t)

            def turn(n, u, last=False):
                pe.wait_ge(placed, 6 * n + 6)
                score(n, u, 0)
                score(n, u, 1)
                if not last:
                    pe.wait_ge(added, n + 1)
                    front_start(n + 1, 0)
                for s in range(4):
                    turn_over(n, s)
                    score(n, u, s + 2)
                    value(n, u, s)
                    if s == 1 and not last:
                        front_start(n + 1, 1)
                turn_over(n, 4)
                value(n, u, 4)
                if not last:
                    flip(n + 1, 0)
                turn_over(n, 5)
                value(n, u, 5)
                if not last:
                    pe.wait_ge(placed, 6 * n + 9)
                    flip(n + 1, 1)
                project_out(n, last)

            pe.wait_ge(ready, 4)
            front_start(0, 0)
            front_start(0, 1)
            flip(0, 0)
            pe.wait_ge(placed, 3)
            flip(0, 1)
            turns(pe, turn)

        @block.vector
        def _(dve):
            def sums_and_rotary(n, t):
                dve.wait_ge(squared, 2 * n + t + 1)
                dve.tensor_reduce(sumsq[:, t, :], square[:, :, :], AX.X, ALU.add).then_inc(summed, 1)
                heads = lambda ap: ap.rearrange("p (m h) d -> p m h d", m=2)
                half = FD // 2
                table = lambda tab, lo, hi: tab[:, t, :, lo:hi].unsqueeze(2).broadcast_to([P, 2, FH, hi - lo])
                dve.tensor_tensor(heads(direct[t][:, :, :]), heads(psqk[:, :, :]), table(tabA, 0, FD),
                                  ALU.mult).then_inc(rotated, 1)
                for lo, frm in ((0, half), (half, 0)):
                    dve.tensor_tensor(heads(turned_half[t][:, :, lo:lo + half]), heads(psqk[:, :, frm:frm + half]),
                                      table(tabB, lo, lo + half), ALU.mult).then_inc(rotated, 1)

            def inverse_norms(n):
                own = Own(dve, newton, NEWTON)
                own.turn(n)
                flat = lambda x: x[:, :, :].rearrange("p t h -> p (t h)")
                x, y, a, b = flat(sumsq), flat(inv_norm), flat(tmp_a), flat(tmp_b)
                dve.wait_ge(summed, 2 * n + 2)
                own.step(dve.tensor_scalar(x, x, 1e-24, None, ALU.max))
                own.wait()
                own.step(dve.tensor_scalar(a.bitcast(I32), x.bitcast(I32), 1, None, ALU.logical_shift_right))
                own.wait()
                own.step(dve.tensor_scalar(y.bitcast(I32), a.bitcast(I32), -1.0, float(0x5f3759df), ALU.mult, ALU.add))
                for _ in range(3):
                    own.wait()
                    own.step(dve.scalar_tensor_tensor(a, y, -0.5, x, ALU.mult, ALU.mult))
                    own.wait()
                    own.step(dve.tensor_tensor(b, a, y, ALU.mult))
                    own.wait()
                    own.step(dve.scalar_tensor_tensor(y, b, 1.5, y, ALU.add, ALU.mult))
                assert own.n == NEWTON

            def scale(n, t):
                dve.wait_ge(newton, (n + 1) * NEWTON)
                dve.wait_ge(joined, 2 * n + t + 1)
                dve.tensor_tensor(direct[t][:, :, :], direct[t][:, :, :],
                                  inv_norm[:, t, :].unsqueeze(2).broadcast_to([P, QK, FD]), ALU.mult).then_inc(scaled, 1)

            def mask(n, s):
                blk, heads = UNIT[s]
                r, c, nh = s % 2, n * NSU + s, len(heads)
                k = CH // nh
                dve.wait_ge(scored, c + 1)
                dve.tensor_tensor(unit(sim[r], s), unit(pss[r], s),
                                  w["window"][:, blk, 0:k].unsqueeze(1).broadcast_to([P, nh, k]), ALU.add).then_inc(masked, 1)
                dve.wait_ge(masked, c + 1)
                dve.tensor_reduce(top[r][:, 0:nh], unit(sim[r], s), AX.X, ALU.max).then_inc(topped, 1)
                dve.wait_ge(topped, c + 1)
                dve.tensor_scalar(neg_top[r][:, 0:nh], top[r][:, 0:nh], -1.0, None, ALU.mult).then_inc(negated, 1)

            def norm(n, s):
                blk, heads = UNIT[s]
                r, c, nh = s % 2, n * NSU + s, len(heads)
                dve.wait_ge(exped, c + 1)
                dve.reciprocal(inv_total[r][:, 0:nh], total[r][:, 0:nh]).then_inc(inverted, 1)
                dve.wait_ge(inverted, c + 1)
                dve.tensor_tensor(unit(prob[r], s), unit(prob[r], s),
                                  inv_total[r][:, 0:nh].unsqueeze(2).broadcast_to([P, nh, CH // nh]),
                                  ALU.mult).then_inc(normed, 1)

            def turn(n, u, last=False):
                mask(n, 0)
                mask(n, 1)
                norm(n, 0)
                if not last:
                    sums_and_rotary(n + 1, 0)
                mask(n, 2)
                norm(n, 1)
                mask(n, 3)
                norm(n, 2)
                if not last:
                    sums_and_rotary(n + 1, 1)
                mask(n, 4)
                norm(n, 3)
                if not last:
                    inverse_norms(n + 1)
                mask(n, 5)
                norm(n, 4)
                if not last:
                    scale(n + 1, 0)
                norm(n, 5)
                if not last:
                    scale(n + 1, 1)
                dve.wait_ge(out_ready, n + 1)
                at = ds(n * S, S)
                dve.tensor_tensor(zT[:, at], psvy[:, 0:S], zT[:, at], ALU.add).then_inc(added, 1)

            dve.memset(hs[64:P, 0:1], 0.0).then_inc(ready, 1)
            dve.memset(qz[0][:, :, :], 0.0).then_inc(ready, 1)
            dve.memset(qz[1][:, :, :], 0.0).then_inc(ready, 1)
            for tab, const, scales in ((tabA, "cosine", "scales"), (tabB, "sine", "scales_turned")):
                ins = dve.tensor_tensor(tab[:, :, :, :].rearrange("p t m d -> p t (m d)"),
                                        w[const][:, :, :, :].rearrange("p t m d -> p t (m d)"),
                                        w[scales][:, :, :].rearrange("p m d -> p (m d)").unsqueeze(1).broadcast_to([P, 2, 2 * FD]),
                                        ALU.mult)
            ins.then_inc(ready, 1)
            dve.wait_ge(ready, 4)
            dve.memset(tmp_a[:, :, :], 0.0).then_inc(added, 1)
            sums_and_rotary(0, 0)
            sums_and_rotary(0, 1)
            inverse_norms(0)
            scale(0, 0)
            scale(0, 1)
            turns(dve, turn)

        @block.scalar
        def _(act):
            def square_and_values(n, t, u):
                act.wait_ge(projected, 2 * n + t + 1)
                act.activation(square[:, :, :], psqk[:, :, :], ACT.Square).then_inc(squared, 1)
                act.activation(vt[u][:, t, :], psvy[:, :], ACT.Copy).then_inc(v_ready, 1)

            def place(n, t, u):
                act.wait_ge(flipped, 2 * n + t + 1)
                q = psqk[:, 0:FH, :].rearrange("p (h e) d -> p h (e d)", e=2)
                k = psqk[:, FH:QK, :].rearrange("p (h e) d -> p h (e d)", e=2)
                at = slice(t * P, (t + 1) * P)
                for e in range(2):
                    rows = slice(64 * e, 64 * e + 64)
                    act.activation(qz[u][rows, e:FH:2, at], q[rows, :, :], ACT.Copy).then_inc(placed, 1)
                act.activation(kT[u][:, :, at], k, ACT.Copy).then_inc(placed, 1)

            def exps(n, s):
                blk, heads = UNIT[s]
                r = s % 2
                act.wait_ge(negated, n * NSU + s + 1)
                for m in range(len(heads)):
                    ins = act.activation(unit(prob[r], s)[:, m, :], unit(sim[r], s)[:, m, :], ACT.Exp,
                                         bias=neg_top[r][:, m:m + 1], accum_out=total[r][:, m:m + 1])
                ins.then_inc(exped, 1)

            def copy(n, s):
                act.wait_ge(turned, n * NSU + s + 1)
                act.activation(probT[s % 2][:, :], pst[:, :], ACT.Copy).then_inc(copied, 1)

            def turn(n, u, last=False):
                exps(n, 0)
                exps(n, 1)
                if not last:
                    square_and_values(n + 1, 0, 1 - u)
                copy(n, 0)
                exps(n, 2)
                copy(n, 1)
                exps(n, 3)
                if not last:
                    square_and_values(n + 1, 1, 1 - u)
                copy(n, 2)
                exps(n, 4)
                copy(n, 3)
                exps(n, 5)
                copy(n, 4)
                if not last:
                    place(n + 1, 0, 1 - u)
                copy(n, 5)
                if not last:
                    place(n + 1, 1, 1 - u)
                act.wait_ge(valued, (n + 1) * NSU)
                for p in range(2):
                    act.activation(oT[:, 2 * p:2 * p + 2, :], pso[:, 2 * p:2 * p + 2, :], ACT.Copy).then_inc(o_ready, 1)

            act.wait_ge(ready, 4)
            square_and_values(0, 0, 0)
            square_and_values(0, 1, 0)
            place(0, 0, 0)
            place(0, 1, 0)
            turns(act, turn)


def shift_tokens(nc, tag, zT, hs):
    with ExitStack() as ctx:
        shifted = ctx.enter_context(nc.semaphore(f"{tag}_shifted"))
        block = ctx.enter_context(nc.Block())
        by_batch = lambda x: x[64:P, :].rearrange("p (b s) -> p b s", b=B)

        @block.vector
        def _(dve):
            dve.tensor_copy(hs[0:64, :], zT[0:64, :]).then_inc(shifted, 1)
            dve.tensor_copy(by_batch(hs)[:, :, 1:S], by_batch(zT)[:, :, 0:S - 1]).then_inc(shifted, 1)
            dve.memset(by_batch(hs)[:, :, 0:1], 0.0).then_inc(shifted, 1)
            dve.wait_ge(shifted, 3)


def gated_unit(nc, tag, zT, hs, w):
    with ExitStack() as ctx:
        sb = lambda name, shape, dt=F32: ctx.enter_context(nc.sbuf_tensor(f"{tag}_{name}", shape, dt))
        ps = lambda name, shape: ctx.enter_context(nc.psum_tensor(f"{tag}_{name}", shape, F32))
        sem = lambda name: ctx.enter_context(nc.semaphore(f"{tag}_{name}"))
        psa = [ps(f"psa{c}", [P, CH]) for c in range(HC)]
        psg = [ps(f"psg{c}", [P, CH]) for c in range(HC)]
        psy = ps("psy", [P, CH])
        gelu = [sb(f"gelu{c}", [P, CH]) for c in range(HC)]
        gated = [sb(f"gated{c}", [P, CH]) for c in range(HC)]
        affine, up, gelu_ready, gate_ready = sem("affine"), sem("up"), sem("gelu_ready"), sem("gate_ready")
        down, added = sem("down"), sem("added")
        block = ctx.enter_context(nc.Block())

        @block.tensor
        def _(pe):
            pe.wait_ge(affine, 1)
            with pe.Fori(0, NCH) as n:
                for c in range(HC):
                    for m, out in ((HC + c, psg[c]), (c, psa[c])):
                        ins = pe.matmul(out[:, :], w["w1"][:, m * P:(m + 1) * P], hs[:, ds(n * CH, CH)],
                                        start=True, stop=True)
                    ins.then_inc(up, 1)
                for c in range(HC):
                    pe.wait_ge(gate_ready, HC * n + c + 1)
                    ins = pe.matmul(psy[:, :], w["w2"][:, c, :], gated[c][:, :], start=(c == 0), stop=(c == HC - 1))
                ins.then_inc(down, 1)

        @block.scalar
        def _(act):
            with act.Fori(0, NCH) as n:
                for c in range(HC):
                    act.wait_ge(up, HC * n + c + 1)
                    act.activation(gelu[c][:, :], psg[c][:, :], ACT.Gelu,
                                   bias=w["b1"][:, HC + c:HC + c + 1]).then_inc(gelu_ready, 1)

        @block.vector
        def _(dve):
            dve.tensor_scalar(hs[:, :], hs[:, :], w["ln_g"][:, 0:1], w["ln_b"][:, 0:1], ALU.mult, ALU.add).then_inc(affine, 1)
            with dve.Fori(0, NCH) as n:
                for c in range(HC):
                    dve.wait_ge(gelu_ready, HC * n + c + 1)
                    dve.scalar_tensor_tensor(gated[c][:, :], psa[c][:, :], w["b1"][:, c:c + 1], gelu[c][:, :],
                                             ALU.add, ALU.mult).then_inc(gate_ready, 1)
                dve.wait_ge(down, n + 1)
                at = ds(n * CH, CH)
                dve.scalar_tensor_tensor(zT[:, at], psy[:, :], w["b2"][:, 0:1], zT[:, at],
                                         ALU.add, ALU.add).then_inc(added, 1)


def build(nc, a, out):
    with ExitStack() as ctx:
        sb = lambda name, shape, dt=F32: ctx.enter_context(nc.sbuf_tensor(name, shape, dt))
        xT = sb("xT", [P, T])
        zT = sb("zT", [P, T])
        ones_mean = sb("ones_mean", [P, P])
        eps = sb("eps", [P, 1])
        loaded, made, stored = (ctx.enter_context(nc.semaphore(n)) for n in ("loaded", "made", "stored"))
        if 1 in PHASES or 2 in PHASES or 3 in PHASES:
            with nc.Block() as block:
                @block.sync
                def _(sp):
                    sp.dma_start(xT[:, :], a["x"]).then_inc(loaded, 16)
                    sp.wait_ge(loaded, 16)

                @block.vector
                def _(dve):
                    dve.memset(ones_mean[:, :], 1.0 / D)
                    dve.memset(eps[:, :], 1e-5).then_inc(made, 1)
                    dve.wait_ge(made, 1)
        if 1 in PHASES:
            layer_norm(nc, "n1", xT, zT, ones_mean, eps)
            with ExitStack() as c1:
                w = load_weights(nc, c1, "w1", {
                    "wq": (a["r_wq"], [P, D]), "wk": (a["r_wk"], [P, D]), "wn": (a["r_wn"], [P, D]),
                    "wv": (a["r_wv"], [P, D]), "bq": (a["r_bq"], [P, 1]), "bk": (a["r_bk"], [P, 1]),
                    "bn": (a["r_bn"], [P, 1]), "bv": (a["r_bv"], [P, D]), "wo": (a["r_wo"], [P, HG, D]),
                    "bo": (a["r_bo"], [P, 1]), "causal": (a["causal"], [P, S])})
                s1 = lambda name, shape, dt=F32: c1.enter_context(nc.sbuf_tensor(name, shape, dt))
                qp, kp = s1("qp", [P, PARTS, T], BF16), s1("kp", [P, PARTS, T], BF16)
                vtok = s1("vtok", [P, T // P, D])
                retention_project(nc, zT, w, qp, kp, vtok)
                retention(nc, xT, w, qp, kp, vtok, w["causal"])
        if 2 in PHASES:
            layer_norm(nc, "n2", xT, zT, ones_mean, eps)
            with ExitStack() as c2:
                w = load_weights(nc, c2, "w2", {
                    "wq": (a["x_wq"], [P, D]), "wk": (a["x_wk"], [P, D]), "wv": (a["x_wv"], [P, D]),
                    "wo": (a["x_wo"], [P, HG, D])})
                qp = c2.enter_context(nc.sbuf_tensor("x_qp", [P, PARTS, T], BF16))
                cross_queries(nc, zT, w["wq"], qp)
                cross_attention(nc, xT, w, qp, a["context"])
        if 3 in PHASES:
            layer_norm(nc, "n3", xT, zT, ones_mean, eps)
            for l in range(DEPTH):
                with ExitStack() as c3:
                    w = load_weights(nc, c3, f"w3{l}", {
                        "wqkv": (a["f_wqkv"][l], [P, 3 * INNER]), "wo": (a["f_wo"][l], [P, FH // 2, D]),
                        "cosine": (a["cosine"], [P, 2, 2, FD]), "sine": (a["sine"], [P, 2, 2, FD]),
                        "scales": (a["f_scales"][l], [P, 2, FD]), "scales_turned": (a["f_scales_turned"][l], [P, 2, FD]),
                        "window": (a["window"], [P, 2, S]), "identity": (a["identity"], [P, P]),
                        "ln_g": (a["f_ln_g"][l], [P, 1]), "ln_b": (a["f_ln_b"][l], [P, 1]),
                        "w1": (a["f_w1"][l], [P, 2 * HC * P]), "b1": (a["f_b1"][l], [P, 2 * HC]),
                        "w2": (a["f_w2"][l], [P, HC, D]), "b2": (a["f_b2"][l], [P, 1])})
                    local_attention(nc, f"l{l}", zT, w)
                    hs = c3.enter_context(nc.sbuf_tensor(f"hs{l}", [P, T], F32))
                    shift_tokens(nc, f"t{l}", zT, hs)
                    layer_norm(nc, f"m{l}", hs, hs, ones_mean, eps)
                    gated_unit(nc, f"g{l}", zT, hs, w)
            with ExitStack() as c4:
                done = c4.enter_context(nc.semaphore("sum_done"))
                block = c4.enter_context(nc.Block())

                @block.vector
                def _(dve):
                    dve.tensor_tensor(xT[:, :], xT[:, :], zT[:, :], ALU.add).then_inc(done, 1)
                    dve.wait_ge(done, 1)
        with nc.Block() as block:
            @block.sync
            def _(sp):
                sp.dma_start(out, xT[:, :]).then_inc(stored, 16)
                sp.wait_ge(stored, 16)


def load_weights(nc, ctx, tag, table):
    tiles = {k: ctx.enter_context(nc.sbuf_tensor(f"{tag}_{k}", shape, F32)) for k, (_, shape) in table.items()}
    landed = ctx.enter_context(nc.semaphore(f"{tag}_landed"))
    with nc.Block() as block:
        @block.sync
        def _(sp):
            for k, (dram, shape) in table.items():
                full = tuple(slice(None) for _ in shape)
                sp.dma_start(tiles[k][full], dram).then_inc(landed, 16)
            sp.wait_ge(landed, 16 * len(table))
    return tiles


def layouts(x, ctx_1024, L0_attn_Wqk, L0_attn_bqk, L0_attn_Wv, L0_attn_bv, L0_attn_Wn, L0_attn_bn, L0_attn_Wo,
            L0_attn_bo, L0_xattn_Wq, L0_xattn_Wk, L0_xattn_Wv, L0_xattn_Wo, L0_ffn_wqkv, L0_ffn_q_scale,
            L0_ffn_k_scale, L0_ffn_wo, L0_ffn_ln_g, L0_ffn_ln_b, L0_ffn_w1, L0_ffn_b1, L0_ffn_w2, L0_ffn_b2):
    import numpy as np

    f = lambda v: np.ascontiguousarray(np.asarray(v), dtype=np.float32)
    col = lambda v: f(v).reshape(-1, 1)
    rep = lambda v: f(np.broadcast_to(np.asarray(v), (P, np.asarray(v).shape[-1])))
    s = np.arange(P)[:, None]
    t = np.arange(S)[None, :]
    halves = np.array([(e * 8 + h) * HD + d for e in range(2) for d in range(HD) for h in range(8)])
    context = np.zeros((B, D, CTXP), np.float32)
    context[:, :, 0:CTX] = np.asarray(ctx_1024).transpose(0, 2, 1)
    dmaj = np.array([h * HD + d for d in range(HD) for h in range(H)])
    hmaj = np.array([h for d in range(HD) for h in range(H)])
    wqk, bqk = np.asarray(L0_attn_Wqk), np.asarray(L0_attn_bqk)

    def spread(wo):
        o = np.zeros((HL, 32, HG, D), np.float32)
        o[:, 0:HD] = np.asarray(wo).reshape(HG, HL, HD, D).transpose(1, 2, 0, 3)
        return o.reshape(P, HG, D)

    w1 = np.zeros((DEPTH, D, 2, HC * P), np.float32)
    w1[..., 0:HID] = np.asarray(L0_ffn_w1).reshape(DEPTH, D, 2, HID)
    b1 = np.zeros((DEPTH, 2, HC * P), np.float32)
    b1[..., 0:HID] = np.asarray(L0_ffn_b1).reshape(DEPTH, 2, HID)
    w2 = np.zeros((DEPTH, HC * P, D), np.float32)
    w2[:, 0:HID] = np.asarray(L0_ffn_w2)
    qk_scales = np.stack([np.asarray(L0_ffn_q_scale), np.asarray(L0_ffn_k_scale)], 1)
    both = lambda g: f(np.broadcast_to(g(qk_scales)[:, None], (DEPTH, P, 2, FD)))
    half = np.arange(0, FD, 2, dtype=np.float32)
    place = np.arange(S, dtype=np.float32)
    freq = (place[:, None] * (np.float32(1.0) / np.float32(10000.0) ** (half / np.float32(FD)))[None, :]).astype(np.float32)
    power = (place - S // 2) / np.float32(WINDOW // 2)
    xpos = ((half + 0.4 * FD) / (1.4 * FD))[None, :].astype(np.float64) ** power[:, None]
    cos, sin = np.cos(freq.astype(np.float64)), np.sin(freq.astype(np.float64))
    by_scale = lambda v: np.stack([v * xpos * 8.0, v / xpos], 1)
    cosine = by_scale(cos)[:, :, None, :].repeat(2, 2)
    sine = np.stack([-by_scale(sin), by_scale(sin)], 2)
    tiles = lambda v: f(v.reshape(2, P, 2, FD).transpose(1, 0, 2, 3))
    cosine, sine = tiles(cosine), tiles(sine)
    window = np.full((P, 2, S), NEG, np.float32)
    for blk in range(2):
        i = blk * P + s
        window[:, blk][(t <= i) & (t >= i - WINDOW)] = 0.0
    return {
        "x": f(np.asarray(x).reshape(T, D).T),
        "r_wq": f(wqk[:, 0:D][:, dmaj]), "r_wk": f(wqk[:, D:][:, dmaj]), "r_wn": f(np.asarray(L0_attn_Wn)[:, hmaj]),
        "r_wv": f(L0_attn_Wv), "r_bq": col(bqk[0:D][dmaj]), "r_bk": col(bqk[D:][dmaj]),
        "r_bn": col(np.asarray(L0_attn_bn)[hmaj]), "r_bv": rep(L0_attn_bv), "r_wo": spread(L0_attn_Wo),
        "r_bo": col(L0_attn_bo),
        "x_wq": f(np.asarray(L0_xattn_Wq).T[:, halves]), "x_wk": f(np.asarray(L0_xattn_Wk).T[:, halves]),
        "x_wv": f(np.asarray(L0_xattn_Wv).T), "x_wo": spread(np.asarray(L0_xattn_Wo).T),
        "context": context,
        "f_wqkv": f(L0_ffn_wqkv), "f_wo": f(np.asarray(L0_ffn_wo).reshape(DEPTH, FH // 2, P, D).transpose(0, 2, 1, 3)),
        "f_scales": both(lambda v: v), "f_scales_turned": both(lambda v: np.roll(v, FD // 2, axis=-1)),
        "f_ln_g": f(L0_ffn_ln_g)[:, :, None], "f_ln_b": f(L0_ffn_ln_b)[:, :, None],
        "f_w1": w1.reshape(DEPTH, D, 2 * HC * P), "f_b1": f(b1.reshape(DEPTH, 2 * HC, P).transpose(0, 2, 1)),
        "f_w2": f(w2.reshape(DEPTH, HC, P, D).transpose(0, 2, 1, 3)), "f_b2": f(L0_ffn_b2)[:, :, None],
        "cosine": cosine, "sine": sine, "window": window, "identity": np.eye(P, dtype=np.float32),
        "causal": (s <= t).astype(np.float32),
    }


def kernel(**inputs):
    import numpy as _np
    import concourse.bacc as _bacc
    from concourse import mybir as _mybir
    from concourse.bass_utils import run_bass_kernel_spmd as _run

    nc = _bacc.Bacc("TRN2", target_bir_lowering=False, num_devices=1)
    arrays, args = {}, {}
    for name, arr in layouts(**inputs).items():
        arrays[f"in_{name}"] = arr
        args[name] = nc.dram_tensor(f"in_{name}", arr.shape, _mybir.dt.from_np(arr.dtype), kind="ExternalInput").ap()
    out = nc.dram_tensor("out_x", (P, T), F32, kind="ExternalOutput").ap()
    build(nc, args, out)
    r = _run(nc, [arrays], core_ids=[0])
    return _np.ascontiguousarray(r.results[0]["out_x"].T).reshape(B, S, D)
```

```python
from contextlib import ExitStack

import concourse.bass as bass
from concourse import mybir
from concourse.bass import ds

F32 = mybir.dt.float32
BF16 = mybir.dt.bfloat16
I32 = mybir.dt.int32
ALU = mybir.AluOpType
ACT = mybir.ActivationFunctionType
AX = mybir.AxisListType

P = 128
B, S, D = 16, 256, 128
T = B * S
H, HD = 16, 8
HG, HL = 4, 4
PARTS = 3
COMBOS = PARTS * PARTS
ROWS = COMBOS * HD
CTX = 1601
ST = (CTX + P - 1) // P
CTXP = ST * P
KCH = CTXP // HG
CH = 512
NCH = T // CH
FH, FD = 8, 64
INNER = FH * FD
WINDOW = 64
DEPTH = 2
HID = 341
HC = (HID + P - 1) // P
NEG = -3.0e38


class Own:

    def __init__(self, eng, sem, per):
        self.eng, self.sem, self.per, self.base, self.n = eng, sem, per, 0, 0

    def turn(self, i):
        assert self.n in (0, self.per), (self.n, self.per)
        self.base, self.n = i * self.per, 0

    def step(self, ins):
        ins.then_inc(self.sem, 1)
        self.n += 1
        return self.n

    def wait(self, n=None):
        self.eng.wait_ge(self.sem, self.base + (self.n if n is None else n))


def layer_norm(nc, tag, norms, src, dst, loads=(), zeros=()):
    U = 4
    ones_mean, eps, base = norms["ones_mean"], norms["eps"], norms["runs"] * NCH
    norms["runs"] += 1
    mean_ready, centered, square_ready, var_ready, log_ready, rstd_ready, rsquare_ready, newton, normed = norms["sems"]
    with ExitStack() as ctx:
        sb = lambda name, shape, dt: ctx.enter_context(nc.sbuf_tensor(f"{tag}_{name}", shape, dt))
        ps = lambda name, shape: ctx.enter_context(nc.psum_tensor(f"{tag}_{name}", shape, F32))
        sem = lambda name: ctx.enter_context(nc.semaphore(f"{tag}_{name}"))
        square = [sb(f"square{u}", [P, CH], F32) for u in range(U)]
        rstd = [sb(f"rstd{u}", [P, CH], F32) for u in range(U)]
        mean = [ps(f"mean{u}", [P, CH]) for u in range(U)]
        var = [ps(f"var{u}", [P, CH]) for u in range(U)]
        landed = sem("landed") if loads else None
        cleared = sem("cleared") if zeros else None
        block = ctx.enter_context(nc.Block())

        if loads:
            @block.sync
            def _(sp):
                for tile, dram in loads:
                    sp.dma_start(tile, dram).then_inc(landed, 16)
                sp.wait_ge(landed, 16 * len(loads))

        if zeros:
            @block.gpsimd
            def _(pool):
                for n, ap in enumerate(zeros):
                    pool.memset(ap, 0.0).then_inc(cleared, 1)
                    pool.wait_ge(cleared, n + 1)

        @block.tensor
        def _(pe):
            with pe.Fori(0, NCH // U) as i:
                for u in range(U):
                    pe.matmul(mean[u][:, :], ones_mean[:, :], src[:, ds((U * i + u) * CH, CH)],
                              start=True, stop=True).then_inc(mean_ready, 1)
                for u in range(U):
                    pe.wait_ge(square_ready, base + U * i + u + 1)
                    pe.matmul(var[u][:, :], ones_mean[:, :], square[u][:, :],
                              start=True, stop=True).then_inc(var_ready, 1)

        @block.vector
        def _(dve):
            with dve.Fori(0, NCH // U) as i:
                for u in range(U):
                    at = ds((U * i + u) * CH, CH)
                    dve.wait_ge(mean_ready, base + U * i + u + 1)
                    dve.tensor_tensor(dst[:, at], src[:, at], mean[u][:, :], ALU.subtract).then_inc(centered, 1)
                for u in range(U):
                    dve.wait_ge(rsquare_ready, base + U * i + u + 1)
                    dve.scalar_tensor_tensor(square[u][:, :], var[u][:, :], eps[:, 0:1], square[u][:, :],
                                             ALU.add, ALU.mult).then_inc(newton, 1)
                for u in range(U):
                    dve.wait_ge(newton, 2 * (base + U * i) + u + 1)
                    dve.scalar_tensor_tensor(rstd[u][:, :], square[u][:, :], 3.0, rstd[u][:, :],
                                             ALU.subtract, ALU.mult).then_inc(newton, 1)
                for u in range(U):
                    at = ds((U * i + u) * CH, CH)
                    dve.wait_ge(newton, 2 * (base + U * i) + U + u + 1)
                    dve.scalar_tensor_tensor(dst[:, at], rstd[u][:, :], -0.5, dst[:, at],
                                             ALU.mult, ALU.mult).then_inc(normed, 1)

        @block.scalar
        def _(act):
            with act.Fori(0, NCH // U) as i:
                for u in range(U):
                    act.wait_ge(centered, base + U * i + u + 1)
                    act.activation(square[u][:, :], dst[:, ds((U * i + u) * CH, CH)],
                                   ACT.Square).then_inc(square_ready, 1)
                for u in range(U):
                    act.wait_ge(var_ready, base + U * i + u + 1)
                    act.activation(rstd[u][:, :], var[u][:, :], ACT.Ln, bias=eps[:, 0:1]).then_inc(log_ready, 1)
                for u in range(U):
                    act.wait_ge(log_ready, base + U * i + u + 1)
                    act.activation(rstd[u][:, :], rstd[u][:, :], ACT.Exp, scale=-0.5).then_inc(rstd_ready, 1)
                for u in range(U):
                    act.wait_ge(rstd_ready, base + U * i + u + 1)
                    act.activation(square[u][:, :], rstd[u][:, :], ACT.Square).then_inc(rsquare_ready, 1)


def retention_project(nc, zT, w, qp, kp, vtok):
    with ExitStack() as ctx:
        sb = lambda name, shape, dt=F32: ctx.enter_context(nc.sbuf_tensor(f"r_{name}", shape, dt))
        ps = lambda name, shape: ctx.enter_context(nc.psum_tensor(f"r_{name}", shape, F32))
        sem = lambda name: ctx.enter_context(nc.semaphore(f"r_{name}"))
        hc = [sb(f"hc{u}", [P, CH]) for u in range(2)]
        inv_n = [sb(f"inv_n{u}", [P, CH]) for u in range(2)]
        q32 = [sb(f"q32{u}", [P, CH]) for u in range(2)]
        k32 = [sb(f"k32{u}", [P, CH]) for u in range(2)]
        psq = [ps(f"psq{u}", [P, CH]) for u in range(2)]
        psk = [ps(f"psk{u}", [P, CH]) for u in range(2)]
        psn = [ps(f"psn{u}", [P, CH]) for u in range(2)]
        psv = [ps(f"psv{u}", [P, CH]) for u in range(2)]
        h_ready, projected, neg_bn = sem("h_ready"), sem("projected"), sem("neg_bn")
        n_exp, k_ready, hi_ready, mid_ready = sem("n_exp"), sem("k_ready"), sem("hi_ready"), sem("mid_ready")
        q_ready, v_ready, rest, last = sem("q_ready"), sem("v_ready"), sem("rest"), sem("last")
        nbn = sb("nbn", [P, 1])
        block = ctx.enter_context(nc.Block())

        @block.tensor
        def _(pe):
            with pe.Fori(0, NCH // 2) as i:
                for u in range(2):
                    n = 2 * i + u
                    pe.wait_ge(h_ready, n + 1)
                    pe.matmul(psn[u][:, :], w["wn"][:, :], hc[u][:, :], start=True, stop=True)
                    pe.matmul(psq[u][:, :], w["wq"][:, :], hc[u][:, :], start=True, stop=True)
                    pe.matmul(psk[u][:, :], w["wk"][:, :], hc[u][:, :], start=True, stop=True)
                    for t in range(CH // P):
                        ins = pe.matmul(psv[u][:, t * P:(t + 1) * P], hc[u][:, t * P:(t + 1) * P],
                                        w["wv"][:, :], start=True, stop=True)
                    ins.then_inc(projected, 1)

        @block.gpsimd
        def _(pool):
            for u in range(2):
                pool.tensor_copy(hc[u][:, :], zT[:, u * CH:(u + 1) * CH]).then_inc(h_ready, 1)
            with pool.Fori(0, NCH // 2 - 1) as i:
                for u in range(2):
                    n = 2 * i + u
                    pool.wait_ge(last, 2 * n + 2)
                    pool.tensor_copy(hc[u][:, :], zT[:, ds((n + 2) * CH, CH)]).then_inc(h_ready, 1)

        @block.scalar
        def _(act):
            act.mul(nbn[:, :], w["bn"][:, :], -1.0).then_inc(neg_bn, 1)
            act.wait_ge(neg_bn, 1)
            with act.Fori(0, NCH // 2) as i:
                for u in range(2):
                    n = 2 * i + u
                    at = ds(n * CH, CH)
                    act.wait_ge(projected, n + 1)
                    act.activation(inv_n[u][:, :], psn[u][:, :], ACT.Exp, bias=nbn[:, 0:1], scale=-1.0).then_inc(n_exp, 1)
                    act.activation(k32[u][:, :], psk[u][:, :], ACT.Identity, bias=w["bk"][:, 0:1]).then_inc(k_ready, 1)
                    act.wait_ge(k_ready, n + 1)
                    act.activation(kp[:, 0, at], k32[u][:, :], ACT.Copy).then_inc(hi_ready, 1)
                    act.wait_ge(q_ready, n + 1)
                    act.activation(qp[:, 0, at], q32[u][:, :], ACT.Copy).then_inc(hi_ready, 1)
                    act.wait_ge(rest, 2 * n + 1)
                    act.activation(kp[:, 1, at], k32[u][:, :], ACT.Copy).then_inc(mid_ready, 1)
                    act.wait_ge(rest, 2 * n + 2)
                    act.activation(qp[:, 1, at], q32[u][:, :], ACT.Copy).then_inc(mid_ready, 1)

        @block.vector
        def _(dve):
            with dve.Fori(0, NCH // 2) as i:
                for u in range(2):
                    n = 2 * i + u
                    at = ds(n * CH, CH)
                    dve.wait_ge(n_exp, n + 1)
                    dve.scalar_tensor_tensor(q32[u][:, :], psq[u][:, :], w["bq"][:, 0:1], inv_n[u][:, :],
                                             ALU.add, ALU.mult).then_inc(q_ready, 1)
                    dve.tensor_tensor(vtok[:, ds(n * (CH // P), CH // P), :],
                                      psv[u][:, :].rearrange("p (t n) -> p t n", n=P),
                                      w["bv"][:, :].unsqueeze(1).broadcast_to([P, CH // P, P]),
                                      ALU.add).then_inc(v_ready, 1)
                    for m, (x, parts) in enumerate(((k32[u], kp), (q32[u], qp))):
                        dve.wait_ge(hi_ready, 2 * n + m + 1)
                        dve.tensor_tensor(x[:, :], x[:, :], parts[:, 0, at], ALU.subtract).then_inc(rest, 1)
                    for m, (x, parts) in enumerate(((k32[u], kp), (q32[u], qp))):
                        dve.wait_ge(mid_ready, 2 * n + m + 1)
                        dve.tensor_tensor(parts[:, 2, at], x[:, :], parts[:, 1, at], ALU.subtract).then_inc(last, 1)


def retention(nc, xT, w, qp, kp, vtok, causal, q9, k9):
    with ExitStack() as ctx:
        sb = lambda name, shape, dt=F32: ctx.enter_context(nc.sbuf_tensor(f"a_{name}", shape, dt))
        ps = lambda name, shape: ctx.enter_context(nc.psum_tensor(f"a_{name}", shape, F32))
        sem = lambda name: ctx.enter_context(nc.semaphore(f"a_{name}"))
        vb = [sb(f"vb{u}", [P, 2, D]) for u in range(2)]
        m0 = [sb(f"m0{r}", [P, HL, S]) for r in range(2)]
        m1 = [sb(f"m1{r}", [P, HL, P]) for r in range(2)]
        oT = sb("oT", [P, HG, S])
        ps0 = [ps(f"ps0{r}", [P, HL, S]) for r in range(2)]
        ps1 = ps("ps1", [P, HL, P])
        pso = [ps(f"pso{r}", [P, 2, S]) for r in range(2)]
        psy = ps("psy", [P, CH])
        zeroed, packs = sem("zeroed"), [sem(f"packs{u}") for u in range(2)]
        v_ready = sem("v_ready")
        score0, score1, masked0, masked1 = sem("score0"), sem("score1"), sem("masked0"), sem("masked1")
        mixed, o_ready, out_ready, added = sem("mixed"), sem("o_ready"), sem("out_ready"), sem("added")
        block = ctx.enter_context(nc.Block())
        NDMA = 2 * COMBOS

        @block.sync
        def _(sp):
            def stack(m, w):
                for a in range(PARTS):
                    for b in range(PARTS):
                        r = (a * PARTS + b) * HD
                        at = ds(m * 2 * S, 2 * S)
                        sp.dma_start(q9[w][r:r + HD, :, :], qp[:, a, at]).then_inc(packs[w], 16)
                        sp.dma_start(k9[w][r:r + HD, :, :], kp[:, b, at]).then_inc(packs[w], 16)

            stack(0, 0)
            stack(1, 1)
            with sp.Fori(0, B // 4 - 1) as i:
                for w in range(2):
                    sp.wait_ge(score1, (2 * i + w + 1) * 2 * HG)
                    stack(2 * i + w + 2, w)

        @block.gpsimd
        def _(pool):
            for u in range(2):
                pool.tensor_copy(vb[u][:, :, :], vtok[:, 2 * u:2 * u + 2, :]).then_inc(v_ready, 1)
            with pool.Fori(0, B // 2 - 1) as i:
                for u in range(2):
                    n = 2 * i + u
                    pool.wait_ge(mixed, (n + 1) * HG)
                    pool.tensor_copy(vb[u][:, :, :], vtok[:, ds(2 * (n + 2), 2), :]).then_inc(v_ready, 1)

        @block.tensor
        def _(pe):
            pe.wait_ge(zeroed, 1)
            with pe.Fori(0, B // 4) as i:
                for w4 in range(4):
                    n, wp, u = 4 * i + w4, w4 // 2, w4 % 2
                    q, k = q9[wp][:, :, u * S:(u + 1) * S], k9[wp][:, :, u * S:(u + 1) * S]

                    def scores(g):
                        c = n * HG + g
                        pe.wait_ge(masked0, c + 1)
                        for h in range(HL):
                            ins = pe.matmul(ps0[g % 2][:, h, :], k[:, HL * g + h, 0:P], q[:, HL * g + h, :],
                                            start=True, stop=True)
                        ins.then_inc(score0, 1)
                        pe.wait_ge(masked1, c + 1)
                        for h in range(HL):
                            ins = pe.matmul(ps1[:, h, :], k[:, HL * g + h, P:S], q[:, HL * g + h, P:S],
                                            start=True, stop=True)
                        ins.then_inc(score1, 1)

                    def mix(g):
                        c = n * HG + g
                        if g == 0:
                            pe.wait_ge(v_ready, n + 1)
                        pe.wait_ge(masked0, c + 3)
                        for h in range(HL):
                            lo = (HL * g + h) * HD
                            pe.matmul(pso[g // 2][32 * h:32 * h + HD, g % 2, :], vb[u][:, 0, lo:lo + HD],
                                      m0[g % 2][:, h, :], start=True, stop=False)
                        pe.wait_ge(masked1, c + 2)
                        for h in range(HL):
                            lo = (HL * g + h) * HD
                            ins = pe.matmul(pso[g // 2][32 * h:32 * h + HD, g % 2, P:S], vb[u][:, 1, lo:lo + HD],
                                            m1[g % 2][:, h, :], start=False, stop=True)
                        ins.then_inc(mixed, 1)

                    if u == 0:
                        pe.wait_ge(packs[wp], (i + 1) * NDMA * 16)
                    scores(0)
                    for g in range(1, HG):
                        scores(g)
                        mix(g - 1)
                    mix(HG - 1)
                    for g in range(HG):
                        pe.wait_ge(o_ready, 2 * n + g // 2 + 1)
                        ins = pe.matmul(psy[:, 0:S], w["wo"][:, g, :], oT[:, g, :], start=(g == 0), stop=(g == HG - 1))
                    ins.then_inc(out_ready, 1)

        @block.vector
        def _(dve):
            for r in range(2):
                dve.memset(pso[r][:, :, :], 0.0)
            dve.memset(psy[:, :], 0.0).then_inc(zeroed, 1)
            dve.memset(m0[0][:, 0, 0:1], 0.0).then_inc(masked0, 2)
            dve.memset(m1[0][:, 0, 0:1], 0.0).then_inc(masked1, 1)
            with dve.Fori(0, B // 2) as i:
                for u in range(2):
                    n = 2 * i + u
                    for g in range(HG):
                        c = n * HG + g
                        dve.wait_ge(score0, c + 1)
                        dve.tensor_tensor(m0[g % 2][:, :, :], ps0[g % 2][:, :, :],
                                          causal[:, :].unsqueeze(1).broadcast_to([P, HL, S]),
                                          ALU.mult).then_inc(masked0, 1)
                        dve.wait_ge(score1, c + 1)
                        dve.tensor_tensor(m1[g % 2][:, :, :], ps1[:, :, :],
                                          causal[:, 0:P].unsqueeze(1).broadcast_to([P, HL, P]),
                                          ALU.mult).then_inc(masked1, 1)
                    dve.wait_ge(out_ready, n + 1)
                    at = ds(n * S, S)
                    dve.scalar_tensor_tensor(xT[:, at], psy[:, 0:S], w["bo"][:, 0:1], xT[:, at],
                                             ALU.add, ALU.add).then_inc(added, 1)

        @block.scalar
        def _(act):
            act.wait_ge(zeroed, 1)
            with act.Fori(0, B // 2) as i:
                for u in range(2):
                    n = 2 * i + u
                    for r in range(2):
                        act.wait_ge(mixed, n * HG + 2 * r + 2)
                        act.activation(oT[:, 2 * r:2 * r + 2, :], pso[r][:, :, :], ACT.Copy).then_inc(o_ready, 1)


def cross_queries(nc, zT, wq, qp):
    with ExitStack() as ctx:
        sb = lambda name, shape, dt=F32: ctx.enter_context(nc.sbuf_tensor(f"xq_{name}", shape, dt))
        ps = lambda name, shape: ctx.enter_context(nc.psum_tensor(f"xq_{name}", shape, F32))
        sem = lambda name: ctx.enter_context(nc.semaphore(f"xq_{name}"))
        rest = [sb(f"rest{u}", [P, CH]) for u in range(2)]
        psq = [ps(f"psq{u}", [P, CH]) for u in range(2)]
        projected, hi_ready, rest_ready = sem("projected"), sem("hi_ready"), sem("rest_ready")
        mid_ready, lo_ready = sem("mid_ready"), sem("lo_ready")
        block = ctx.enter_context(nc.Block())

        @block.tensor
        def _(pe):
            for n in range(2):
                pe.matmul(psq[n][:, :], wq[:, :], zT[:, n * CH:(n + 1) * CH], start=True, stop=True).then_inc(projected, 1)
            with pe.Fori(0, NCH // 2 - 1) as i:
                for u in range(2):
                    n = 2 * i + u
                    pe.wait_ge(rest_ready, n + 1)
                    pe.matmul(psq[u][:, :], wq[:, :], zT[:, ds((n + 2) * CH, CH)],
                              start=True, stop=True).then_inc(projected, 1)

        @block.scalar
        def _(act):
            with act.Fori(0, NCH // 2) as i:
                for u in range(2):
                    n = 2 * i + u
                    act.wait_ge(projected, n + 1)
                    act.activation(qp[:, 0, ds(n * CH, CH)], psq[u][:, :], ACT.Copy).then_inc(hi_ready, 1)
                    act.wait_ge(rest_ready, n + 1)
                    act.activation(qp[:, 1, ds(n * CH, CH)], rest[u][:, :], ACT.Copy).then_inc(mid_ready, 1)

        @block.vector
        def _(dve):
            with dve.Fori(0, NCH // 2) as i:
                for u in range(2):
                    n = 2 * i + u
                    at = ds(n * CH, CH)
                    dve.wait_ge(hi_ready, n + 1)
                    dve.tensor_tensor(rest[u][:, :], psq[u][:, :], qp[:, 0, at], ALU.subtract).then_inc(rest_ready, 1)
                    dve.wait_ge(mid_ready, n + 1)
                    dve.tensor_tensor(qp[:, 2, at], rest[u][:, :], qp[:, 1, at], ALU.subtract).then_inc(lo_ready, 1)


def cross_attention(nc, xT, w, qp, context):
    UNITS = HG * ST
    HALF = H // 2
    NSTACK = 2 * COMBOS * 16
    VCH = [(0, 4), (4, 7), (7, 10), (10, 13)]
    K_AT = {9: 0, 16: 1, 22: 2, 29: 3}
    V_AT = {32: 0, 35: 1, 42: 2, 45: 3}
    WO_AT = 3
    NP = 4
    with ExitStack() as ctx:
        sb = lambda name, shape, dt=F32: ctx.enter_context(nc.sbuf_tensor(f"x_{name}", shape, dt))
        ps = lambda name, shape: ctx.enter_context(nc.psum_tensor(f"x_{name}", shape, F32))
        sem = lambda name: ctx.enter_context(nc.semaphore(f"x_{name}"))
        cT = sb("cT", [P, CTXP])
        kx = [sb(f"kx{e}", [P, HALF, CTXP], BF16) for e in range(2)]
        qx = [sb(f"qx{e}", [P, HALF, S], BF16) for e in range(2)]
        kp = sb("kp", [P, PARTS, CTXP], BF16)
        krest = sb("krest", [P, KCH])
        vnext = sb("vnext", [P, ST, D])
        v = sb("v", [P, ST, D])
        probs = [sb(f"probs{r}", [P, HL, S]) for r in range(NP)]
        oT = sb("oT", [P, HG, S])
        pss = [ps(f"pss{r}", [P, HL, S]) for r in range(2)]
        acc = [ps(f"acc{r}", [P, CH]) for r in range(2)]
        psk = ps("psk", [P, CH])
        psv = ps("psv", [P, CH])
        zeroed, c_landed, stacked = sem("zeroed"), sem("c_landed"), [sem(f"stacked{e}") for e in range(2)]
        k_projected, k_cut, v_projected, v_copied, v_set = (
            sem("k_projected"), sem("k_cut"), sem("v_projected"), sem("v_copied"), sem("v_set"))
        scored, weighed, mixed, o_ready = sem("scored"), sem("weighed"), sem("mixed"), sem("o_ready")
        out_ready, added = sem("out_ready"), sem("added")
        block = ctx.enter_context(nc.Block())

        def turns(eng, body):
            body(0)
            with eng.Fori(1, B - 1) as i:
                body(i)
            body(B - 1, last=True)

        @block.sync
        def _(sp):
            def load(n):
                sp.dma_start(cT[:, :], context[ds(n, 1), :, :].rearrange("a p s -> (a p) s")).then_inc(c_landed, 16)

            def stack(n, e):
                for a in range(PARTS):
                    for b in range(PARTS):
                        r = (a * PARTS + b) * HD
                        sp.dma_start(qx[e][r:r + HD, :, :],
                                     qp[64 * e:64 * e + 64, a, ds(n * S, S)]).then_inc(stacked[e], 16)
                        sp.dma_start(kx[e][r:r + HD, :, :], kp[64 * e:64 * e + 64, b, :]).then_inc(stacked[e], 16)

            def turn(n, last=False):
                if not (isinstance(n, int) and n == 0):
                    sp.wait_ge(scored, n * UNITS)
                stack(n, 1)
                if not last:
                    sp.wait_ge(k_cut, (n + 2) * 4 * HG)
                    stack(n + 1, 0)
                    if not (isinstance(n, int) and n == B - 2):
                        sp.wait_ge(v_projected, (n + 2) * HG)
                        load(n + 2)

            load(0)
            sp.wait_ge(zeroed, 5)
            sp.wait_ge(k_cut, 4 * HG)
            stack(0, 0)
            sp.wait_ge(v_projected, HG)
            load(1)
            turn(0)
            with sp.Fori(1, B - 2) as i:
                turn(i)
            turn(B - 2)
            turn(B - 1, last=True)

        @block.gpsimd
        def _(pool):
            for e in range(2):
                pool.memset(qx[e][64:P, :, :], 0.0).then_inc(zeroed, 1)
                pool.memset(kx[e][64:P, :, :], 0.0).then_inc(zeroed, 1)

        @block.tensor
        def _(pe):
            def project_keys(m, c):
                pe.wait_ge(c_landed, (m + 1) * 16)
                if not (isinstance(m, int) and m == 0 and c == 0):
                    pe.wait_ge(k_cut, (m * HG + c) * 4 - 2)
                pe.matmul(psk[:, 0:KCH], w["wk"][:, :], cT[:, c * KCH:(c + 1) * KCH],
                          start=True, stop=True).then_inc(k_projected, 1)

            def project_values(m, c):
                if not (isinstance(m, int) and m == 0 and c == 0):
                    pe.wait_ge(v_copied, m * HG + c)
                if c == 0 and not (isinstance(m, int) and m < 2):
                    pe.wait_ge(added, m - 1)
                for j in range(*VCH[c]):
                    ins = pe.matmul(psv[:, (j - VCH[c][0]) * P:(j - VCH[c][0] + 1) * P], cT[:, j * P:(j + 1) * P],
                                    w["wv"][:, :], start=True, stop=True)
                ins.then_inc(v_projected, 1)

            def score(n, u):
                g, j = u // ST, u % ST
                if u % (UNITS // 2) == 0:
                    pe.wait_ge(stacked[g // 2], (n + 1) * NSTACK)
                if not (isinstance(n, int) and n == 0 and u < 2):
                    pe.wait_ge(weighed, n * UNITS + u - 1)
                for h in range(HL):
                    hh = (g % 2) * HL + h
                    ins = pe.matmul(pss[u % 2][:, h, :], kx[g // 2][:, hh, j * P:(j + 1) * P], qx[g // 2][:, hh, :],
                                    start=True, stop=True)
                ins.then_inc(scored, 1)

            def mix(n, u):
                g, j = u // ST, u % ST
                if j == 0:
                    pe.wait_ge(v_set, n * HG + g + 1)
                    if not (isinstance(n, int) and n == 0 and g < 2):
                        pe.wait_ge(o_ready, n * HG + g - 1)
                pe.wait_ge(weighed, n * UNITS + u + 1)
                for h in range(HL):
                    lo = (HL * g + h) * HD
                    ins = pe.matmul(acc[g % 2][32 * h:32 * h + HD, 0:S], v[:, j, lo:lo + HD],
                                    probs[u % NP][:, h, :], start=(j == 0), stop=(j == ST - 1))
                ins.then_inc(mixed, 1)

            def project_out(n):
                pe.wait_ge(o_ready, (n + 1) * HG)
                for g in range(HG):
                    ins = pe.matmul(psv[:, 0:S], w["wo"][:, g, :], oT[:, g, :], start=(g == 0), stop=(g == HG - 1))
                ins.then_inc(out_ready, 1)

            def turn(n, last=False):
                first = isinstance(n, int) and n == 0
                for u in range(UNITS):
                    if u + 2 < UNITS:
                        score(n, u + 2)
                    elif not last:
                        score(n + 1, u + 2 - UNITS)
                    mix(n, u)
                    if u == WO_AT and not first:
                        project_out(n - 1)
                    if u in K_AT and not last:
                        project_keys(n + 1, K_AT[u])
                    if u in V_AT and not last:
                        project_values(n + 1, V_AT[u])

            pe.wait_ge(zeroed, 5)
            for c in range(HG):
                project_keys(0, c)
            for c in range(HG):
                project_values(0, c)
            score(0, 0)
            score(0, 1)
            turns(pe, turn)
            project_out(B - 1)

        @block.scalar
        def _(act):
            def turn(n, last=False):
                for u in range(UNITS):
                    act.wait_ge(scored, n * UNITS + u + 1)
                    if not (isinstance(n, int) and n == 0 and u < NP):
                        act.wait_ge(mixed, n * UNITS + u - NP + 1)
                    act.activation(probs[u % NP][:, :, :], pss[u % 2][:, :, :], ACT.Sigmoid,
                                   scale=HD ** -0.5).then_inc(weighed, 1)

            turns(act, turn)

        @block.vector
        def _(dve):
            def cut_keys(m, c):
                at = slice(c * KCH, (c + 1) * KCH)
                done = (m * HG + c) * 4
                dve.wait_ge(k_projected, m * HG + c + 1)
                dve.tensor_copy(kp[:, 0, at], psk[:, 0:KCH]).then_inc(k_cut, 1)
                dve.wait_ge(k_cut, done + 1)
                dve.tensor_tensor(krest[:, :], psk[:, 0:KCH], kp[:, 0, at], ALU.subtract).then_inc(k_cut, 1)
                dve.wait_ge(k_cut, done + 2)
                dve.tensor_copy(kp[:, 1, at], krest[:, :]).then_inc(k_cut, 1)
                dve.wait_ge(k_cut, done + 3)
                dve.tensor_tensor(kp[:, 2, at], krest[:, :], kp[:, 1, at], ALU.subtract).then_inc(k_cut, 1)

            def copy_values(m, c):
                a, b = VCH[c]
                dve.wait_ge(v_projected, m * HG + c + 1)
                dve.tensor_copy(vnext[:, a:b, :],
                                psv[:, 0:(b - a) * P].rearrange("p (t n) -> p t n", n=P)).then_inc(v_copied, 1)

            def set_values(n, g):
                dve.wait_ge(v_copied, (n + 1) * HG)
                if not (isinstance(n, int) and n == 0):
                    dve.wait_ge(mixed, (n - 1) * UNITS + (g + 1) * ST)
                lo = g * HL * HD
                dve.tensor_copy(v[:, :, lo:lo + HL * HD], vnext[:, :, lo:lo + HL * HD]).then_inc(v_set, 1)

            def take_out(n, g):
                dve.wait_ge(mixed, n * UNITS + (g + 1) * ST)
                dve.tensor_copy(oT[:, g, :], acc[g % 2][:, 0:S]).then_inc(o_ready, 1)

            def add(n):
                dve.wait_ge(out_ready, n + 1)
                at = ds(n * S, S)
                dve.tensor_tensor(xT[:, at], psv[:, 0:S], xT[:, at], ALU.add).then_inc(added, 1)

            def turn(n, last=False):
                first = isinstance(n, int) and n == 0
                if not first:
                    take_out(n - 1, 3)
                for g in range(1, HG):
                    set_values(n, g)
                if not first:
                    add(n - 1)
                if not last:
                    dve.wait_ge(stacked[1], (n + 1) * NSTACK)
                    cut_keys(n + 1, 0)
                take_out(n, 0)
                if not last:
                    cut_keys(n + 1, 1)
                    cut_keys(n + 1, 2)
                take_out(n, 1)
                if not last:
                    cut_keys(n + 1, 3)
                    copy_values(n + 1, 0)
                    copy_values(n + 1, 1)
                take_out(n, 2)
                if not last:
                    copy_values(n + 1, 2)
                    copy_values(n + 1, 3)
                    set_values(n + 1, 0)

            for r in range(2):
                dve.memset(acc[r][:, :], 0.0)
            dve.memset(oT[:, :, :], 0.0).then_inc(zeroed, 1)
            for c in range(HG):
                cut_keys(0, c)
            for c in range(HG):
                copy_values(0, c)
            set_values(0, 0)
            turns(dve, turn)
            take_out(B - 1, 3)
            add(B - 1)


def local_attention(nc, tag, zT, w):
    NSU = 6
    UNIT = [(0, (0, 1, 2, 3)), (0, (4, 5, 6, 7)), (1, (0, 1)), (1, (2, 3)), (1, (4, 5)), (1, (6, 7))]
    KEYS = [(0, P), (WINDOW, S)]
    NEWTON = 12
    QK = 2 * FH
    with ExitStack() as ctx:
        sb = lambda name, shape, dt=F32: ctx.enter_context(nc.sbuf_tensor(f"{tag}_{name}", shape, dt))
        ps = lambda name, shape: ctx.enter_context(nc.psum_tensor(f"{tag}_{name}", shape, F32))
        sem = lambda name: ctx.enter_context(nc.semaphore(f"{tag}_{name}"))
        hs = [sb(f"hs{u}", [P, S]) for u in range(2)]
        tabA, tabB = sb("tabA", [P, 2, 2, FD]), sb("tabB", [P, 2, 2, FD])
        square = sb("square", [P, QK, FD])
        direct = [[sb(f"direct{u}{t}", [P, QK, FD]) for t in range(2)] for u in range(2)]
        raw = [sb(f"raw{t}", [P, QK, FD]) for t in range(2)]
        turned_half = [sb(f"turned_half{t}", [P, QK, FD]) for t in range(2)]
        sumsq, inv_norm = sb("sumsq", [P, 2, QK]), sb("inv_norm", [P, 2, QK])
        tmp_a, tmp_b = sb("tmp_a", [P, 2, QK]), sb("tmp_b", [P, 2, QK])
        qz = [sb(f"qz{u}", [P, FH, S]) for u in range(2)]
        kT = [sb(f"kT{u}", [P, FH // 2, S]) for u in range(2)]
        vt = [sb(f"vt{u}", [P, 2, INNER]) for u in range(2)]
        sim = [sb(f"sim{r}", [P, CH]) for r in range(2)]
        prob = [sb(f"prob{s}", [P, CH]) for s in range(NSU)]
        probT = [sb(f"probT{r}", [P, CH]) for r in range(2)]
        top, neg_top = [sb(f"top{r}", [P, 4]) for r in range(2)], [sb(f"neg_top{r}", [P, 4]) for r in range(2)]
        total, inv_total = [sb(f"total{r}", [P, 4]) for r in range(2)], [sb(f"inv_total{r}", [P, 4]) for r in range(2)]
        oT = sb("oT", [P, FH // 2, S])
        beat = sb("beat", [P, 1])
        psqk = ps("psqk", [P, QK, FD])
        psvy = ps("psvy", [P, CH])
        pst = ps("pst", [P, CH])
        pss = [ps(f"pss{r}", [P, CH]) for r in range(2)]
        pso = ps("pso", [P, FH // 2, S])
        ready, shifted, qk_projected, squared = sem("ready"), sem("shifted"), sem("qk_projected"), sem("squared")
        v_projected, v_ready, summed, raw_ready = sem("v_projected"), sem("v_ready"), sem("summed"), sem("raw_ready")
        straight, halved = sem("straight"), sem("halved")
        joined, newton, scaled = sem("joined"), sem("newton"), [sem(f"scaled{t}") for t in range(2)]
        flipped, placed, scored, masked = sem("flipped"), sem("placed"), sem("scored"), sem("masked")
        negated, exped, inverted, normed = sem("negated"), sem("exped"), sem("inverted"), sem("normed")
        turned, copied, valued, o_ready = sem("turned"), sem("copied"), sem("valued"), sem("o_ready")
        out_ready, added = sem("out_ready"), sem("added")
        block = ctx.enter_context(nc.Block())

        def exists(n):
            return not isinstance(n, int) or 0 <= n < B

        def at_least(eng, sem, value):
            if not isinstance(value, int) or value > 0:
                eng.wait_ge(sem, value)

        def turns(eng, body):
            for n in range(-2, 2):
                body(n, n % 2)
            with eng.Fori(1, B // 2 - 1) as i:
                for u in range(2):
                    body(2 * i + u, u)
            for n in range(B - 2, B + 1):
                body(n, n % 2)

        def ahead(n, u, s, by):
            over, s = divmod(s + by, NSU)
            return n + over, (u + over) % 2, s

        def keys_of(s):
            lo, hi = KEYS[UNIT[s][0]]
            return len(UNIT[s][1]), lo, hi

        def scores_of(tile, s):
            nh, lo, hi = keys_of(s)
            return tile[:, 0:nh * (hi - lo)].rearrange("p (h k) -> p h k", h=nh)

        def probs_of(s):
            nh, lo, hi = keys_of(s)
            return prob[s][:, :].rearrange("p (h k) -> p h k", h=nh)[:, :, lo:hi]

        def heads(ap):
            return ap.rearrange("p (m h) d -> p m h d", m=2)

        def table(tab, t, lo, hi):
            return tab[:, t, :, lo:hi].unsqueeze(2).broadcast_to([P, 2, FH, hi - lo])

        @block.gpsimd
        def _(pool):
            def turn_halves(n, t):
                if exists(n):
                    pool.wait_ge(raw_ready, 2 * n + t + 1)
                    for lo, frm in ((0, FD // 2), (FD // 2, 0)):
                        pool.tensor_tensor(heads(turned_half[t][:, :, lo:lo + FD // 2]),
                                           heads(raw[t][:, :, frm:frm + FD // 2]),
                                           table(tabB, t, lo, lo + FD // 2), ALU.mult).then_inc(halved, 1)

            def join(n, u, t):
                if exists(n):
                    pool.wait_ge(halved, (2 * n + t) * 2 + 2)
                    pool.wait_ge(straight, 2 * n + t + 1)
                    pool.tensor_tensor(direct[u][t][:, :, :], direct[u][t][:, :, :], turned_half[t][:, :, :],
                                       ALU.add).then_inc(joined, 1)

            def turn(n, u):
                for s in range(NSU):
                    if s == 3:
                        turn_halves(n + 2, 0)
                        join(n + 2, u, 0)
                    if s == 4:
                        turn_halves(n + 2, 1)
                        join(n + 2, u, 1)

            pool.wait_ge(ready, 5)
            turns(pool, turn)

        @block.tensor
        def _(pe):
            def project_qk(n, u, t):
                if exists(n):
                    if t == 0:
                        pe.wait_ge(shifted, 2 * n + 2)
                        at_least(pe, placed, 6 * n)
                    else:
                        pe.wait_ge(raw_ready, 2 * n + 1)
                    for m in range(2):
                        ins = pe.matmul(psqk[:, m * FH:(m + 1) * FH, :], hs[u][:, t * P:(t + 1) * P],
                                        w["wqkv"][:, m * INNER:(m + 1) * INNER], start=True, stop=True)
                    ins.then_inc(qk_projected, 1)

            def project_v(n, u, t):
                if exists(n):
                    if t == 0:
                        at_least(pe, added, n - 1)
                    else:
                        pe.wait_ge(v_ready, 2 * n + 1)
                    pe.matmul(psvy[:, :], hs[u][:, t * P:(t + 1) * P], w["wqkv"][:, 2 * INNER:3 * INNER],
                              start=True, stop=True).then_inc(v_projected, 1)

            def flip(n, u, t):
                if exists(n):
                    pe.wait_ge(scaled[t], n + 1)
                    if t == 1:
                        pe.wait_ge(placed, 6 * n + 3)
                    for p in range(FH):
                        ins = pe.transpose(psqk[:, 2 * p:2 * p + 2, :].rearrange("p h d -> p (h d)"),
                                           direct[u][t][:, 2 * p:2 * p + 2, :].rearrange("p h d -> p (h d)"),
                                           w["identity"][:, :])
                    ins.then_inc(flipped, 1)

            def score(n, u, s):
                if exists(n):
                    blk, heads = UNIT[s]
                    nh, lo, hi = keys_of(s)
                    if s == 0:
                        pe.wait_ge(placed, 6 * n + 6)
                    at_least(pe, masked, n * NSU + s - 1)
                    for m, h in enumerate(heads):
                        ins = pe.matmul(scores_of(pss[s % 2], s)[:, m, :], qz[u][:, h, blk * P:(blk + 1) * P],
                                        kT[u][:, h // 2, lo:hi], start=True, stop=True)
                    ins.then_inc(scored, 1)

            def turn_over(n, s):
                if exists(n):
                    pe.wait_ge(normed, n * NSU + s + 1)
                    at_least(pe, copied, n * NSU + s)
                    for m in range(CH // P):
                        ins = pe.transpose(pst[:, m * P:(m + 1) * P], prob[s][:, m * P:(m + 1) * P], w["identity"][:, :])
                    ins.then_inc(turned, 1)

            def value(n, u, s):
                if exists(n):
                    blk, heads = UNIT[s]
                    pe.wait_ge(copied, n * NSU + s + 1)
                    if s == 0:
                        pe.wait_ge(v_ready, 2 * n + 2)
                    if s < 2:
                        at_least(pe, o_ready, 2 * n - 1 + s)
                    for m, h in enumerate(heads):
                        for j in range(blk + 1):
                            at = (m * (blk + 1) + j) * P
                            ins = pe.matmul(pso[64 * (h % 2):64 * (h % 2) + 64, h // 2, blk * P:(blk + 1) * P],
                                            vt[u][:, j, h * FD:(h + 1) * FD], probT[s % 2][:, at:at + P],
                                            start=(j == 0), stop=(j == blk))
                    ins.then_inc(valued, 1)

            def project_out(n):
                if exists(n):
                    pe.wait_ge(o_ready, 2 * n + 2)
                    pe.wait_ge(v_ready, 2 * n + 4 if exists(n + 1) else 2 * B)
                    for p in range(FH // 2):
                        ins = pe.matmul(psvy[:, 0:S], w["wo"][:, p, :], oT[:, p, :], start=(p == 0), stop=(p == FH // 2 - 1))
                    ins.then_inc(out_ready, 1)

            def turn(n, u):
                for s in range(NSU):
                    score(*ahead(n, u, s, 3))
                    turn_over(n, s)
                    value(*ahead(n, u, s, -1))
                    if s == 0:
                        flip(n + 1, 1 - u, 0)
                    if s == 1:
                        project_out(n - 1)
                        flip(n + 1, 1 - u, 1)
                    if s == 2:
                        project_qk(n + 2, u, 0)
                    if s == 3:
                        project_qk(n + 2, u, 1)
                    if s == 4:
                        project_v(n + 1, 1 - u, 0)
                    if s == 5:
                        project_v(n + 1, 1 - u, 1)

            pe.wait_ge(ready, 5)
            turns(pe, turn)

        @block.vector
        def _(dve):
            def shift(n, u):
                if exists(n):
                    at_least(dve, v_projected, 2 * n - 2)
                    dve.tensor_copy(hs[u][0:64, :], zT[0:64, ds(n * S, S)]).then_inc(shifted, 1)
                    dve.tensor_copy(hs[u][64:P, 1:S], zT[64:P, ds(n * S, S - 1)]).then_inc(shifted, 1)

            def sums(n, t):
                if exists(n):
                    dve.wait_ge(squared, 2 * n + t + 1)
                    dve.tensor_reduce(sumsq[:, t, :], square[:, :, :], AX.X, ALU.add).then_inc(summed, 1)

            def straight_part(n, u, t):
                if exists(n):
                    dve.wait_ge(raw_ready, 2 * n + t + 1)
                    dve.tensor_tensor(heads(direct[u][t][:, :, :]), heads(raw[t][:, :, :]), table(tabA, t, 0, FD),
                                      ALU.mult).then_inc(straight, 1)

            def inverse_norms(n):
                if not exists(n):
                    return
                own = Own(dve, newton, NEWTON)
                own.turn(n)
                flat = lambda x: x[:, :, :].rearrange("p t h -> p (t h)")
                x, y, a, b = flat(sumsq), flat(inv_norm), flat(tmp_a), flat(tmp_b)
                dve.wait_ge(summed, 2 * n + 2)
                own.step(dve.tensor_scalar(x, x, 1e-24, None, ALU.max))
                own.wait()
                own.step(dve.tensor_scalar(a.bitcast(I32), x.bitcast(I32), 1, None, ALU.logical_shift_right))
                own.wait()
                own.step(dve.tensor_scalar(y.bitcast(I32), a.bitcast(I32), -1.0, float(0x5f3759df), ALU.mult, ALU.add))
                for _ in range(3):
                    own.wait()
                    own.step(dve.scalar_tensor_tensor(a, y, -0.5, x, ALU.mult, ALU.mult))
                    own.wait()
                    own.step(dve.tensor_tensor(b, a, y, ALU.mult))
                    own.wait()
                    own.step(dve.scalar_tensor_tensor(y, b, 1.5, y, ALU.add, ALU.mult))
                assert own.n == NEWTON

            def scale(n, u, t):
                if exists(n):
                    dve.wait_ge(newton, (n + 1) * NEWTON)
                    dve.wait_ge(joined, 2 * n + t + 1)
                    dve.tensor_tensor(direct[u][t][:, :, :], direct[u][t][:, :, :],
                                      inv_norm[:, t, :].unsqueeze(2).broadcast_to([P, QK, FD]),
                                      ALU.mult).then_inc(scaled[t], 1)

            def mask(n, u, s):
                if not exists(n):
                    return
                blk, heads = UNIT[s]
                nh, lo, hi = keys_of(s)
                r, c = s % 2, n * NSU + s
                dve.wait_ge(scored, c + 1)
                dve.memset(beat[:, :], 0.0)
                for m in range(nh):
                    ins = dve.tensor_tensor_reduce(out=scores_of(sim[r], s)[:, m, :], in0=scores_of(pss[r], s)[:, m, :],
                                                   in1=w["window"][:, blk, lo:hi], scale=1.0, scalar=NEG, op0=ALU.add,
                                                   op1=ALU.max, accum_out=top[r][:, m:m + 1])
                ins.then_inc(masked, 1)
                dve.wait_ge(masked, c + 1)
                dve.tensor_scalar(neg_top[r][:, 0:nh], top[r][:, 0:nh], -1.0, None, ALU.mult).then_inc(negated, 1)

            def invert(n, u, s):
                if exists(n):
                    r, c, nh = s % 2, n * NSU + s, len(UNIT[s][1])
                    dve.wait_ge(exped, c + 1)
                    dve.reciprocal(inv_total[r][:, 0:nh], total[r][:, 0:nh]).then_inc(inverted, 1)

            def norm(n, u, s):
                if exists(n):
                    nh, lo, hi = keys_of(s)
                    dve.wait_ge(inverted, n * NSU + s + 1)
                    dve.tensor_tensor(probs_of(s), probs_of(s),
                                       inv_total[s % 2][:, 0:nh].unsqueeze(2).broadcast_to([P, nh, hi - lo]),
                                       ALU.mult).then_inc(normed, 1)

            def add(n):
                if exists(n):
                    dve.wait_ge(out_ready, n + 1)
                    at = ds(n * S, S)
                    dve.tensor_tensor(zT[:, at], psvy[:, 0:S], zT[:, at], ALU.add).then_inc(added, 1)

            def turn(n, u):
                for s in range(NSU):
                    mask(*ahead(n, u, s, 2))
                    invert(*ahead(n, u, s, 1))
                    norm(*ahead(n, u, s, 1))
                    if s == 0:
                        scale(n + 1, 1 - u, 1)
                        shift(n + 2, u)
                    if s == 2:
                        add(n - 1)
                    if s == 3:
                        sums(n + 2, 0)
                        straight_part(n + 2, u, 0)
                    if s == 4:
                        sums(n + 2, 1)
                        straight_part(n + 2, u, 1)
                    if s == 5:
                        inverse_norms(n + 2)
                        scale(n + 2, u, 0)

            for u in range(2):
                dve.memset(hs[u][64:P, 0:1], 0.0)
                dve.memset(qz[u][:, :, :], 0.0).then_inc(ready, 1)
            for s in range(2, NSU):
                ins = dve.memset(prob[s][:, :].rearrange("p (h k) -> p h k", h=2)[:, :, 0:WINDOW], 0.0)
            ins.then_inc(ready, 1)
            for tab, const, scales in ((tabA, "cosine", "scales"), (tabB, "sine", "scales_turned")):
                dve.tensor_tensor(tab[:, :, :, :].rearrange("p t m d -> p t (m d)"),
                                  w[const][:, :, :, :].rearrange("p t m d -> p t (m d)"),
                                  w[scales][:, :, :].rearrange("p m d -> p (m d)").unsqueeze(1).broadcast_to([P, 2, 2 * FD]),
                                  ALU.mult).then_inc(ready, 1)
            dve.wait_ge(ready, 5)
            turns(dve, turn)

        @block.scalar
        def _(act):
            def squares(n, t):
                if exists(n):
                    act.wait_ge(qk_projected, 2 * n + t + 1)
                    at_least(act, summed, 2 * n + t)
                    act.activation(square[:, :, :], psqk[:, :, :], ACT.Square).then_inc(squared, 1)
                    at_least(act, joined, 2 * n + t - 1)
                    act.activation(raw[t][:, :, :], psqk[:, :, :], ACT.Copy).then_inc(raw_ready, 1)

            def copy_v(n, u, t):
                if exists(n):
                    act.wait_ge(v_projected, 2 * n + t + 1)
                    act.activation(vt[u][:, t, :], psvy[:, :], ACT.Copy).then_inc(v_ready, 1)

            def place(n, u, t):
                if not exists(n):
                    return
                act.wait_ge(flipped, 2 * n + t + 1)
                q = psqk[:, 0:FH, :].rearrange("p (h e) d -> p h (e d)", e=2)
                k = psqk[:, FH:QK, :].rearrange("p (h e) d -> p h (e d)", e=2)
                at = slice(t * P, (t + 1) * P)
                for e in range(2):
                    rows = slice(64 * e, 64 * e + 64)
                    act.activation(qz[u][rows, e:FH:2, at], q[rows, :, :], ACT.Copy).then_inc(placed, 1)
                act.activation(kT[u][:, :, at], k, ACT.Copy).then_inc(placed, 1)

            def exps(n, u, s):
                if not exists(n):
                    return
                nh, r = len(UNIT[s][1]), s % 2
                act.wait_ge(negated, n * NSU + s + 1)
                for m in range(nh):
                    ins = act.activation(probs_of(s)[:, m, :], scores_of(sim[r], s)[:, m, :], ACT.Exp,
                                         bias=neg_top[r][:, m:m + 1], accum_out=total[r][:, m:m + 1])
                ins.then_inc(exped, 1)

            def copy(n, s):
                if exists(n):
                    act.wait_ge(turned, n * NSU + s + 1)
                    act.activation(probT[s % 2][:, :], pst[:, :], ACT.Copy).then_inc(copied, 1)

            def copy_out(n, b):
                if exists(n):
                    act.wait_ge(valued, n * NSU + (4, 6)[b])
                    at_least(act, out_ready, n)
                    act.activation(oT[:, 2 * b:2 * b + 2, :], pso[:, 2 * b:2 * b + 2, :], ACT.Copy).then_inc(o_ready, 1)

            def turn(n, u):
                for s in range(NSU):
                    exps(*ahead(n, u, s, 2))
                    copy(n, s)
                    if s == 0:
                        copy_out(n - 1, 1)
                        place(n + 1, 1 - u, 0)
                    if s == 1:
                        place(n + 1, 1 - u, 1)
                    if s == 2:
                        squares(n + 2, 0)
                    if s == 3:
                        squares(n + 2, 1)
                    if s == 4:
                        copy_v(n + 1, 1 - u, 0)
                    if s == 5:
                        copy_v(n + 1, 1 - u, 1)
                        copy_out(n, 0)

            act.wait_ge(ready, 5)
            turns(act, turn)


def shift_tokens(nc, tag, zT, hs):
    with ExitStack() as ctx:
        shifted = ctx.enter_context(nc.semaphore(f"{tag}_shifted"))
        block = ctx.enter_context(nc.Block())
        by_batch = lambda x: x[64:P, :].rearrange("p (b s) -> p b s", b=B)

        @block.vector
        def _(dve):
            dve.tensor_copy(hs[0:64, :], zT[0:64, :]).then_inc(shifted, 1)
            dve.tensor_copy(by_batch(hs)[:, :, 1:S], by_batch(zT)[:, :, 0:S - 1]).then_inc(shifted, 1)
            dve.memset(by_batch(hs)[:, :, 0:1], 0.0).then_inc(shifted, 1)
            dve.wait_ge(shifted, 3)


def gated_unit(nc, tag, zT, hs, w):
    with ExitStack() as ctx:
        sb = lambda name, shape, dt=F32: ctx.enter_context(nc.sbuf_tensor(f"{tag}_{name}", shape, dt))
        ps = lambda name, shape: ctx.enter_context(nc.psum_tensor(f"{tag}_{name}", shape, F32))
        sem = lambda name: ctx.enter_context(nc.semaphore(f"{tag}_{name}"))
        psa = [ps(f"psa{c}", [P, CH]) for c in range(HC)]
        psg = [ps(f"psg{c}", [P, CH]) for c in range(HC)]
        psy = ps("psy", [P, CH])
        gelu = [sb(f"gelu{c}", [P, CH]) for c in range(HC)]
        gated = [[sb(f"gated{u}{c}", [P, CH]) for c in range(HC)] for u in range(2)]
        affine, up, gelu_ready, gate_ready = sem("affine"), sem("up"), sem("gelu_ready"), sem("gate_ready")
        down, added = sem("down"), sem("added")
        block = ctx.enter_context(nc.Block())

        def chunks(eng, body):
            body(0, 0)
            with eng.Fori(0, NCH // 2 - 1) as i:
                for u in range(2):
                    body(2 * i + 1 + u, 1 - u)
            body(NCH - 1, 1)

        @block.tensor
        def _(pe):
            def widen(n, c):
                if not isinstance(n, int) or n > 0:
                    pe.wait_ge(gate_ready, HC * (n - 1) + c + 1)
                for m, out in ((HC + c, psg[c]), (c, psa[c])):
                    ins = pe.matmul(out[:, :], w["w1"][:, m * P:(m + 1) * P], hs[:, ds(n * CH, CH)],
                                    start=True, stop=True)
                ins.then_inc(up, 1)

            def narrow(n, u):
                pe.wait_ge(gate_ready, HC * (n + 1))
                if not isinstance(n, int) or n > 0:
                    pe.wait_ge(added, n)
                for c in range(HC):
                    ins = pe.matmul(psy[:, :], w["w2"][:, c, :], gated[u][c][:, :], start=(c == 0), stop=(c == HC - 1))
                ins.then_inc(down, 1)

            def chunk(n, u):
                widen(n, 0)
                if not isinstance(n, int) or n > 0:
                    narrow(n - 1, 1 - u)
                widen(n, 1)
                widen(n, 2)

            assert HC == 3
            pe.wait_ge(affine, 1)
            chunks(pe, chunk)
            narrow(NCH - 1, 1)

        @block.scalar
        def _(act):
            with act.Fori(0, NCH) as n:
                for c in range(HC):
                    act.wait_ge(up, HC * n + c + 1)
                    act.activation(gelu[c][:, :], psg[c][:, :], ACT.Gelu,
                                   bias=w["b1"][:, HC + c:HC + c + 1]).then_inc(gelu_ready, 1)

        @block.vector
        def _(dve):
            def add(n):
                dve.wait_ge(down, n + 1)
                at = ds(n * CH, CH)
                dve.scalar_tensor_tensor(zT[:, at], psy[:, :], w["b2"][:, 0:1], zT[:, at],
                                         ALU.add, ALU.add).then_inc(added, 1)

            def chunk(n, u):
                for c in range(HC):
                    dve.wait_ge(gelu_ready, HC * n + c + 1)
                    dve.scalar_tensor_tensor(gated[u][c][:, :], psa[c][:, :], w["b1"][:, c:c + 1], gelu[c][:, :],
                                             ALU.add, ALU.mult).then_inc(gate_ready, 1)
                    if c == 0 and (not isinstance(n, int) or n > 0):
                        add(n - 1)

            dve.tensor_scalar(hs[:, :], hs[:, :], w["ln_g"][:, 0:1], w["ln_b"][:, 0:1], ALU.mult, ALU.add).then_inc(affine, 1)
            chunks(dve, chunk)
            add(NCH - 1)


def build(nc, a, out):
    with ExitStack() as ctx:
        sb = lambda name, shape, dt=F32: ctx.enter_context(nc.sbuf_tensor(name, shape, dt))
        xT = sb("xT", [P, T])
        zT = sb("zT", [P, T])
        ones_mean = sb("ones_mean", [P, P])
        eps = sb("eps", [P, 1])
        norms = {"ones_mean": ones_mean, "eps": eps, "runs": 0, "sems": [
            ctx.enter_context(nc.semaphore(f"norm_{n}")) for n in (
                "mean_ready", "centered", "square_ready", "var_ready", "log_ready", "rstd_ready", "rsquare_ready",
                "newton", "normed")]}
        loaded, made, stored = (ctx.enter_context(nc.semaphore(n)) for n in ("loaded", "made", "stored"))
        with nc.Block() as block:
            @block.sync
            def _(sp):
                sp.dma_start(xT[:, :], a["x"]).then_inc(loaded, 16)
                sp.wait_ge(loaded, 16)

            @block.vector
            def _(dve):
                dve.memset(ones_mean[:, :], 1.0 / D)
                dve.memset(eps[:, :], 1e-5).then_inc(made, 1)
                dve.wait_ge(made, 1)
        with ExitStack() as c1:
            w, loads = tiles_for(nc, c1, "w1", {
                "wq": (a["r_wq"], [P, D]), "wk": (a["r_wk"], [P, D]), "wn": (a["r_wn"], [P, D]),
                "wv": (a["r_wv"], [P, D]), "bq": (a["r_bq"], [P, 1]), "bk": (a["r_bk"], [P, 1]),
                "bn": (a["r_bn"], [P, 1]), "bv": (a["r_bv"], [P, D]), "wo": (a["r_wo"], [P, HG, D]),
                "bo": (a["r_bo"], [P, 1]), "causal": (a["causal"], [P, S])})
            s1 = lambda name, shape, dt=F32: c1.enter_context(nc.sbuf_tensor(name, shape, dt))
            q9, k9 = ([s1(f"{x}9{m}", [P, H, 2 * S], BF16) for m in range(2)] for x in "qk")
            layer_norm(nc, "n1", norms, xT, zT, loads,
                       [x[64:P, :, :].bitcast(F32) for x in (*q9, *k9)])
            qp, kp = s1("qp", [P, PARTS, T], BF16), s1("kp", [P, PARTS, T], BF16)
            vtok = s1("vtok", [P, T // P, D])
            retention_project(nc, zT, w, qp, kp, vtok)
            retention(nc, xT, w, qp, kp, vtok, w["causal"], q9, k9)
        with ExitStack() as c2:
            w, loads = tiles_for(nc, c2, "w2", {
                "wq": (a["x_wq"], [P, D]), "wk": (a["x_wk"], [P, D]), "wv": (a["x_wv"], [P, D]),
                "wo": (a["x_wo"], [P, HG, D])})
            layer_norm(nc, "n2", norms, xT, zT, loads)
            qp = c2.enter_context(nc.sbuf_tensor("x_qp", [P, PARTS, T], BF16))
            cross_queries(nc, zT, w["wq"], qp)
            cross_attention(nc, xT, w, qp, a["context"])
        with ExitStack() as c3:
            ws, loads = [], []
            for l in range(DEPTH):
                w, more = tiles_for(nc, c3, f"w3{l}", {
                    "wqkv": (a["f_wqkv"][l], [P, 3 * INNER]), "wo": (a["f_wo"][l], [P, FH // 2, D]),
                    "cosine": (a["cosine"], [P, 2, 2, FD]), "sine": (a["sine"], [P, 2, 2, FD]),
                    "scales": (a["f_scales"][l], [P, 2, FD]), "scales_turned": (a["f_scales_turned"][l], [P, 2, FD]),
                    "window": (a["window"], [P, 2, S]), "identity": (a["identity"], [P, P]),
                    "ln_g": (a["f_ln_g"][l], [P, 1]), "ln_b": (a["f_ln_b"][l], [P, 1]),
                    "w1": (a["f_w1"][l], [P, 2 * HC * P]), "b1": (a["f_b1"][l], [P, 2 * HC]),
                    "w2": (a["f_w2"][l], [P, HC, D]), "b2": (a["f_b2"][l], [P, 1])})
                ws.append(w)
                loads += more
            layer_norm(nc, "n3", norms, xT, zT, loads)
            hs = c3.enter_context(nc.sbuf_tensor("hs", [P, T], F32))
            for l, w in enumerate(ws):
                local_attention(nc, f"l{l}", zT, w)
                shift_tokens(nc, f"t{l}", zT, hs)
                layer_norm(nc, f"m{l}", norms, hs, hs)
                gated_unit(nc, f"g{l}", zT, hs, w)
        with ExitStack() as c4:
            done = c4.enter_context(nc.semaphore("sum_done"))
            block = c4.enter_context(nc.Block())

            @block.vector
            def _(dve):
                dve.tensor_tensor(xT[:, :], xT[:, :], zT[:, :], ALU.add).then_inc(done, 1)
                dve.wait_ge(done, 1)
        with nc.Block() as block:
            @block.sync
            def _(sp):
                sp.dma_start(out, xT[:, :]).then_inc(stored, 16)
                sp.wait_ge(stored, 16)


def tiles_for(nc, ctx, tag, table):
    tiles = {k: ctx.enter_context(nc.sbuf_tensor(f"{tag}_{k}", shape, F32)) for k, (_, shape) in table.items()}
    return tiles, [(tiles[k][tuple(slice(None) for _ in shape)], dram) for k, (dram, shape) in table.items()]


def layouts(x, ctx_1024, L0_attn_Wqk, L0_attn_bqk, L0_attn_Wv, L0_attn_bv, L0_attn_Wn, L0_attn_bn, L0_attn_Wo,
            L0_attn_bo, L0_xattn_Wq, L0_xattn_Wk, L0_xattn_Wv, L0_xattn_Wo, L0_ffn_wqkv, L0_ffn_q_scale,
            L0_ffn_k_scale, L0_ffn_wo, L0_ffn_ln_g, L0_ffn_ln_b, L0_ffn_w1, L0_ffn_b1, L0_ffn_w2, L0_ffn_b2):
    import numpy as np

    f = lambda v: np.ascontiguousarray(np.asarray(v), dtype=np.float32)
    col = lambda v: f(v).reshape(-1, 1)
    rep = lambda v: f(np.broadcast_to(np.asarray(v), (P, np.asarray(v).shape[-1])))
    s = np.arange(P)[:, None]
    t = np.arange(S)[None, :]
    halves = np.array([(e * 8 + h) * HD + d for e in range(2) for d in range(HD) for h in range(8)])
    context = np.zeros((B, D, CTXP), np.float32)
    context[:, :, 0:CTX] = np.asarray(ctx_1024).transpose(0, 2, 1)
    dmaj = np.array([h * HD + d for d in range(HD) for h in range(H)])
    hmaj = np.array([h for d in range(HD) for h in range(H)])
    wqk, bqk = np.asarray(L0_attn_Wqk), np.asarray(L0_attn_bqk)

    def spread(wo):
        o = np.zeros((HL, 32, HG, D), np.float32)
        o[:, 0:HD] = np.asarray(wo).reshape(HG, HL, HD, D).transpose(1, 2, 0, 3)
        return o.reshape(P, HG, D)

    w1 = np.zeros((DEPTH, D, 2, HC * P), np.float32)
    w1[..., 0:HID] = np.asarray(L0_ffn_w1).reshape(DEPTH, D, 2, HID)
    b1 = np.zeros((DEPTH, 2, HC * P), np.float32)
    b1[..., 0:HID] = np.asarray(L0_ffn_b1).reshape(DEPTH, 2, HID)
    w2 = np.zeros((DEPTH, HC * P, D), np.float32)
    w2[:, 0:HID] = np.asarray(L0_ffn_w2)
    qk_scales = np.stack([np.asarray(L0_ffn_q_scale), np.asarray(L0_ffn_k_scale)], 1)
    both = lambda g: f(np.broadcast_to(g(qk_scales)[:, None], (DEPTH, P, 2, FD)))
    half = np.arange(0, FD, 2, dtype=np.float32)
    place = np.arange(S, dtype=np.float32)
    freq = (place[:, None] * (np.float32(1.0) / np.float32(10000.0) ** (half / np.float32(FD)))[None, :]).astype(np.float32)
    power = (place - S // 2) / np.float32(WINDOW // 2)
    xpos = ((half + 0.4 * FD) / (1.4 * FD))[None, :].astype(np.float64) ** power[:, None]
    cos, sin = np.cos(freq.astype(np.float64)), np.sin(freq.astype(np.float64))
    by_scale = lambda v: np.stack([v * xpos * 8.0, v / xpos], 1)
    cosine = by_scale(cos)[:, :, None, :].repeat(2, 2)
    sine = np.stack([-by_scale(sin), by_scale(sin)], 2)
    tiles = lambda v: f(v.reshape(2, P, 2, FD).transpose(1, 0, 2, 3))
    cosine, sine = tiles(cosine), tiles(sine)
    window = np.full((P, 2, S), NEG, np.float32)
    for blk in range(2):
        i = blk * P + s
        window[:, blk][(t <= i) & (t >= i - WINDOW)] = 0.0
    return {
        "x": f(np.asarray(x).reshape(T, D).T),
        "r_wq": f(wqk[:, 0:D][:, dmaj]), "r_wk": f(wqk[:, D:][:, dmaj]), "r_wn": f(np.asarray(L0_attn_Wn)[:, hmaj]),
        "r_wv": f(L0_attn_Wv), "r_bq": col(bqk[0:D][dmaj]), "r_bk": col(bqk[D:][dmaj]),
        "r_bn": col(np.asarray(L0_attn_bn)[hmaj]), "r_bv": rep(L0_attn_bv), "r_wo": spread(L0_attn_Wo),
        "r_bo": col(L0_attn_bo),
        "x_wq": f(np.asarray(L0_xattn_Wq).T[:, halves]), "x_wk": f(np.asarray(L0_xattn_Wk).T[:, halves]),
        "x_wv": f(np.asarray(L0_xattn_Wv).T), "x_wo": spread(np.asarray(L0_xattn_Wo).T),
        "context": context,
        "f_wqkv": f(L0_ffn_wqkv), "f_wo": f(np.asarray(L0_ffn_wo).reshape(DEPTH, FH // 2, P, D).transpose(0, 2, 1, 3)),
        "f_scales": both(lambda v: v), "f_scales_turned": both(lambda v: np.roll(v, FD // 2, axis=-1)),
        "f_ln_g": f(L0_ffn_ln_g)[:, :, None], "f_ln_b": f(L0_ffn_ln_b)[:, :, None],
        "f_w1": w1.reshape(DEPTH, D, 2 * HC * P), "f_b1": f(b1.reshape(DEPTH, 2 * HC, P).transpose(0, 2, 1)),
        "f_w2": f(w2.reshape(DEPTH, HC, P, D).transpose(0, 2, 1, 3)), "f_b2": f(L0_ffn_b2)[:, :, None],
        "cosine": cosine, "sine": sine, "window": window, "identity": np.eye(P, dtype=np.float32),
        "causal": (s <= t).astype(np.float32),
    }


def kernel(**inputs):
    import numpy as _np
    import concourse.bacc as _bacc
    from concourse import mybir as _mybir
    from concourse.bass_utils import run_bass_kernel_spmd as _run

    nc = _bacc.Bacc("TRN2", target_bir_lowering=False, num_devices=1)
    arrays, args = {}, {}
    for name, arr in layouts(**inputs).items():
        arrays[f"in_{name}"] = arr
        args[name] = nc.dram_tensor(f"in_{name}", arr.shape, _mybir.dt.from_np(arr.dtype), kind="ExternalInput").ap()
    out = nc.dram_tensor("out_x", (P, T), F32, kind="ExternalOutput").ap()
    build(nc, args, out)
    r = _run(nc, [arrays], core_ids=[0])
    return _np.ascontiguousarray(r.results[0]["out_x"].T).reshape(B, S, D)
```

```python
from contextlib import ExitStack

import concourse.bass as bass
from concourse import mybir
from concourse.bass import ds

F32 = mybir.dt.float32
BF16 = mybir.dt.bfloat16
I32 = mybir.dt.int32
ALU = mybir.AluOpType
ACT = mybir.ActivationFunctionType
AX = mybir.AxisListType

P = 128
B, S, D = 16, 256, 128
T = B * S
H, HD = 16, 8
HG, HL = 4, 4
PARTS = 3
COMBOS = PARTS * PARTS
ROWS = COMBOS * HD
PAIR_DMAS = 2 * COMBOS
CTX = 1601
ST = (CTX + P - 1) // P
CTXP = ST * P
KCH = CTXP // HG
VCH = [(0, 4), (4, 7), (7, 10), (10, 13)]
CH = 512
NCH = T // CH
FH, FD = 8, 64
INNER = FH * FD
WINDOW = 64
DEPTH = 2
HID = 341
HC = (HID + P - 1) // P
NEG = -3.0e38


class Own:

    def __init__(self, eng, sem, per):
        self.eng, self.sem, self.per, self.base, self.n = eng, sem, per, 0, 0

    def turn(self, i):
        assert self.n in (0, self.per), (self.n, self.per)
        self.base, self.n = i * self.per, 0

    def step(self, ins):
        ins.then_inc(self.sem, 1)
        self.n += 1
        return self.n

    def wait(self, n=None):
        self.eng.wait_ge(self.sem, self.base + (self.n if n is None else n))


def layer_norm(nc, tag, norms, src, dst, loads=(), zeros=(), gain=None, source=None,
               shift_of=None):
    ones_mean, eps, pick, run = norms["ones_mean"], norms["eps"], norms["pick"], norms["runs"]
    norms["runs"] += 1
    base, NG, WARM = run * NCH, NCH // 4, 8
    mean_ready, centered, square_ready, var_ready, log_ready, guess_ready, newton, spread, normed = norms["sems"]
    with ExitStack() as ctx:
        sb = lambda name, shape, dt: ctx.enter_context(nc.sbuf_tensor(f"{tag}_{name}", shape, dt))
        ps = lambda name, shape: ctx.enter_context(nc.psum_tensor(f"{tag}_{name}", shape, F32))
        sem = lambda name: ctx.enter_context(nc.semaphore(f"{tag}_{name}"))
        square = [sb(f"square{u}", [P, CH], F32) for u in range(4)]
        rstd = [sb(f"rstd{g}", [P, CH], F32) for g in range(NG)]
        rsquare = [sb(f"rsquare{g}", [P, CH], F32) for g in range(NG)]
        mean = [ps(f"mean{u}", [P, CH]) for u in range(3)]
        var = [ps(f"var{g}", [P, CH]) for g in range(NG)]
        wide = [ps(f"wide{u}", [P, CH]) for u in range(3)]
        early = sb("early", [P, 1], F32)
        at = [slice(n * CH, (n + 1) * CH) for n in range(NCH)]
        landed = sem("landed") if loads else None
        arrived = [sem(f"arrived{n}") for n in range(NCH)] if source is not None else None
        shifted = sem("shifted") if shift_of is not None else None
        cleared = sem("cleared") if zeros else None
        block = ctx.enter_context(nc.Block())

        if loads or source is not None:
            @block.sync
            def _(sp):
                if source is not None:
                    for n in range(NCH):
                        sp.dma_start(src[:, at[n]], source[:, at[n]]).then_inc(arrived[n], 16)
                for tile, dram in loads:
                    sp.dma_start(tile, dram).then_inc(landed, 16)
                if loads:
                    sp.wait_ge(landed, 16 * len(loads))

        if zeros:
            @block.gpsimd
            def _(pool):
                for n, ap in enumerate(zeros):
                    pool.memset(ap, 0.0).then_inc(cleared, 1)
                    pool.wait_ge(cleared, n + 1)

        @block.tensor
        def _(pe):
            def variance(n):
                pe.wait_ge(square_ready, base + n + 1)
                lo = 32 * (n % 4)
                pe.matmul(var[n // 4][lo:lo + 32, :], ones_mean[:, 0:32], square[n % 4][:, :],
                          start=True, stop=True).then_inc(var_ready, 1)

            def mean_of(n):
                if source is not None:
                    pe.wait_ge(arrived[n], 16)
                if shift_of is not None:
                    pe.wait_ge(shifted, 3 * (n + 1))
                if n >= 3:
                    pe.wait_ge(centered, base + n - 2)
                pe.matmul(mean[n % 3][:, :], ones_mean[:, :], src[:, at[n]], start=True, stop=True).then_inc(mean_ready, 1)

            def widen(n):
                if n % 4 == 0:
                    pe.wait_ge(newton, (run * NG + n // 4) * 3 + 3)
                if n >= 3:
                    pe.wait_ge(normed, base + n - 2)
                lo = 32 * (n % 4)
                pe.matmul(wide[n % 3][:, :], pick[lo:lo + 32, :], rstd[n // 4][lo:lo + 32, :],
                          start=True, stop=True).then_inc(spread, 1)

            def keep_warm(times, bank):
                for _ in range(times):
                    pe.matmul(bank[:, 0:P], ones_mean[:, :], ones_mean[:, :], start=True, stop=True)

            for n in range(5):
                mean_of(n)
            for n in range(4):
                variance(n)
            for n in range(5, NCH):
                mean_of(n)
            keep_warm(WARM, wide[0])
            for n in range(4, NCH):
                variance(n)
                keep_warm(2, wide[0])
            for n in range(4):
                widen(n)
            keep_warm(WARM, mean[0])
            for n in range(4, NCH):
                widen(n)

        @block.vector
        def _(dve):
            def refine(g):
                done = (run * NG + g) * 3
                dve.wait_ge(guess_ready, (run * NG + g) * 2 + 2)
                dve.scalar_tensor_tensor(rsquare[g][:, :], var[g][:, :], eps[:, 0:1], rsquare[g][:, :],
                                         ALU.add, ALU.mult).then_inc(newton, 1)
                dve.wait_ge(newton, done + 1)
                dve.tensor_scalar(rsquare[g][:, :], rsquare[g][:, :], -0.5, 1.5, ALU.mult, ALU.add).then_inc(newton, 1)
                dve.wait_ge(newton, done + 2)
                dve.tensor_tensor(rstd[g][:, :], rsquare[g][:, :], rstd[g][:, :], ALU.mult).then_inc(newton, 1)

            def shift(n):
                by_batch = lambda x: x[64:P, at[n]].rearrange("p (b s) -> p b s", s=S)
                dve.tensor_copy(src[0:64, at[n]], shift_of[0:64, at[n]]).then_inc(shifted, 1)
                dve.tensor_copy(by_batch(src)[:, :, 1:S], by_batch(shift_of)[:, :, 0:S - 1]).then_inc(shifted, 1)
                dve.memset(by_batch(src)[:, :, 0:1], 0.0).then_inc(shifted, 1)

            if shift_of is not None:
                shift(0)
                shift(1)
            for n in range(NCH):
                if shift_of is not None and n + 2 < NCH:
                    shift(n + 2)
                dve.wait_ge(mean_ready, base + n + 1)
                dve.tensor_tensor(dst[:, at[n]], src[:, at[n]], mean[n % 3][:, :], ALU.subtract).then_inc(centered, 1)
            for n in range(NCH):
                if n % 4 == 0:
                    refine(n // 4)
                dve.wait_ge(spread, base + n + 1)
                if gain is None:
                    ins = dve.tensor_tensor(dst[:, at[n]], wide[n % 3][:, :], dst[:, at[n]], ALU.mult)
                else:
                    ins = dve.scalar_tensor_tensor(dst[:, at[n]], wide[n % 3][:, :], gain, dst[:, at[n]],
                                                   ALU.mult, ALU.mult)
                ins.then_inc(normed, 1)

        @block.scalar
        def _(act):
            def log(g):
                act.wait_ge(var_ready, base + 4 * g + 4)
                act.activation(rstd[g][:, :], var[g][:, :], ACT.Ln, bias=eps[:, 0:1]).then_inc(log_ready, 1)

            act.activation(early[:, :], eps[:, :], ACT.Ln)
            for g in range(NG):
                for n in range(4 * g, 4 * g + 4):
                    if n >= 4:
                        act.wait_ge(var_ready, base + n - 3)
                    act.wait_ge(centered, base + n + 1)
                    act.activation(square[n % 4][:, :], dst[:, at[n]], ACT.Square).then_inc(square_ready, 1)
                log(g)
                act.wait_ge(log_ready, run * NG + g + 1)
                act.activation(rstd[g][:, :], rstd[g][:, :], ACT.Exp, scale=-0.5).then_inc(guess_ready, 1)
                act.wait_ge(guess_ready, (run * NG + g) * 2 + 1)
                act.activation(rsquare[g][:, :], rstd[g][:, :], ACT.Square).then_inc(guess_ready, 1)


def stack_pair(sp, m, qp, kp, q9, k9, packed):
    for a in range(PARTS):
        for b in range(PARTS):
            r = (a * PARTS + b) * HD
            at = ds(m * 2 * S, 2 * S)
            sp.dma_start(q9[r:r + HD, :, :], qp[:, a, at]).then_inc(packed, 16)
            sp.dma_start(k9[r:r + HD, :, :], kp[:, b, at]).then_inc(packed, 16)


def retention_project(nc, zT, w, qp, kp, vtok, q9, k9, packed):
    with ExitStack() as ctx:
        sb = lambda name, shape, dt=F32: ctx.enter_context(nc.sbuf_tensor(f"r_{name}", shape, dt))
        ps = lambda name, shape: ctx.enter_context(nc.psum_tensor(f"r_{name}", shape, F32))
        sem = lambda name: ctx.enter_context(nc.semaphore(f"r_{name}"))
        hc = [sb(f"hc{u}", [P, CH]) for u in range(2)]
        inv_n = [sb(f"inv_n{u}", [P, CH]) for u in range(2)]
        q32 = [sb(f"q32{u}", [P, CH]) for u in range(2)]
        k32 = [sb(f"k32{u}", [P, CH]) for u in range(2)]
        psq = [ps(f"psq{u}", [P, CH]) for u in range(2)]
        psk = [ps(f"psk{u}", [P, CH]) for u in range(2)]
        psn = [ps(f"psn{u}", [P, CH]) for u in range(2)]
        psv = [ps(f"psv{u}", [P, CH]) for u in range(2)]
        h_ready, projected, neg_bn = sem("h_ready"), sem("projected"), sem("neg_bn")
        n_exp, k_ready, hi_ready, mid_ready = sem("n_exp"), sem("k_ready"), sem("hi_ready"), sem("mid_ready")
        q_ready, v_ready, rest, last = sem("q_ready"), sem("v_ready"), sem("rest"), sem("last")
        nbn = sb("nbn", [P, 1])
        block = ctx.enter_context(nc.Block())

        def chunks(eng, body):
            for u in range(2):
                body(u, u)
            with eng.Fori(1, NCH // 2) as i:
                for u in range(2):
                    body(2 * i + u, u)

        assert CH == 2 * S

        @block.sync
        def _(sp):
            for m in range(2):
                sp.wait_ge(last, 2 * m + 2)
                stack_pair(sp, m, qp, kp, q9[m], k9[m], packed[m])
            for m in range(2):
                sp.wait_ge(packed[m], PAIR_DMAS * 16)

        @block.tensor
        def _(pe):
            def chunk(n, u):
                pe.wait_ge(h_ready, n + 1)
                if not isinstance(n, int):
                    pe.wait_ge(k_ready, n - 1)
                    pe.wait_ge(v_ready, n - 1)
                pe.matmul(psn[u][:, :], w["wn"][:, :], hc[u][:, :], start=True, stop=True)
                pe.matmul(psq[u][:, :], w["wq"][:, :], hc[u][:, :], start=True, stop=True)
                pe.matmul(psk[u][:, :], w["wk"][:, :], hc[u][:, :], start=True, stop=True)
                for t in range(CH // P):
                    ins = pe.matmul(psv[u][:, t * P:(t + 1) * P], hc[u][:, t * P:(t + 1) * P],
                                    w["wv"][:, :], start=True, stop=True)
                ins.then_inc(projected, 1)

            chunks(pe, chunk)

        @block.gpsimd
        def _(pool):
            def chunk(n, u):
                if not isinstance(n, int):
                    pool.wait_ge(projected, n - 1)
                pool.tensor_copy(hc[u][:, :], zT[:, ds(n * CH, CH)]).then_inc(h_ready, 1)

            chunks(pool, chunk)

        @block.scalar
        def _(act):
            act.mul(nbn[:, :], w["bn"][:, :], -1.0).then_inc(neg_bn, 1)
            act.wait_ge(neg_bn, 1)
            with act.Fori(0, NCH // 2) as i:
                for u in range(2):
                    n = 2 * i + u
                    at = ds(n * CH, CH)
                    act.wait_ge(projected, n + 1)
                    act.activation(inv_n[u][:, :], psn[u][:, :], ACT.Exp, bias=nbn[:, 0:1], scale=-1.0).then_inc(n_exp, 1)
                    act.activation(k32[u][:, :], psk[u][:, :], ACT.Identity, bias=w["bk"][:, 0:1]).then_inc(k_ready, 1)
                    act.wait_ge(k_ready, n + 1)
                    act.activation(kp[:, 0, at], k32[u][:, :], ACT.Copy).then_inc(hi_ready, 1)
                    act.wait_ge(q_ready, n + 1)
                    act.activation(qp[:, 0, at], q32[u][:, :], ACT.Copy).then_inc(hi_ready, 1)
                    act.wait_ge(rest, 2 * n + 1)
                    act.activation(kp[:, 1, at], k32[u][:, :], ACT.Copy).then_inc(mid_ready, 1)
                    act.wait_ge(rest, 2 * n + 2)
                    act.activation(qp[:, 1, at], q32[u][:, :], ACT.Copy).then_inc(mid_ready, 1)

        @block.vector
        def _(dve):
            with dve.Fori(0, NCH // 2) as i:
                for u in range(2):
                    n = 2 * i + u
                    at = ds(n * CH, CH)
                    dve.wait_ge(n_exp, n + 1)
                    dve.scalar_tensor_tensor(q32[u][:, :], psq[u][:, :], w["bq"][:, 0:1], inv_n[u][:, :],
                                             ALU.add, ALU.mult).then_inc(q_ready, 1)
                    dve.tensor_tensor(vtok[:, ds(n * (CH // P), CH // P), :],
                                      psv[u][:, :].rearrange("p (t n) -> p t n", n=P),
                                      w["bv"][:, :].unsqueeze(1).broadcast_to([P, CH // P, P]),
                                      ALU.add).then_inc(v_ready, 1)
                    for m, (x, parts) in enumerate(((k32[u], kp), (q32[u], qp))):
                        dve.wait_ge(hi_ready, 2 * n + m + 1)
                        dve.tensor_tensor(x[:, :], x[:, :], parts[:, 0, at], ALU.subtract).then_inc(rest, 1)
                    for m, (x, parts) in enumerate(((k32[u], kp), (q32[u], qp))):
                        dve.wait_ge(mid_ready, 2 * n + m + 1)
                        dve.tensor_tensor(parts[:, 2, at], x[:, :], parts[:, 1, at], ALU.subtract).then_inc(last, 1)


def retention(nc, xT, w, qp, kp, vtok, causal, q9, k9, vb, packed):
    with ExitStack() as ctx:
        sb = lambda name, shape, dt=F32: ctx.enter_context(nc.sbuf_tensor(f"a_{name}", shape, dt))
        ps = lambda name, shape: ctx.enter_context(nc.psum_tensor(f"a_{name}", shape, F32))
        sem = lambda name: ctx.enter_context(nc.semaphore(f"a_{name}"))
        m0 = [sb(f"m0{r}", [P, HL, S]) for r in range(2)]
        m1 = [sb(f"m1{r}", [P, HL, P]) for r in range(2)]
        oT = [sb(f"oT{u}", [P, S]) for u in range(2)]
        ps0 = [ps(f"ps0{r}", [P, HL, P]) for r in range(2)]
        ps_full = [ps(f"ps_full{r}", [P, HL, P]) for r in range(2)]
        ps1 = [ps(f"ps1{r}", [P, HL, P]) for r in range(2)]
        pso = ps("pso", [P, CH])
        psy = ps("psy", [P, CH])
        v_ready = sem("v_ready")
        score0, score_full, score1 = sem("score0"), sem("score_full"), sem("score1")
        masked0, copied, masked1 = sem("masked0"), sem("copied"), sem("masked1")
        mixed, o_ready, out_ready, added = sem("mixed"), sem("o_ready"), sem("out_ready"), sem("added")
        block = ctx.enter_context(nc.Block())

        def turns(eng, body):
            for w4 in range(4):
                body(w4, w4)
            with eng.Fori(1, B // 4) as i:
                for w4 in range(4):
                    body(4 * i + w4, w4)

        diagonal = causal[:, 0:P].unsqueeze(1).broadcast_to([P, HL, P])

        @block.sync
        def _(sp):
            with sp.Fori(0, B // 4 - 1) as i:
                for w2 in range(2):
                    sp.wait_ge(score1, (2 * i + w2 + 1) * 2 * HG)
                    stack_pair(sp, 2 * i + w2 + 2, qp, kp, q9[w2], k9[w2], packed[w2])

        @block.gpsimd
        def _(pool):
            def turn(n, w4):
                if not isinstance(n, int) or n >= 2:
                    pool.wait_ge(mixed, (n - 1) * HG)
                for g in range(HG):
                    lo = g * HL * HD
                    ins = pool.tensor_copy(vb[w4 % 2][:, :, g, :, HD * g:HD * (g + 1)],
                                           vtok[:, ds(2 * n, 2), lo:lo + HL * HD].rearrange("p t (h d) -> p t h d", h=HL))
                ins.then_inc(v_ready, 1)

            turns(pool, turn)

        @block.tensor
        def _(pe):
            def project_out(n, u):
                pe.wait_ge(o_ready, n + 1)
                pe.matmul(psy[:, 0:S], w["wo"][:, :], oT[u][:, :], start=True, stop=True).then_inc(out_ready, 1)

            def turn(n, w4):
                u = w4 % 2
                q, k = q9[w4 // 2][:, :, u * S:(u + 1) * S], k9[w4 // 2][:, :, u * S:(u + 1) * S]

                def scores(g):
                    c = n * HG + g
                    for out, signal, left, kat, qat in ((ps0, score0, masked0, slice(0, P), slice(0, P)),
                                                        (ps_full, score_full, copied, slice(0, P), slice(P, S)),
                                                        (ps1, score1, masked1, slice(P, S), slice(P, S))):
                        if not isinstance(c, int) or c >= 2:
                            pe.wait_ge(left, c - 1)
                        for h in range(HL):
                            ins = pe.matmul(out[g % 2][:, h, :], k[:, HL * g + h, kat], q[:, HL * g + h, qat],
                                            start=True, stop=True)
                        ins.then_inc(signal, 1)

                def mix(g):
                    c = n * HG + g
                    if g == 0:
                        pe.wait_ge(v_ready, n + 1)
                    pe.wait_ge(masked0, c + 1)
                    pe.wait_ge(copied, c + 1)
                    for h in range(HL):
                        pe.matmul(pso[32 * h:32 * h + 32, u * S:(u + 1) * S], vb[u][:, 0, g, h, :], m0[g % 2][:, h, :],
                                  start=(g == 0), stop=False)
                    pe.wait_ge(masked1, c + 1)
                    for h in range(HL):
                        ins = pe.matmul(pso[32 * h:32 * h + 32, u * S + P:(u + 1) * S], vb[u][:, 1, g, h, :],
                                        m1[g % 2][:, h, :], start=False, stop=(g == HG - 1))
                    ins.then_inc(mixed, 1)

                if u == 0:
                    pe.wait_ge(packed[w4 // 2], (n - w4 + 4) * (PAIR_DMAS * 4))
                scores(0)
                scores(1)
                if not isinstance(n, int) or n > 0:
                    project_out(n - 1, 1 - u)
                mix(0)
                for g in range(2, HG):
                    scores(g)
                    mix(g - 1)
                mix(HG - 1)

            turns(pe, turn)
            project_out(B - 1, 1)

        @block.vector
        def _(dve):
            def add(n):
                dve.wait_ge(out_ready, n + 1)
                at = ds(n * S, S)
                dve.scalar_tensor_tensor(xT[:, at], psy[:, 0:S], w["bo"][:, 0:1], xT[:, at],
                                         ALU.add, ALU.add).then_inc(added, 1)

            def turn(n, w4):
                for g in range(HG):
                    c = n * HG + g
                    dve.wait_ge(score0, c + 1)
                    dve.tensor_tensor(m0[g % 2][:, :, 0:P], ps0[g % 2][:, :, :], diagonal,
                                      ALU.mult).then_inc(masked0, 1)
                    dve.wait_ge(score1, c + 1)
                    dve.tensor_tensor(m1[g % 2][:, :, :], ps1[g % 2][:, :, :], diagonal,
                                      ALU.mult).then_inc(masked1, 1)
                    if g == 1 and (not isinstance(n, int) or n > 0):
                        add(n - 1)

            turns(dve, turn)
            add(B - 1)

        @block.scalar
        def _(act):
            def turn(n, w4):
                u = w4 % 2
                for g in range(HG):
                    c = n * HG + g
                    act.wait_ge(score_full, c + 1)
                    act.activation(m0[g % 2][:, :, P:S], ps_full[g % 2][:, :, :], ACT.Copy).then_inc(copied, 1)
                act.wait_ge(mixed, (n + 1) * HG)
                act.activation(oT[u][:, :], pso[:, u * S:(u + 1) * S], ACT.Copy).then_inc(o_ready, 1)

            turns(act, turn)


def stack_half(sp, e, tiles, queries, keys, stacked):
    for a in range(PARTS):
        for b in range(PARTS):
            r = (a * PARTS + b) * HD
            sp.dma_start(tiles["qx"][e][r:r + HD, :, :], tiles["qp"][64 * e:64 * e + 64, a, queries]).then_inc(stacked, 16)
            sp.dma_start(tiles["kx"][e][r:r + HD, :, :], tiles["kp"][64 * e:64 * e + 64, b, :]).then_inc(stacked, 16)


def cross_start(nc, zT, w, tiles):
    with ExitStack() as ctx:
        sb = lambda name, shape, dt=F32: ctx.enter_context(nc.sbuf_tensor(f"xq_{name}", shape, dt))
        ps = lambda name, shape: ctx.enter_context(nc.psum_tensor(f"xq_{name}", shape, F32))
        sem = lambda name: ctx.enter_context(nc.semaphore(f"xq_{name}"))
        qp, kp, cT, vnext = tiles["qp"], tiles["kp"], tiles["cT"], tiles["vnext"]
        rest = [sb(f"rest{u}", [P, CH]) for u in range(4)]
        psq = [ps(f"psq{u}", [P, CH]) for u in range(4)]
        psv = [ps(f"psv{c}", [P, CH]) for c in range(4)]
        projected, hi_ready, rest_ready = sem("projected"), sem("hi_ready"), sem("rest_ready")
        mid_ready, lo_ready, stacked = sem("mid_ready"), sem("lo_ready"), sem("stacked")
        v_projected, v_copied = sem("v_projected"), sem("v_copied")
        block = ctx.enter_context(nc.Block())

        def groups(eng, body):
            body(0, KCH, kp, lambda u: slice(u * KCH, (u + 1) * KCH))
            with eng.Fori(1, NCH // 4 + 1) as i:
                body(i, CH, qp, lambda u: ds((4 * (i - 1) + u) * CH, CH))

        @block.sync
        def _(sp):
            kx, qx = tiles["kx"][0], tiles["qx"][0]
            for b, ready in enumerate((hi_ready, mid_ready, lo_ready)):
                sp.wait_ge(ready, 4)
                for a in range(PARTS):
                    r = (a * PARTS + b) * HD
                    sp.dma_start(kx[r:r + HD, :, :], kp[0:64, b, :]).then_inc(stacked, 16)
            for a, ready in enumerate((hi_ready, mid_ready, lo_ready)):
                sp.wait_ge(ready, 5)
                for b in range(PARTS):
                    r = (a * PARTS + b) * HD
                    sp.dma_start(qx[r:r + HD, :, :], qp[0:64, a, 0:S]).then_inc(stacked, 16)
            sp.wait_ge(stacked, 2 * COMBOS * 16)

        @block.tensor
        def _(pe):
            for c in range(4):
                pe.matmul(psq[c][:, 0:KCH], w["wk"][:, :], cT[:, c * KCH:(c + 1) * KCH],
                          start=True, stop=True).then_inc(projected, 1)
            with pe.Fori(1, NCH // 4 + 1) as i:
                for u in range(4):
                    pe.wait_ge(rest_ready, 4 * (i - 1) + u + 1)
                    pe.matmul(psq[u][:, :], w["wq"][:, :], zT[:, ds((4 * (i - 1) + u) * CH, CH)],
                              start=True, stop=True).then_inc(projected, 1)
            for c, (a, b) in enumerate(VCH):
                for j in range(a, b):
                    ins = pe.matmul(psv[c][:, (j - a) * P:(j - a + 1) * P], cT[:, j * P:(j + 1) * P],
                                    w["wv"][:, :], start=True, stop=True)
                ins.then_inc(v_projected, 1)

        @block.scalar
        def _(act):
            def group(i, width, parts, at):
                for u in range(4):
                    act.wait_ge(projected, 4 * i + u + 1)
                    act.activation(parts[:, 0, at(u)], psq[u][:, 0:width], ACT.Copy).then_inc(hi_ready, 1)
                for u in range(4):
                    act.wait_ge(rest_ready, 4 * i + u + 1)
                    act.activation(parts[:, 1, at(u)], rest[u][:, 0:width], ACT.Copy).then_inc(mid_ready, 1)

            groups(act, group)
            for c, (a, b) in enumerate(VCH):
                act.wait_ge(v_projected, c + 1)
                act.activation(vnext[:, a:b, :], psv[c][:, 0:(b - a) * P].rearrange("p (t n) -> p t n", n=P),
                               ACT.Copy).then_inc(v_copied, 1)

        @block.vector
        def _(dve):
            def group(i, width, parts, at):
                for u in range(4):
                    dve.wait_ge(hi_ready, 4 * i + u + 1)
                    if not isinstance(i, int):
                        dve.wait_ge(lo_ready, 4 * (i - 1) + u + 1)
                    dve.tensor_tensor(rest[u][:, 0:width], psq[u][:, 0:width], parts[:, 0, at(u)],
                                      ALU.subtract).then_inc(rest_ready, 1)
                for u in range(4):
                    dve.wait_ge(mid_ready, 4 * i + u + 1)
                    dve.tensor_tensor(parts[:, 2, at(u)], rest[u][:, 0:width], parts[:, 1, at(u)],
                                      ALU.subtract).then_inc(lo_ready, 1)

            groups(dve, group)


def cross_attention(nc, xT, w, tiles, context):
    UNITS = HG * ST
    NSTACK = 2 * COMBOS * 16
    K_AT = {9: 0, 16: 1, 22: 2, 29: 3}
    V_AT = {32: 0, 35: 1, 42: 2, 45: 3}
    WO_AT = 3
    NP = 4
    with ExitStack() as ctx:
        sb = lambda name, shape, dt=F32: ctx.enter_context(nc.sbuf_tensor(f"x_{name}", shape, dt))
        ps = lambda name, shape: ctx.enter_context(nc.psum_tensor(f"x_{name}", shape, F32))
        sem = lambda name: ctx.enter_context(nc.semaphore(f"x_{name}"))
        cT, kx, qx, kp, vnext = (tiles[k] for k in ("cT", "kx", "qx", "kp", "vnext"))
        krest = sb("krest", [P, KCH])
        v = tiles["v"]
        probs = [sb(f"probs{r}", [P, HL, S]) for r in range(NP)]
        oT = sb("oT", [P, S])
        pss = [ps(f"pss{r}", [P, HL, S]) for r in range(2)]
        acc = [ps(f"acc{r}", [P, CH]) for r in range(2)]
        psk = ps("psk", [P, CH])
        psv = ps("psv", [P, CH])
        c_landed, stacked = sem("c_landed"), [sem(f"stacked{e}") for e in range(2)]
        k_projected, k_cut, v_projected, v_copied, v_set = (
            sem("k_projected"), sem("k_cut"), sem("v_projected"), sem("v_copied"), sem("v_set"))
        scored, weighed, mixed, o_ready = sem("scored"), sem("weighed"), sem("mixed"), sem("o_ready")
        out_ready, added = sem("out_ready"), sem("added")
        block = ctx.enter_context(nc.Block())

        def turns(eng, body):
            body(0, 0)
            with eng.Fori(0, B // 2 - 1) as i:
                body(2 * i + 1, 1)
                body(2 * i + 2, 0)
            body(B - 1, 1, last=True)

        @block.sync
        def _(sp):
            def load(n):
                sp.dma_start(cT[:, :], context[ds(n, 1), :, :].rearrange("a p s -> (a p) s")).then_inc(c_landed, 16)

            def stack(n, e):
                stack_half(sp, e, tiles, ds(n * S, S), slice(0, CTXP), stacked[e])

            def turn(n, par, last=False):
                if not (isinstance(n, int) and n == 0):
                    sp.wait_ge(scored, n * UNITS)
                stack(n, 1)
                if not last:
                    sp.wait_ge(k_cut, (n + 1) * 4 * HG)
                    stack(n + 1, 0)
                    if not (isinstance(n, int) and n == B - 2):
                        sp.wait_ge(v_projected, (n + 1) * HG)
                        load(n + 2)

            load(1)
            turn(0, 0)
            with sp.Fori(1, B - 2) as i:
                turn(i, None)
            turn(B - 2, 0)
            turn(B - 1, 1, last=True)

        @block.tensor
        def _(pe):
            def project_keys(m, c):
                pe.wait_ge(c_landed, m * 16)
                if not (isinstance(m, int) and m == 1 and c == 0):
                    pe.wait_ge(k_cut, ((m - 1) * HG + c) * 4 - 2)
                pe.matmul(psk[:, 0:KCH], w["wk"][:, :], cT[:, c * KCH:(c + 1) * KCH],
                          start=True, stop=True).then_inc(k_projected, 1)

            def project_values(m, c):
                if not (isinstance(m, int) and m == 1 and c == 0):
                    pe.wait_ge(v_copied, (m - 1) * HG + c)
                if c == 0 and not (isinstance(m, int) and m < 2):
                    pe.wait_ge(added, m - 1)
                for j in range(*VCH[c]):
                    ins = pe.matmul(psv[:, (j - VCH[c][0]) * P:(j - VCH[c][0] + 1) * P], cT[:, j * P:(j + 1) * P],
                                    w["wv"][:, :], start=True, stop=True)
                ins.then_inc(v_projected, 1)

            def score(n, u):
                g, j = u // ST, u % ST
                if u % (UNITS // 2) == 0:
                    wanted = (n + g // 2) * NSTACK
                    if not (isinstance(n, int) and n == 0 and g == 0):
                        pe.wait_ge(stacked[g // 2], wanted)
                if not (isinstance(n, int) and n == 0 and u < 2):
                    pe.wait_ge(weighed, n * UNITS + u - 1)
                for h in range(HL):
                    hh = (g % 2) * HL + h
                    ins = pe.matmul(pss[u % 2][:, h, :], kx[g // 2][:, hh, j * P:(j + 1) * P], qx[g // 2][:, hh, :],
                                    start=True, stop=True)
                ins.then_inc(scored, 1)

            def mix(n, par, u):
                g, j = u // ST, u % ST
                if j == 0:
                    pe.wait_ge(v_set, n * HG + g + 1)
                if u == 0 and not (isinstance(n, int) and n < 2):
                    pe.wait_ge(o_ready, n - 1)
                pe.wait_ge(weighed, n * UNITS + u + 1)
                for h in range(HL):
                    ins = pe.matmul(acc[par][32 * h:32 * h + 32, 0:S], v[:, j, g, h, :],
                                    probs[u % NP][:, h, :], start=(u == 0), stop=(u == UNITS - 1))
                ins.then_inc(mixed, 1)

            def project_out(n):
                pe.wait_ge(o_ready, n + 1)
                pe.matmul(psv[:, 0:S], w["wo"][:, :], oT[:, :], start=True, stop=True).then_inc(out_ready, 1)

            def turn(n, par, last=False):
                first = isinstance(n, int) and n == 0
                for u in range(UNITS):
                    if u + 2 < UNITS:
                        score(n, u + 2)
                    elif not last:
                        score(n + 1, u + 2 - UNITS)
                    mix(n, par, u)
                    if u == WO_AT and not first:
                        project_out(n - 1)
                    if u in K_AT and not last:
                        project_keys(n + 1, K_AT[u])
                    if u in V_AT and not last:
                        project_values(n + 1, V_AT[u])

            score(0, 0)
            score(0, 1)
            turns(pe, turn)
            project_out(B - 1)

        @block.scalar
        def _(act):
            def turn(n, par, last=False):
                for u in range(UNITS):
                    act.wait_ge(scored, n * UNITS + u + 1)
                    if not (isinstance(n, int) and n == 0 and u < NP):
                        act.wait_ge(mixed, n * UNITS + u - NP + 1)
                    act.activation(probs[u % NP][:, :, :], pss[u % 2][:, :, :], ACT.Sigmoid,
                                   scale=HD ** -0.5).then_inc(weighed, 1)

            turns(act, turn)

        @block.vector
        def _(dve):
            def cut_keys(m, c):
                at = slice(c * KCH, (c + 1) * KCH)
                done = ((m - 1) * HG + c) * 4
                dve.wait_ge(k_projected, (m - 1) * HG + c + 1)
                dve.tensor_copy(kp[:, 0, at], psk[:, 0:KCH]).then_inc(k_cut, 1)
                dve.wait_ge(k_cut, done + 1)
                dve.tensor_tensor(krest[:, :], psk[:, 0:KCH], kp[:, 0, at], ALU.subtract).then_inc(k_cut, 1)
                dve.wait_ge(k_cut, done + 2)
                dve.tensor_copy(kp[:, 1, at], krest[:, :]).then_inc(k_cut, 1)
                dve.wait_ge(k_cut, done + 3)
                dve.tensor_tensor(kp[:, 2, at], krest[:, :], kp[:, 1, at], ALU.subtract).then_inc(k_cut, 1)

            def copy_values(m, c):
                a, b = VCH[c]
                dve.wait_ge(v_projected, (m - 1) * HG + c + 1)
                dve.tensor_copy(vnext[:, a:b, :],
                                psv[:, 0:(b - a) * P].rearrange("p (t n) -> p t n", n=P)).then_inc(v_copied, 1)

            def set_values(n, g):
                if not (isinstance(n, int) and n == 0):
                    dve.wait_ge(v_copied, n * HG)
                    dve.wait_ge(mixed, (n - 1) * UNITS + (g + 1) * ST)
                lo = g * HL * HD
                dve.tensor_copy(v[:, :, g, :, HD * g:HD * (g + 1)],
                                vnext[:, :, lo:lo + HL * HD].rearrange("p j (h d) -> p j h d", h=HL)).then_inc(v_set, 1)

            def take_out(n, par):
                dve.wait_ge(mixed, (n + 1) * UNITS)
                dve.tensor_copy(oT[:, :], acc[par][:, 0:S]).then_inc(o_ready, 1)

            def add(n):
                dve.wait_ge(out_ready, n + 1)
                at = ds(n * S, S)
                dve.tensor_tensor(xT[:, at], psv[:, 0:S], xT[:, at], ALU.add).then_inc(added, 1)

            def turn(n, par, last=False):
                first = isinstance(n, int) and n == 0
                if not first:
                    take_out(n - 1, 1 - par)
                for g in range(1, HG):
                    set_values(n, g)
                if not first:
                    add(n - 1)
                if not last:
                    dve.wait_ge(stacked[1], (n + 1) * NSTACK)
                    cut_keys(n + 1, 0)
                if not last:
                    cut_keys(n + 1, 1)
                    cut_keys(n + 1, 2)
                if not last:
                    cut_keys(n + 1, 3)
                    copy_values(n + 1, 0)
                    copy_values(n + 1, 1)
                if not last:
                    copy_values(n + 1, 2)
                    copy_values(n + 1, 3)
                    set_values(n + 1, 0)

            set_values(0, 0)
            turns(dve, turn)
            take_out(B - 1, 1)
            add(B - 1)


def local_attention(nc, tag, zT, w, cleared):
    NSU = 6
    UNIT = [(0, (0, 1, 2, 3)), (0, (4, 5, 6, 7)), (1, (0, 1)), (1, (2, 3)), (1, (4, 5)), (1, (6, 7))]
    KEYS = [(0, P), (WINDOW, S)]
    NEWTON = 12
    QK = 2 * FH
    with ExitStack() as ctx:
        sb = lambda name, shape, dt=F32: ctx.enter_context(nc.sbuf_tensor(f"{tag}_{name}", shape, dt))
        ps = lambda name, shape: ctx.enter_context(nc.psum_tensor(f"{tag}_{name}", shape, F32))
        sem = lambda name: ctx.enter_context(nc.semaphore(f"{tag}_{name}"))
        hs, qz, prob = cleared
        tabA, tabB = sb("tabA", [P, 2, 2, FD]), sb("tabB", [P, 2, 2, FD])
        square = sb("square", [P, QK, FD])
        direct = [[sb(f"direct{u}{t}", [P, QK, FD]) for t in range(2)] for u in range(2)]
        raw = [sb(f"raw{t}", [P, QK, FD]) for t in range(2)]
        turned_half = [sb(f"turned_half{t}", [P, QK, FD]) for t in range(2)]
        sumsq, inv_norm = sb("sumsq", [P, 2, QK]), [sb(f"inv_norm{u}", [P, 2, QK]) for u in range(2)]
        tmp_a, tmp_b = sb("tmp_a", [P, 2, QK]), sb("tmp_b", [P, 2, QK])
        kT = [sb(f"kT{u}", [P, FH // 2, S]) for u in range(2)]
        vt = [sb(f"vt{u}", [P, 2, INNER]) for u in range(2)]
        sim = [sb(f"sim{r}", [P, CH]) for r in range(2)]
        probT = [sb(f"probT{r}", [P, CH]) for r in range(2)]
        top, neg_top = [sb(f"top{r}", [P, 4]) for r in range(2)], [sb(f"neg_top{r}", [P, 4]) for r in range(2)]
        total, inv_total = [sb(f"total{r}", [P, 4]) for r in range(2)], [sb(f"inv_total{r}", [P, 4]) for r in range(2)]
        oT = sb("oT", [P, FH // 2, S])
        beat = sb("beat", [P, 1])
        psqk = ps("psqk", [P, QK, FD])
        psvy = ps("psvy", [P, CH])
        pst = ps("pst", [P, CH])
        pss = [ps(f"pss{r}", [P, CH]) for r in range(2)]
        pso = ps("pso", [P, FH // 2, S])
        ready, shifted, qk_projected, squared = sem("ready"), sem("shifted"), sem("qk_projected"), sem("squared")
        v_projected, v_ready, summed, raw_ready = sem("v_projected"), sem("v_ready"), sem("summed"), sem("raw_ready")
        straight, halved = sem("straight"), sem("halved")
        joined, newton, scaled = sem("joined"), sem("newton"), [sem(f"scaled{t}") for t in range(2)]
        flipped, placed, scored, masked = sem("flipped"), sem("placed"), sem("scored"), sem("masked")
        negated, exped, inverted, normed = sem("negated"), sem("exped"), sem("inverted"), sem("normed")
        turned, copied, valued, o_ready = sem("turned"), sem("copied"), sem("valued"), sem("o_ready")
        placed_k, out_ready, added = sem("placed_k"), sem("out_ready"), sem("added")
        block = ctx.enter_context(nc.Block())

        def exists(n):
            return not isinstance(n, int) or 0 <= n < B

        def at_least(eng, sem, value):
            if not isinstance(value, int) or value > 0:
                eng.wait_ge(sem, value)

        def turns(eng, body):
            for n in range(-2, 2):
                body(n, n % 2)
            with eng.Fori(1, B // 2 - 1) as i:
                for u in range(2):
                    body(2 * i + u, u)
            for n in range(B - 2, B + 1):
                body(n, n % 2)

        def ahead(n, u, s, by):
            over, s = divmod(s + by, NSU)
            return n + over, (u + over) % 2, s

        def keys_of(s):
            lo, hi = KEYS[UNIT[s][0]]
            return len(UNIT[s][1]), lo, hi

        def scores_of(tile, s):
            nh, lo, hi = keys_of(s)
            return tile[:, 0:nh * (hi - lo)].rearrange("p (h k) -> p h k", h=nh)

        def probs_of(s):
            nh, lo, hi = keys_of(s)
            return prob[s][:, :].rearrange("p (h k) -> p h k", h=nh)[:, :, lo:hi]

        def heads(ap):
            return ap.rearrange("p (m h) d -> p m h d", m=2)

        def table(tab, t, lo, hi):
            return tab[:, t, :, lo:hi].unsqueeze(2).broadcast_to([P, 2, FH, hi - lo])

        @block.gpsimd
        def _(pool):
            def turn_halves(n, t):
                if exists(n):
                    pool.wait_ge(raw_ready, 2 * n + t + 1)
                    for lo, frm in ((0, FD // 2), (FD // 2, 0)):
                        pool.tensor_tensor(heads(turned_half[t][:, :, lo:lo + FD // 2]),
                                           heads(raw[t][:, :, frm:frm + FD // 2]),
                                           table(tabB, t, lo, lo + FD // 2), ALU.mult).then_inc(halved, 1)

            def join(n, u, t):
                if exists(n):
                    pool.wait_ge(halved, (2 * n + t) * 2 + 2)
                    pool.wait_ge(straight, 2 * n + t + 1)
                    pool.tensor_tensor(direct[u][t][:, :, :], direct[u][t][:, :, :], turned_half[t][:, :, :],
                                       ALU.add).then_inc(joined, 1)

            def scale_keys(n, u, t):
                if exists(n):
                    pool.wait_ge(newton, (n + 1) * NEWTON)
                    pool.wait_ge(joined, 2 * n + t + 1)
                    pool.tensor_tensor(direct[u][t][:, FH:QK, :], direct[u][t][:, FH:QK, :],
                                       inv_norm[u][:, t, FH:QK].unsqueeze(2).broadcast_to([P, FH, FD]),
                                       ALU.mult).then_inc(scaled[t], 1)

            def turn(n, u):
                for s in range(NSU):
                    if s == 3:
                        turn_halves(n + 2, 0)
                        join(n + 2, u, 0)
                        turn_halves(n + 2, 1)
                    if s == 4:
                        join(n + 2, u, 1)
                        scale_keys(n + 2, u, 0)
                        scale_keys(n + 2, u, 1)

            pool.wait_ge(ready, 2)
            turns(pool, turn)

        @block.tensor
        def _(pe):
            def project_qk(n, u, t):
                if exists(n):
                    if t == 0:
                        pe.wait_ge(shifted, 2 * n + 2)
                        at_least(pe, placed, 4 * n)
                        at_least(pe, placed_k, 2 * n)
                    else:
                        pe.wait_ge(raw_ready, 2 * n + 1)
                    for m in range(2):
                        ins = pe.matmul(psqk[:, m * FH:(m + 1) * FH, :], hs[u][:, t * P:(t + 1) * P],
                                        w["wqkv"][:, m * INNER:(m + 1) * INNER], start=True, stop=True)
                    ins.then_inc(qk_projected, 1)

            def project_v(n, u, t):
                if exists(n):
                    if t == 0:
                        at_least(pe, added, n - 1)
                    else:
                        pe.wait_ge(v_ready, 2 * n + 1)
                    pe.matmul(psvy[:, :], hs[u][:, t * P:(t + 1) * P], w["wqkv"][:, 2 * INNER:3 * INNER],
                              start=True, stop=True).then_inc(v_projected, 1)

            def flip(n, u, t):
                if exists(n):
                    pe.wait_ge(scaled[t], n + 1)
                    if t == 1:
                        pe.wait_ge(placed, 4 * n + 2)
                        pe.wait_ge(placed_k, 2 * n + 1)
                    for p in range(FH):
                        ins = pe.transpose(psqk[:, 2 * p:2 * p + 2, :].rearrange("p h d -> p (h d)"),
                                           direct[u][t][:, 2 * p:2 * p + 2, :].rearrange("p h d -> p (h d)"),
                                           w["identity"][:, :])
                    ins.then_inc(flipped, 1)

            def score(n, u, s):
                if exists(n):
                    blk, heads = UNIT[s]
                    nh, lo, hi = keys_of(s)
                    if s == 0:
                        pe.wait_ge(placed, 4 * n + 4)
                        pe.wait_ge(placed_k, 2 * n + 2)
                    at_least(pe, masked, n * NSU + s - 1)
                    for m, h in enumerate(heads):
                        ins = pe.matmul(scores_of(pss[s % 2], s)[:, m, :], qz[u][:, h, blk * P:(blk + 1) * P],
                                        kT[u][:, h // 2, lo:hi], start=True, stop=True)
                    ins.then_inc(scored, 1)

            def turn_over(n, u, s):
                if exists(n):
                    pe.wait_ge(normed, n * NSU + s + 1)
                    at_least(pe, copied, n * NSU + s)
                    for m in range(CH // P):
                        ins = pe.transpose(pst[:, m * P:(m + 1) * P], prob[s][:, m * P:(m + 1) * P], w["identity"][:, :])
                    ins.then_inc(turned, 1)

            def value(n, u, s):
                if exists(n):
                    blk, heads = UNIT[s]
                    pe.wait_ge(copied, n * NSU + s + 1)
                    if s == 0:
                        pe.wait_ge(v_ready, 2 * n + 2)
                    if s < 2:
                        at_least(pe, o_ready, 2 * n - 1 + s)
                    for m, h in enumerate(heads):
                        for j in range(blk + 1):
                            at = (m * (blk + 1) + j) * P
                            ins = pe.matmul(pso[64 * (h % 2):64 * (h % 2) + 64, h // 2, blk * P:(blk + 1) * P],
                                            vt[u][:, j, h * FD:(h + 1) * FD], probT[s % 2][:, at:at + P],
                                            start=(j == 0), stop=(j == blk))
                    ins.then_inc(valued, 1)

            def project_out(n):
                if exists(n):
                    pe.wait_ge(o_ready, 2 * n + 2)
                    pe.wait_ge(v_ready, 2 * n + 4 if exists(n + 1) else 2 * B)
                    for p in range(FH // 2):
                        ins = pe.matmul(psvy[:, 0:S], w["wo"][:, p, :], oT[:, p, :], start=(p == 0), stop=(p == FH // 2 - 1))
                    ins.then_inc(out_ready, 1)

            def turn(n, u):
                for s in range(NSU):
                    if s == 3:
                        project_out(n - 1)
                    if s == 5:
                        project_v(n + 1, 1 - u, 0)
                    score(*ahead(n, u, s, 3))
                    turn_over(*ahead(n, u, s, -1))
                    if s == 3:
                        project_qk(n + 2, u, 1)
                    value(*ahead(n, u, s, -2))
                    if s == 0:
                        flip(n + 1, 1 - u, 0)
                    if s == 1:
                        flip(n + 1, 1 - u, 1)
                    if s == 2:
                        project_qk(n + 2, u, 0)
                    if s == 5:
                        project_v(n + 1, 1 - u, 1)

            turns(pe, turn)

        @block.vector
        def _(dve):
            def shift(n, u):
                if exists(n):
                    at_least(dve, v_projected, 2 * n - 2)
                    dve.tensor_copy(hs[u][0:64, :], zT[0:64, ds(n * S, S)]).then_inc(shifted, 1)
                    dve.tensor_copy(hs[u][64:P, 1:S], zT[64:P, ds(n * S, S - 1)]).then_inc(shifted, 1)

            def place_keys(n, u, t):
                if exists(n):
                    dve.wait_ge(flipped, 2 * n + t + 1)
                    dve.tensor_copy(kT[u][:, :, t * P:(t + 1) * P],
                                    psqk[:, FH:QK, :].rearrange("p (h e) d -> p h (e d)", e=2)).then_inc(placed_k, 1)

            def sums(n, t):
                if exists(n):
                    dve.wait_ge(squared, 2 * n + t + 1)
                    dve.tensor_reduce(sumsq[:, t, :], square[:, :, :], AX.X, ALU.add).then_inc(summed, 1)

            def straight_part(n, u, t):
                if exists(n):
                    dve.wait_ge(raw_ready, 2 * n + t + 1)
                    dve.tensor_tensor(heads(direct[u][t][:, :, :]), heads(raw[t][:, :, :]), table(tabA, t, 0, FD),
                                      ALU.mult).then_inc(straight, 1)

            def inverse_norms(n, u, k):
                if not exists(n):
                    return
                own = Own(dve, newton, NEWTON)
                own.turn(n)
                own.n = 3 * k
                flat = lambda x: x[:, :, :].rearrange("p t h -> p (t h)")
                x, y, a, b = flat(sumsq), flat(inv_norm[u]), flat(tmp_a), flat(tmp_b)
                if k == 0:
                    dve.wait_ge(summed, 2 * n + 2)
                    own.step(dve.tensor_scalar(x, x, 1e-24, None, ALU.max))
                    own.wait()
                    own.step(dve.tensor_scalar(a.bitcast(I32), x.bitcast(I32), 1, None, ALU.logical_shift_right))
                    own.wait()
                    own.step(dve.tensor_scalar(y.bitcast(I32), a.bitcast(I32), -1.0, float(0x5f3759df), ALU.mult, ALU.add))
                else:
                    own.wait()
                    own.step(dve.scalar_tensor_tensor(a, y, -0.5, x, ALU.mult, ALU.mult))
                    own.wait()
                    own.step(dve.tensor_tensor(b, a, y, ALU.mult))
                    own.wait()
                    own.step(dve.scalar_tensor_tensor(y, b, 1.5, y, ALU.add, ALU.mult))

            def mask(n, u, s):
                if not exists(n):
                    return
                blk, heads = UNIT[s]
                nh, lo, hi = keys_of(s)
                r, c = s % 2, n * NSU + s
                dve.wait_ge(scored, c + 1)
                dve.memset(beat[:, :], 0.0)
                for m in range(nh):
                    ins = dve.tensor_tensor_reduce(out=scores_of(sim[r], s)[:, m, :], in0=scores_of(pss[r], s)[:, m, :],
                                                   in1=w["window"][:, blk, lo:hi], scale=1.0, scalar=NEG, op0=ALU.add,
                                                   op1=ALU.max, accum_out=top[r][:, m:m + 1])
                ins.then_inc(masked, 1)
                dve.wait_ge(masked, c + 1)
                dve.scalar_tensor_tensor(neg_top[r][:, 0:nh], top[r][:, 0:nh], -1.0,
                                         inv_norm[u][:, blk, heads[0]:heads[0] + nh], ALU.mult, ALU.mult).then_inc(negated, 1)

            def invert(n, u, s):
                if exists(n):
                    r, c, nh = s % 2, n * NSU + s, len(UNIT[s][1])
                    dve.wait_ge(exped, c + 1)
                    dve.reciprocal(inv_total[r][:, 0:nh], total[r][:, 0:nh]).then_inc(inverted, 1)

            def norm(n, u, s):
                if exists(n):
                    nh, lo, hi = keys_of(s)
                    dve.wait_ge(inverted, n * NSU + s + 1)
                    dve.tensor_tensor(probs_of(s), probs_of(s),
                                       inv_total[s % 2][:, 0:nh].unsqueeze(2).broadcast_to([P, nh, hi - lo]),
                                       ALU.mult).then_inc(normed, 1)

            def add(n):
                if exists(n):
                    dve.wait_ge(out_ready, n + 1)
                    at = ds(n * S, S)
                    dve.tensor_tensor(zT[:, at], psvy[:, 0:S], zT[:, at], ALU.add).then_inc(added, 1)

            def turn(n, u):
                for s in range(NSU):
                    if s == 4:
                        sums(n + 2, 0)
                    if s == 5:
                        sums(n + 2, 1)
                    invert(*ahead(n, u, s, 0))
                    if s == 5:
                        inverse_norms(n + 2, u, 0)
                    norm(*ahead(n, u, s, 0))
                    if s == 0:
                        shift(n + 2, u)
                    mask(*ahead(n, u, s, 2))
                    if s == 0:
                        place_keys(n + 1, 1 - u, 0)
                    if s == 1:
                        place_keys(n + 1, 1 - u, 1)
                    if s == 3:
                        straight_part(n + 2, u, 0)
                        add(n - 1)
                    if s == 4:
                        straight_part(n + 2, u, 1)
                    if s == 5:
                        inverse_norms(n + 2, u, 1)
                        inverse_norms(n + 2, u, 2)
                        inverse_norms(n + 2, u, 3)

            for tab, const, scales in ((tabA, "cosine", "scales"), (tabB, "sine", "scales_turned")):
                dve.tensor_tensor(tab[:, :, :, :].rearrange("p t m d -> p t (m d)"),
                                  w[const][:, :, :, :].rearrange("p t m d -> p t (m d)"),
                                  w[scales][:, :, :].rearrange("p m d -> p (m d)").unsqueeze(1).broadcast_to([P, 2, 2 * FD]),
                                  ALU.mult).then_inc(ready, 1)
            dve.wait_ge(ready, 2)
            turns(dve, turn)

        @block.scalar
        def _(act):
            def copy_qk(n, t):
                if exists(n):
                    act.wait_ge(qk_projected, 2 * n + t + 1)
                    at_least(act, joined, 2 * n + t - 1)
                    act.activation(raw[t][:, :, :], psqk[:, :, :], ACT.Copy).then_inc(raw_ready, 1)

            def squares(n, t):
                if exists(n):
                    act.wait_ge(raw_ready, 2 * n + t + 1)
                    at_least(act, summed, 2 * n + t)
                    act.activation(square[:, :, :], raw[t][:, :, :], ACT.Square).then_inc(squared, 1)

            def copy_v(n, u, t):
                if exists(n):
                    act.wait_ge(v_projected, 2 * n + t + 1)
                    act.activation(vt[u][:, t, :], psvy[:, :], ACT.Copy).then_inc(v_ready, 1)

            def place(n, u, t):
                if not exists(n):
                    return
                act.wait_ge(flipped, 2 * n + t + 1)
                q = psqk[:, 0:FH, :].rearrange("p (h e) d -> p h (e d)", e=2)
                at = slice(t * P, (t + 1) * P)
                for e in range(2):
                    rows = slice(64 * e, 64 * e + 64)
                    act.activation(qz[u][rows, e:FH:2, at], q[rows, :, :], ACT.Copy).then_inc(placed, 1)

            def copy_out(n, b):
                if exists(n):
                    act.wait_ge(valued, n * NSU + (4, 6)[b])
                    at_least(act, out_ready, n)
                    act.activation(oT[:, 2 * b:2 * b + 2, :], pso[:, 2 * b:2 * b + 2, :], ACT.Copy).then_inc(o_ready, 1)

            def exps(n, u, s):
                if not exists(n):
                    return
                (blk, heads), r = UNIT[s], s % 2
                act.wait_ge(negated, n * NSU + s + 1)
                for m, h in enumerate(heads):
                    ins = act.activation(probs_of(s)[:, m, :], scores_of(sim[r], s)[:, m, :], ACT.Exp,
                                         bias=neg_top[r][:, m:m + 1], scale=inv_norm[u][:, blk, h:h + 1],
                                         accum_out=total[r][:, m:m + 1])
                ins.then_inc(exped, 1)

            def copy(n, u, s):
                if exists(n):
                    act.wait_ge(turned, n * NSU + s + 1)
                    act.activation(probT[s % 2][:, :], pst[:, :], ACT.Copy).then_inc(copied, 1)

            def turn(n, u):
                for s in range(NSU):
                    if s == 1:
                        place(n + 1, 1 - u, 0)
                    exps(*ahead(n, u, s, 1))
                    if s == 4:
                        copy_qk(n + 2, 1)
                        squares(n + 2, 1)
                    if s == 5:
                        copy_v(n + 1, 1 - u, 0)
                    copy(*ahead(n, u, s, -1))
                    if s == 1:
                        place(n + 1, 1 - u, 1)
                        copy_out(n - 1, 1)
                    if s == 2:
                        copy_qk(n + 2, 0)
                        squares(n + 2, 0)
                    if s == 5:
                        copy_out(n, 0)
                        copy_v(n + 1, 1 - u, 1)

            turns(act, turn)


def gated_unit(nc, tag, zT, hs, w, xT=None, out=None):
    with ExitStack() as ctx:
        sb = lambda name, shape, dt=F32: ctx.enter_context(nc.sbuf_tensor(f"{tag}_{name}", shape, dt))
        ps = lambda name, shape: ctx.enter_context(nc.psum_tensor(f"{tag}_{name}", shape, F32))
        sem = lambda name: ctx.enter_context(nc.semaphore(f"{tag}_{name}"))
        psa = [ps(f"psa{c}", [P, CH]) for c in range(HC)]
        psg = [ps(f"psg{c}", [P, CH]) for c in range(HC)]
        psy = ps("psy", [P, CH])
        gelu = [sb(f"gelu{c}", [P, CH]) for c in range(HC)]
        gated = [[sb(f"gated{u}{c}", [P, CH]) for c in range(HC)] for u in range(2)]
        affine, up, gelu_ready, gate_ready = sem("affine"), sem("up"), sem("gelu_ready"), sem("gate_ready")
        down, added = sem("down"), sem("added")
        summed, stored = (sem("summed"), sem("stored")) if out is not None else (None, None)
        block = ctx.enter_context(nc.Block())

        if out is not None:
            @block.sync
            def _(sp):
                for n in range(NCH):
                    sp.wait_ge(summed, n + 1)
                    sp.dma_start(out[:, n * CH:(n + 1) * CH], xT[:, n * CH:(n + 1) * CH]).then_inc(stored, 16)
                sp.wait_ge(stored, 16 * NCH)

        def chunks(eng, body):
            body(0, 0)
            with eng.Fori(0, NCH // 2 - 1) as i:
                for u in range(2):
                    body(2 * i + 1 + u, 1 - u)
            body(NCH - 1, 1)

        @block.tensor
        def _(pe):
            def widen(n, c):
                if c == 0:
                    pe.wait_ge(affine, n + 1)
                if not isinstance(n, int) or n > 0:
                    pe.wait_ge(gate_ready, HC * (n - 1) + c + 1)
                for m, out in ((HC + c, psg[c]), (c, psa[c])):
                    ins = pe.matmul(out[:, :], w["w1"][:, m * P:(m + 1) * P], hs[:, ds(n * CH, CH)],
                                    start=True, stop=True)
                ins.then_inc(up, 1)

            def narrow(n, u):
                pe.wait_ge(gate_ready, HC * (n + 1))
                if not isinstance(n, int) or n > 0:
                    pe.wait_ge(added, n)
                for c in range(HC):
                    ins = pe.matmul(psy[:, :], w["w2"][:, c, :], gated[u][c][:, :], start=(c == 0), stop=(c == HC - 1))
                ins.then_inc(down, 1)

            def chunk(n, u):
                widen(n, 0)
                if not isinstance(n, int) or n > 0:
                    narrow(n - 1, 1 - u)
                widen(n, 1)
                widen(n, 2)

            assert HC == 3
            chunks(pe, chunk)
            narrow(NCH - 1, 1)

        @block.scalar
        def _(act):
            with act.Fori(0, NCH) as n:
                for c in range(HC):
                    act.wait_ge(up, HC * n + c + 1)
                    act.activation(gelu[c][:, :], psg[c][:, :], ACT.Gelu,
                                   bias=w["b1"][:, HC + c:HC + c + 1]).then_inc(gelu_ready, 1)

        @block.vector
        def _(dve):
            def add(n):
                dve.wait_ge(down, n + 1)
                at = ds(n * CH, CH)
                dve.scalar_tensor_tensor(zT[:, at], psy[:, :], w["b2"][:, 0:1], zT[:, at],
                                         ALU.add, ALU.add).then_inc(added, 1)
                if out is not None:
                    dve.wait_ge(added, n + 1)
                    dve.tensor_tensor(xT[:, at], xT[:, at], zT[:, at], ALU.add).then_inc(summed, 1)

            def shift_by_bias(n):
                at = ds(n * CH, CH)
                dve.tensor_scalar(hs[:, at], hs[:, at], w["ln_b"][:, 0:1], None, ALU.add).then_inc(affine, 1)

            def chunk(n, u):
                for c in range(HC):
                    dve.wait_ge(gelu_ready, HC * n + c + 1)
                    dve.scalar_tensor_tensor(gated[u][c][:, :], psa[c][:, :], w["b1"][:, c:c + 1], gelu[c][:, :],
                                             ALU.add, ALU.mult).then_inc(gate_ready, 1)
                    if c == 0 and (not isinstance(n, int) or n > 0):
                        add(n - 1)
                    if c == 1 and (not isinstance(n, int) or n < NCH - 1):
                        shift_by_bias(n + 1)

            shift_by_bias(0)
            chunks(dve, chunk)
            add(NCH - 1)


def build(nc, a, out):
    with ExitStack() as ctx:
        sb = lambda name, shape, dt=F32: ctx.enter_context(nc.sbuf_tensor(name, shape, dt))
        xT = sb("xT", [P, T])
        zT = sb("zT", [P, T])
        ones_mean = sb("ones_mean", [P, P])
        eps = sb("eps", [P, 1])
        pick = sb("pick", [P, P])
        norms = {"ones_mean": ones_mean, "eps": eps, "pick": pick, "runs": 0, "sems": [
            ctx.enter_context(nc.semaphore(f"norm_{n}")) for n in (
                "mean_ready", "centered", "square_ready", "var_ready", "log_ready", "guess_ready", "newton",
                "spread", "normed")]}
        made = ctx.enter_context(nc.semaphore("made"))
        with nc.Block() as block:
            @block.vector
            def _(dve):
                dve.memset(pick[:, :], 0.0).then_inc(made, 1)
                dve.wait_ge(made, 1)
                for c in range(4):
                    dve.memset(pick[32 * c:32 * c + 1, :], 1.0).then_inc(made, 1)
                dve.memset(ones_mean[:, :], 1.0 / D)
                dve.memset(eps[:, :], 1e-5).then_inc(made, 1)
                dve.wait_ge(made, 6)
        with ExitStack() as c1:
            w, loads = tiles_for(nc, c1, "w1", {
                "wq": (a["r_wq"], [P, D]), "wk": (a["r_wk"], [P, D]), "wn": (a["r_wn"], [P, D]),
                "wv": (a["r_wv"], [P, D]), "bq": (a["r_bq"], [P, 1]), "bk": (a["r_bk"], [P, 1]),
                "bn": (a["r_bn"], [P, 1]), "bv": (a["r_bv"], [P, D]), "wo": (a["r_wo"], [P, D]),
                "bo": (a["r_bo"], [P, 1]), "causal": (a["causal"], [P, S])})
            s1 = lambda name, shape, dt=F32: c1.enter_context(nc.sbuf_tensor(name, shape, dt))
            q9, k9 = ([s1(f"{x}9{m}", [P, H, 2 * S], BF16) for m in range(2)] for x in "qk")
            vb = [s1(f"vb{u}", [P, 2, HG, HL, 32]) for u in range(2)]
            layer_norm(nc, "n1", norms, xT, zT, loads,
                       [x[64:P, :, :].bitcast(F32) for x in (*q9, *k9)] + [x[:, :, :, :, :] for x in vb],
                       source=a["x"])
            qp, kp = s1("qp", [P, PARTS, T], BF16), s1("kp", [P, PARTS, T], BF16)
            vtok = s1("vtok", [P, T // P, D])
            packed = [c1.enter_context(nc.semaphore(f"packed{m}")) for m in range(2)]
            retention_project(nc, zT, w, qp, kp, vtok, q9, k9, packed)
            retention(nc, xT, w, qp, kp, vtok, w["causal"], q9, k9, vb, packed)
        with ExitStack() as c2:
            w, loads = tiles_for(nc, c2, "w2", {
                "wq": (a["x_wq"], [P, D]), "wk": (a["x_wk"], [P, D]), "wv": (a["x_wv"], [P, D]),
                "wo": (a["x_wo"], [P, D])})
            s2 = lambda name, shape, dt=F32: c2.enter_context(nc.sbuf_tensor(f"x_{name}", shape, dt))
            tiles = {"cT": s2("cT", [P, CTXP]), "qp": s2("qp", [P, PARTS, T], BF16),
                     "kp": s2("kp", [P, PARTS, CTXP], BF16), "vnext": s2("vnext", [P, ST, D]),
                     "v": s2("v", [P, ST, HG, HL, 32]),
                     "kx": [s2(f"kx{e}", [P, H // 2, CTXP], BF16) for e in range(2)],
                     "qx": [s2(f"qx{e}", [P, H // 2, S], BF16) for e in range(2)]}
            loads.append((tiles["cT"][:, :], a["context"][0, :, :]))
            layer_norm(nc, "n2", norms, xT, zT, loads,
                       [x[64:P, :, :].bitcast(F32) for x in (*tiles["qx"], *tiles["kx"])]
                       + [tiles["v"][:, :, :, :, :]])
            cross_start(nc, zT, w, tiles)
            cross_attention(nc, xT, w, tiles, a["context"])
        with ExitStack() as c3:
            ws, loads = [], []
            for l in range(DEPTH):
                w, more = tiles_for(nc, c3, f"w3{l}", {
                    "wqkv": (a["f_wqkv"][l], [P, 3 * INNER]), "wo": (a["f_wo"][l], [P, FH // 2, D]),
                    "cosine": (a["cosine"], [P, 2, 2, FD]), "sine": (a["sine"], [P, 2, 2, FD]),
                    "scales": (a["f_scales"][l], [P, 2, FD]), "scales_turned": (a["f_scales_turned"][l], [P, 2, FD]),
                    "window": (a["window"], [P, 2, S]), "identity": (a["identity"], [P, P]),
                    "ln_g": (a["f_ln_g"][l], [P, 1]), "ln_b": (a["f_ln_b"][l], [P, 1]),
                    "w1": (a["f_w1"][l], [P, 2 * HC * P]), "b1": (a["f_b1"][l], [P, 2 * HC]),
                    "w2": (a["f_w2"][l], [P, HC, D]), "b2": (a["f_b2"][l], [P, 1])})
                ws.append(w)
                loads += more
            s3 = lambda name, shape: c3.enter_context(nc.sbuf_tensor(name, shape, F32))
            shifted = [s3(f"shifted{u}", [P, S]) for u in range(2)]
            qz = [s3(f"qz{u}", [P, FH, S]) for u in range(2)]
            prob = [s3(f"prob{s}", [P, CH]) for s in range(6)]
            hs = s3("hs", [P, T])
            layer_norm(nc, "n3", norms, xT, zT, loads,
                       [x[:, :, :] for x in qz] + [x[:, :] for x in (*prob, *shifted)])
            for l, w in enumerate(ws):
                local_attention(nc, f"l{l}", zT, w, (shifted, qz, prob))
                layer_norm(nc, f"m{l}", norms, hs, hs, gain=w["ln_g"][:, 0:1], shift_of=zT)
                if l + 1 < DEPTH:
                    gated_unit(nc, f"g{l}", zT, hs, w)
                else:
                    gated_unit(nc, f"g{l}", zT, hs, w, xT, out)


def tiles_for(nc, ctx, tag, table):
    tiles = {k: ctx.enter_context(nc.sbuf_tensor(f"{tag}_{k}", shape, F32)) for k, (_, shape) in table.items()}
    return tiles, [(tiles[k][tuple(slice(None) for _ in shape)], dram) for k, (dram, shape) in table.items()]


def layouts(x, ctx_1024, L0_attn_Wqk, L0_attn_bqk, L0_attn_Wv, L0_attn_bv, L0_attn_Wn, L0_attn_bn, L0_attn_Wo,
            L0_attn_bo, L0_xattn_Wq, L0_xattn_Wk, L0_xattn_Wv, L0_xattn_Wo, L0_ffn_wqkv, L0_ffn_q_scale,
            L0_ffn_k_scale, L0_ffn_wo, L0_ffn_ln_g, L0_ffn_ln_b, L0_ffn_w1, L0_ffn_b1, L0_ffn_w2, L0_ffn_b2):
    import numpy as np

    f = lambda v: np.ascontiguousarray(np.asarray(v), dtype=np.float32)
    col = lambda v: f(v).reshape(-1, 1)
    rep = lambda v: f(np.broadcast_to(np.asarray(v), (P, np.asarray(v).shape[-1])))
    s = np.arange(P)[:, None]
    t = np.arange(S)[None, :]
    halves = np.array([(e * 8 + h) * HD + d for e in range(2) for d in range(HD) for h in range(8)])
    context = np.zeros((B, D, CTXP), np.float32)
    context[:, :, 0:CTX] = np.asarray(ctx_1024).transpose(0, 2, 1)
    dmaj = np.array([h * HD + d for d in range(HD) for h in range(H)])
    hmaj = np.array([h for d in range(HD) for h in range(H)])
    wqk, bqk = np.asarray(L0_attn_Wqk), np.asarray(L0_attn_bqk)

    def spread(wo):
        return f(np.asarray(wo).reshape(HG, HL, HD, D).transpose(1, 0, 2, 3).reshape(H * HD, D))

    w1 = np.zeros((DEPTH, D, 2, HC * P), np.float32)
    w1[..., 0:HID] = np.asarray(L0_ffn_w1).reshape(DEPTH, D, 2, HID)
    b1 = np.zeros((DEPTH, 2, HC * P), np.float32)
    b1[..., 0:HID] = np.asarray(L0_ffn_b1).reshape(DEPTH, 2, HID)
    w2 = np.zeros((DEPTH, HC * P, D), np.float32)
    w2[:, 0:HID] = np.asarray(L0_ffn_w2)
    qk_scales = np.stack([np.asarray(L0_ffn_q_scale), np.asarray(L0_ffn_k_scale)], 1)
    both = lambda g: f(np.broadcast_to(g(qk_scales)[:, None], (DEPTH, P, 2, FD)))
    half = np.arange(0, FD, 2, dtype=np.float32)
    place = np.arange(S, dtype=np.float32)
    freq = (place[:, None] * (np.float32(1.0) / np.float32(10000.0) ** (half / np.float32(FD)))[None, :]).astype(np.float32)
    power = (place - S // 2) / np.float32(WINDOW // 2)
    xpos = ((half + 0.4 * FD) / (1.4 * FD))[None, :].astype(np.float64) ** power[:, None]
    cos, sin = np.cos(freq.astype(np.float64)), np.sin(freq.astype(np.float64))
    by_scale = lambda v: np.stack([v * xpos * 8.0, v / xpos], 1)
    cosine = by_scale(cos)[:, :, None, :].repeat(2, 2)
    sine = np.stack([-by_scale(sin), by_scale(sin)], 2)
    tiles = lambda v: f(v.reshape(2, P, 2, FD).transpose(1, 0, 2, 3))
    cosine, sine = tiles(cosine), tiles(sine)
    window = np.full((P, 2, S), NEG, np.float32)
    for blk in range(2):
        i = blk * P + s
        window[:, blk][(t <= i) & (t >= i - WINDOW)] = 0.0
    return {
        "x": f(np.asarray(x).reshape(T, D).T),
        "r_wq": f(wqk[:, 0:D][:, dmaj]), "r_wk": f(wqk[:, D:][:, dmaj]), "r_wn": f(np.asarray(L0_attn_Wn)[:, hmaj]),
        "r_wv": f(L0_attn_Wv), "r_bq": col(bqk[0:D][dmaj]), "r_bk": col(bqk[D:][dmaj]),
        "r_bn": col(np.asarray(L0_attn_bn)[hmaj]), "r_bv": rep(L0_attn_bv), "r_wo": spread(L0_attn_Wo),
        "r_bo": col(L0_attn_bo),
        "x_wq": f(np.asarray(L0_xattn_Wq).T[:, halves]), "x_wk": f(np.asarray(L0_xattn_Wk).T[:, halves]),
        "x_wv": f(np.asarray(L0_xattn_Wv).T), "x_wo": spread(np.asarray(L0_xattn_Wo).T),
        "context": context,
        "f_wqkv": f(L0_ffn_wqkv), "f_wo": f(np.asarray(L0_ffn_wo).reshape(DEPTH, FH // 2, P, D).transpose(0, 2, 1, 3)),
        "f_scales": both(lambda v: v), "f_scales_turned": both(lambda v: np.roll(v, FD // 2, axis=-1)),
        "f_ln_g": f(L0_ffn_ln_g)[:, :, None], "f_ln_b": f(L0_ffn_ln_b)[:, :, None],
        "f_w1": w1.reshape(DEPTH, D, 2 * HC * P), "f_b1": f(b1.reshape(DEPTH, 2 * HC, P).transpose(0, 2, 1)),
        "f_w2": f(w2.reshape(DEPTH, HC, P, D).transpose(0, 2, 1, 3)), "f_b2": f(L0_ffn_b2)[:, :, None],
        "cosine": cosine, "sine": sine, "window": window, "identity": np.eye(P, dtype=np.float32),
        "causal": (s <= t).astype(np.float32),
    }


def kernel(**inputs):
    import numpy as _np
    import concourse.bacc as _bacc
    from concourse import mybir as _mybir
    from concourse.bass_utils import run_bass_kernel_spmd as _run

    nc = _bacc.Bacc("TRN2", target_bir_lowering=False, num_devices=1)
    arrays, args = {}, {}
    for name, arr in layouts(**inputs).items():
        arrays[f"in_{name}"] = arr
        args[name] = nc.dram_tensor(f"in_{name}", arr.shape, _mybir.dt.from_np(arr.dtype), kind="ExternalInput").ap()
    out = nc.dram_tensor("out_x", (P, T), F32, kind="ExternalOutput").ap()
    build(nc, args, out)
    r = _run(nc, [arrays], core_ids=[0])
    return _np.ascontiguousarray(r.results[0]["out_x"].T).reshape(B, S, D)
```
